# Optimizing a Trainium2 kernel written in Bass

```python
import numpy as np
import jax
import jax.numpy as jnp

def _softmax(x, axis=-1):
    return jax.nn.softmax(x, axis=axis)

def _gelu(x):
    return jax.nn.gelu(x, approximate=True)

def _silu(x):
    return jax.nn.silu(x)

def _sigmoid(x):
    return jax.nn.sigmoid(x)

def _layernorm(x, axis=-1, eps=1e-05):
    m = jnp.mean(x, axis=axis, keepdims=True)
    v = jnp.var(x, axis=axis, keepdims=True)
    return (x - m) / jnp.sqrt(v + eps)

def _scatter_add(tgt, idx, src, axis=0):
    return tgt.at[idx].add(src)

def _segment_sum(src, seg, n):
    return jax.ops.segment_sum(src, seg, n)
kernel_name = 'mk_vit_tower_d1_tok_img512_r4_a40001'

def setup_inputs(seed: int=0):
    np.random.seed(seed)
    _w = jnp.asarray

    def _rec_inputs():
        import jax
        import jax.numpy as jnp
        _rk = jax.random.key(seed)
        x = 7.57192e-06 + 1.00007 * jax.random.normal(jax.random.fold_in(_rk, 1), (16, 96, 96, 3), jnp.float32)
        return x
    x = _rec_inputs()

    def _L0_tok_setup():
        import jax, jax.numpy as jnp
        import numpy as np
        B, H, W, C = (64, 224, 224, 3)
        P, D = (16, 128)
        LN_EPS = 0.001

        def _shift4(x):
            pad = lambda a, spec: jnp.pad(a, spec)
            right = pad(x[:, :, :-1, :], ((0, 0), (0, 0), (1, 0), (0, 0)))
            left = pad(x[:, :, 1:, :], ((0, 0), (0, 0), (0, 1), (0, 0)))
            down = pad(x[:, :-1, :, :], ((0, 0), (1, 0), (0, 0), (0, 0)))
            up = pad(x[:, 1:, :, :], ((0, 0), (0, 1), (0, 0), (0, 0)))
            return [right, left, down, up]
        key = jax.random.key(seed)
        k0, k1, k2 = jax.random.split(key, 3)
        x = jax.random.normal(k0, (B, H, W, C), jnp.float32)
        conv_w = jax.random.normal(k1, (P, P, 5 * C, D), jnp.float32) * 0.02
        conv_b = jnp.zeros((D,), jnp.float32)
        gamma = jnp.ones((D,), jnp.float32)
        beta = jnp.zeros((D,), jnp.float32)
        dense_w = jax.random.normal(k2, (D, D), jnp.float32) * 0.02
        dense_b = jnp.zeros((D,), jnp.float32)
        return {'x': x, 'conv_w': conv_w, 'conv_b': conv_b, 'gamma': gamma, 'beta': beta, 'dense_w': dense_w, 'dense_b': dense_b}
    _L0_tok_all = _L0_tok_setup()
    _L0_tok_in = {k: v for k, v in _L0_tok_all.items() if k in ('conv_w', 'conv_b', 'gamma', 'beta', 'dense_w', 'dense_b')}
    del _L0_tok_all

    def _L0_attn_setup():
        import jax, jax.numpy as jnp
        import numpy as np
        LN_EPS = 1e-05
        RMS_EPS = 1.1920929e-07

        def _layernorm(x, g, b):
            m = jnp.mean(x, axis=-1, keepdims=True)
            xc = x - m
            v = jnp.mean(xc * xc, axis=-1, keepdims=True)
            return xc / jnp.sqrt(v + LN_EPS) * g + b
        key = jax.random.key(seed)
        ks = jax.random.split(key, 8)
        L, D, H, M, B, S = (4, 128, 8, 512, 4, 512)
        std = 0.02
        return {'x': jax.random.normal(ks[0], (B, S, D), dtype=jnp.float32), 'Wq': jax.random.normal(ks[1], (L, D, D), dtype=jnp.float32) * std, 'Wk': jax.random.normal(ks[2], (L, D, D), dtype=jnp.float32) * std, 'Wv': jax.random.normal(ks[3], (L, D, D), dtype=jnp.float32) * std, 'rms_w': jnp.ones((L, H, D // H), dtype=jnp.float32), 'Wo': jax.random.normal(ks[4], (L, D, D), dtype=jnp.float32) * std, 'bo': jnp.zeros((L, D), dtype=jnp.float32), 'diffw': jnp.full((L,), 0.2, dtype=jnp.float32), 'g_ffn': jnp.ones((L, D), dtype=jnp.float32), 'b_ffn': jnp.zeros((L, D), dtype=jnp.float32), 'W1': jax.random.normal(ks[5], (L, M, D), dtype=jnp.float32) * std, 'b1': jnp.zeros((L, M), dtype=jnp.float32), 'W2': jax.random.normal(ks[6], (L, D, M), dtype=jnp.float32) * std, 'b2': jnp.zeros((L, D), dtype=jnp.float32), 'g_f': jnp.ones((D,), dtype=jnp.float32), 'b_f': jnp.zeros((D,), dtype=jnp.float32)}
    _L0_attn_all = _L0_attn_setup()
    _L0_attn_in = {k: v for k, v in _L0_attn_all.items() if k in ('Wq', 'Wk', 'Wv', 'rms_w', 'Wo', 'bo', 'diffw', 'g_ffn', 'b_ffn', 'W1', 'b1', 'W2', 'b2', 'g_f', 'b_f')}
    del _L0_attn_all

    def _L0_ffn_setup():
        import jax, jax.numpy as jnp
        import numpy as np
        CAPACITY_FACTOR = 1.2
        key = jax.random.key(seed)
        k1, k2, k3 = jax.random.split(key, 3)
        B, S, D, E = (8, 1024, 128, 16)
        x = jax.random.normal(k1, (B, S, D), dtype=jnp.float32)
        switch_w = jax.random.normal(k2, (E, D), dtype=jnp.float32) * 0.02
        switch_b = jnp.zeros((E,), dtype=jnp.float32)
        expert_w = jax.random.normal(k3, (E, D, D), dtype=jnp.float32) * 0.02
        expert_b = jnp.zeros((E, D), dtype=jnp.float32)
        return {'x': x, 'switch_w': switch_w, 'switch_b': switch_b, 'expert_w': expert_w, 'expert_b': expert_b}
    _L0_ffn_all = _L0_ffn_setup()
    _L0_ffn_in = {k: v for k, v in _L0_ffn_all.items() if k in ('switch_w', 'switch_b', 'expert_w', 'expert_b')}
    del _L0_ffn_all
    return {'x': x, 'L0_tok_conv_w': _L0_tok_in['conv_w'], 'L0_tok_conv_b': _L0_tok_in['conv_b'], 'L0_tok_gamma': _L0_tok_in['gamma'], 'L0_tok_beta': _L0_tok_in['beta'], 'L0_tok_dense_w': _L0_tok_in['dense_w'], 'L0_tok_dense_b': _L0_tok_in['dense_b'], 'L0_attn_Wq': _L0_attn_in['Wq'], 'L0_attn_Wk': _L0_attn_in['Wk'], 'L0_attn_Wv': _L0_attn_in['Wv'], 'L0_attn_rms_w': _L0_attn_in['rms_w'], 'L0_attn_Wo': _L0_attn_in['Wo'], 'L0_attn_bo': _L0_attn_in['bo'], 'L0_attn_diffw': _L0_attn_in['diffw'], 'L0_attn_g_ffn': _L0_attn_in['g_ffn'], 'L0_attn_b_ffn': _L0_attn_in['b_ffn'], 'L0_attn_W1': _L0_attn_in['W1'], 'L0_attn_b1': _L0_attn_in['b1'], 'L0_attn_W2': _L0_attn_in['W2'], 'L0_attn_b2': _L0_attn_in['b2'], 'L0_attn_g_f': _L0_attn_in['g_f'], 'L0_attn_b_f': _L0_attn_in['b_f'], 'L0_ffn_switch_w': _L0_ffn_in['switch_w'], 'L0_ffn_switch_b': _L0_ffn_in['switch_b'], 'L0_ffn_expert_w': _L0_ffn_in['expert_w'], 'L0_ffn_expert_b': _L0_ffn_in['expert_b']}

def reference(x, L0_tok_conv_w, L0_tok_conv_b, L0_tok_gamma, L0_tok_beta, L0_tok_dense_w, L0_tok_dense_b, L0_attn_Wq, L0_attn_Wk, L0_attn_Wv, L0_attn_rms_w, L0_attn_Wo, L0_attn_bo, L0_attn_diffw, L0_attn_g_ffn, L0_attn_b_ffn, L0_attn_W1, L0_attn_b1, L0_attn_W2, L0_attn_b2, L0_attn_g_f, L0_attn_b_f, L0_ffn_switch_w, L0_ffn_switch_b, L0_ffn_expert_w, L0_ffn_expert_b):
    import jax
    import jax.numpy as jnp

    def _L0_tok_ref(x, conv_w, conv_b, gamma, beta, dense_w, dense_b):
        import jax, jax.numpy as jnp
        import numpy as np
        B, H, W, C = (64, 224, 224, 3)
        P, D = (16, 128)
        LN_EPS = 0.001

        def _shift4(x):
            pad = lambda a, spec: jnp.pad(a, spec)
            right = pad(x[:, :, :-1, :], ((0, 0), (0, 0), (1, 0), (0, 0)))
            left = pad(x[:, :, 1:, :], ((0, 0), (0, 0), (0, 1), (0, 0)))
            down = pad(x[:, :-1, :, :], ((0, 0), (1, 0), (0, 0), (0, 0)))
            up = pad(x[:, 1:, :, :], ((0, 0), (0, 1), (0, 0), (0, 0)))
            return [right, left, down, up]
        xs = jnp.concatenate([x, *_shift4(x)], axis=-1)
        y = jax.lax.conv_general_dilated(xs, conv_w, window_strides=(P, P), padding='VALID', dimension_numbers=('NHWC', 'HWIO', 'NHWC')) + conv_b
        y = y.reshape(y.shape[0], -1, D)
        mu = jnp.mean(y, axis=-1, keepdims=True)
        var = jnp.mean(jnp.square(y - mu), axis=-1, keepdims=True)
        y = (y - mu) * jax.lax.rsqrt(var + LN_EPS) * gamma + beta
        return y @ dense_w + dense_b

    def _L0_attn_ref(x, Wq, Wk, Wv, rms_w, Wo, bo, diffw, g_ffn, b_ffn, W1, b1, W2, b2, g_f, b_f):
        import jax, jax.numpy as jnp
        import numpy as np
        LN_EPS = 1e-05
        RMS_EPS = 1.1920929e-07

        def _layernorm(x, g, b):
            m = jnp.mean(x, axis=-1, keepdims=True)
            xc = x - m
            v = jnp.mean(xc * xc, axis=-1, keepdims=True)
            return xc / jnp.sqrt(v + LN_EPS) * g + b

        def layer(xc, p):
            wq, wk, wv, rw, wo, bob, dw, g1, bn1, w1, bb1, w2, bb2 = p
            B, S, D = xc.shape
            H = rw.shape[0]
            F = D // (2 * H)
            qs = (xc @ wq.T).reshape(B, S, H, 2, F)
            ks_ = (xc @ wk.T).reshape(B, S, H, 2, F)
            scores = jnp.einsum('bqhif,bkhif->ibhqk', qs, ks_) * F ** (-0.5)
            atts = jax.nn.softmax(scores, axis=-1)
            att = atts[0] - dw * atts[1]
            vs = (xc @ wv.T).reshape(B, S, H, D // H)
            o = jnp.einsum('bhqk,bkhe->bqhe', att, vs)
            o = o / jnp.sqrt(jnp.mean(o * o, axis=(-2, -1), keepdims=True) + RMS_EPS) * rw
            xa = (o.reshape(B, S, D) @ wo.T + bob) * (1.0 - dw)
            xc = xa + xc
            h = _layernorm(xc, g1, bn1)
            h = jax.nn.gelu(h @ w1.T + bb1, approximate=False)
            xc = h @ w2.T + bb2 + xc
            return (xc, None)
        xf, _ = jax.lax.scan(layer, x, (Wq, Wk, Wv, rms_w, Wo, bo, diffw, g_ffn, b_ffn, W1, b1, W2, b2))
        return _layernorm(xf, g_f, b_f)

    def _L0_ffn_ref(x, switch_w, switch_b, expert_w, expert_b):
        import jax, jax.numpy as jnp
        import numpy as np
        CAPACITY_FACTOR = 1.2
        B, S, D = x.shape
        E = switch_w.shape[0]
        N = B * S
        xf = x.reshape(N, D)
        logits = xf @ switch_w.T + switch_b
        probs = jax.nn.softmax(logits, axis=-1)
        route_probs = jnp.max(probs, axis=-1)
        routes = jnp.argmax(probs, axis=-1)
        oh = jax.nn.one_hot(routes, E, dtype=jnp.int32)
        pos = jnp.take_along_axis(jnp.cumsum(oh, axis=0), routes[:, None], axis=1)[:, 0] - 1
        capacity = int(CAPACITY_FACTOR * N / E)
        keep = pos < capacity
        buf = jnp.zeros((E, capacity, D), dtype=xf.dtype).at[routes, pos].set(xf)
        y = jnp.einsum('ecd,efd->ecf', buf, expert_w) + expert_b[:, None, :]
        gathered = y[routes, jnp.minimum(pos, capacity - 1)]
        out = jnp.where(keep[:, None], gathered, xf) * route_probs[:, None]
        return out.reshape(B, S, D)
    h = _L0_tok_ref(x, L0_tok_conv_w, L0_tok_conv_b, L0_tok_gamma, L0_tok_beta, L0_tok_dense_w, L0_tok_dense_b)
    h = h + _L0_attn_ref(_layernorm(h, axis=-1), L0_attn_Wq, L0_attn_Wk, L0_attn_Wv, L0_attn_rms_w, L0_attn_Wo, L0_attn_bo, L0_attn_diffw, L0_attn_g_ffn, L0_attn_b_ffn, L0_attn_W1, L0_attn_b1, L0_attn_W2, L0_attn_b2, L0_attn_g_f, L0_attn_b_f)
    h = h + _L0_ffn_ref(_layernorm(h, axis=-1), L0_ffn_switch_w, L0_ffn_switch_b, L0_ffn_expert_w, L0_ffn_expert_b)
    return h

_drawn_inputs = setup_inputs


def setup_inputs(seed=0):
    import zlib

    import numpy as np

    out = dict(_drawn_inputs(seed))
    spreads = {'L0_tok_conv_b': (0.0, 0.1),
     'L0_tok_gamma': (1.0, 0.2),
     'L0_tok_beta': (0.0, 0.1),
     'L0_tok_dense_b': (0.0, 0.1),
     'L0_attn_rms_w': (1.0, 0.2),
     'L0_attn_bo': (0.0, 0.1),
     'L0_attn_diffw': (0.20000000298023224, 0.2),
     'L0_attn_g_ffn': (1.0, 0.6),
     'L0_attn_b_ffn': (0.0, 0.797),
     'L0_attn_b1': (0.0, 0.1),
     'L0_attn_b2': (0.0, 0.1),
     'L0_attn_g_f': (1.0, 0.2),
     'L0_attn_b_f': (0.0, 0.1),
     'L0_ffn_switch_b': (0.0, 0.1),
     'L0_ffn_expert_b': (0.0, 0.8)}
    factors = {'L0_attn_Wq': 6.334, 'L0_attn_Wk': 6.103, 'L0_ffn_expert_w': 5.03}
    for name, (base, spread) in spreads.items():
        noise = np.random.default_rng([zlib.crc32(name.encode()), seed]).standard_normal(out[name].shape)
        drawn = base * np.exp(spread * noise) if base else spread * noise
        out[name] = jnp.asarray(drawn.astype(out[name].dtype))
    for name, factor in factors.items():
        out[name] = (out[name] * factor).astype(out[name].dtype)
    return out
```

```python
from contextlib import ExitStack

import numpy as np

import concourse.bass as bass
from concourse import mybir

F32 = mybir.dt.float32
BF16 = mybir.dt.bfloat16
ALU = mybir.AluOpType
ACT = mybir.ActivationFunctionType
AX_X = mybir.AxisListType.X

IMGS, SIDE, CH, PATCH = 16, 96, 3, 16
GRID = SIDE // PATCH
SEQ = GRID * GRID
TOK = IMGS * SEQ
D = 128
LAYERS, HEADS, MLP, EXPERTS = 4, 8, 512, 16
EDIM = D // HEADS
FDIM = EDIM // 2
CAPACITY = int(1.2 * TOK / EXPERTS)
EPS_TOK, EPS_LN, EPS_RMS = 1e-3, 1e-5, 1.1920929e-07

PAIRS = IMGS // 2
HALF = TOK // 2
HPAIR = PAIRS // 2
CHUNK = 96
HCH = HALF // CHUNK
RCH = 2 * SEQ
HSUB = HEADS * 2 // 2
MC = MLP // D
WIN = PATCH + 2
RHO = 6
ROWG = WIN // RHO
KWIN = RHO * WIN
ROWPITCH = SIDE * CH + 48
TOKROWS = IMGS * GRID

C_IDENT, C_MEAN, C_SAMEIMG, C_SUMIMG = 0, 128, 256, 384
C_RMS, C_SUB, C_SELQ, C_CUM, C_ONE = 416, 418, 426, 462, 558
C_RANK, C_TOP, C_BOT, C_POW, C_END = 654, 670, 671, 672, 676

V_BO, V_G, V_B, V_B2, V_B1, V_RMS = 0, 4, 8, 12, 16, 32
V_CONVB, V_GAMMA, V_BETA, V_DENSEB, V_GF, V_BF, V_END = 40, 41, 42, 43, 44, 45, 46
L_BO, L_G, L_B, L_B2, L_B1, L_RMS, L_NDW, L_OMD, L_END = 0, 1, 2, 3, 4, 8, 12, 13, 14


def constants():
    c = np.zeros((128, C_END), np.float32)
    p = np.arange(128)
    c[:, C_IDENT:C_IDENT + 128] = np.eye(128)
    c[:, C_MEAN:C_MEAN + 128] = 1.0 / D
    f = np.arange(128)
    c[:, C_SAMEIMG:C_SAMEIMG + 128] = (p[:, None] // 64 == f[None] // 64) & (f[None] % 64 < SEQ)
    f = np.arange(32)
    c[:, C_SUMIMG:C_SUMIMG + 32] = (p[:, None] // 64 == f[None] // 16) & (p[:, None] % 64 < SEQ)
    c[:, C_RMS:C_RMS + 2] = (p[:, None] // 16 % 2 == np.arange(2)[None]) / D
    c[:, C_SUB:C_SUB + HSUB] = p[:, None] // FDIM % HSUB == np.arange(HSUB)[None]
    c[:, C_SELQ:C_SELQ + SEQ] = p[:, None] % 64 == np.arange(SEQ)[None]
    c[:, C_CUM:C_CUM + CHUNK] = p[:, None] <= np.arange(CHUNK)[None]
    c[:, C_ONE:C_ONE + CHUNK] = 1.0
    c[:, C_RANK:C_RANK + EXPERTS] = EXPERTS - np.arange(EXPERTS)[None]
    c[:, C_TOP] = p % GRID != 0
    c[:, C_BOT] = p % GRID != GRID - 1
    c[:, C_POW:C_POW + 4] = -0.5
    return c


class Chain:

    def __init__(self, eng, sem):
        self.eng, self.sem, self.base, self.n = eng, sem, 0, 0

    def step(self, ins):
        self.n += 1
        ins.then_inc(self.sem, 1)
        self.eng.wait_ge(self.sem, self.base + self.n)

    def rebase(self, base):
        self.base, self.n = base, 0


DVE_BEFORE, DVE_LAYER = 6, 27


def vit_tower(nc, x, conv_w, conv_b, gamma, beta, dense_w, dense_b, Wq, Wk, Wv, rms_w, Wo, bo, diffw,
              g_ffn, b_ffn, W1, b1, W2, b2, g_f, b_f, switch_w, switch_b, expert_w, expert_b, consts, out):
    ctx = ExitStack()
    with ctx:
        def sb(name, shape, dt=F32):
            return ctx.enter_context(nc.sbuf_tensor(name, shape, dt))

        def sem(name):
            return ctx.enter_context(nc.semaphore(name))

        ps = ctx.enter_context(nc.psum_tensor("ps", [128, 8, 512], F32))

        cst = sb("cst", [128, C_END])
        ident = cst[:, C_IDENT:C_IDENT + 128]
        meanw = cst[:, C_MEAN:C_MEAN + 128]
        cstb = sb("cstb", [128, C_RANK], BF16)
        identb = cstb[:, C_IDENT:C_IDENT + 128]
        sameimg_b = cstb[:, C_SAMEIMG:C_SAMEIMG + 128]
        selq_b = cstb[:, C_SELQ:C_SELQ + SEQ]
        vrow = sb("vrow", [V_END, 128])
        vcol = sb("vcol", [128, V_END])
        dwb = sb("dwb", [128, LAYERS])
        params = sb("params", [128, LAYERS, L_END])
        lp = sb("lp", [128, L_END])
        imgbuf = sb("imgbuf", [128, WIN * ROWPITCH])
        winbuf = sb("winbuf", [128, ROWG * CH * GRID * KWIN])
        ximg = imgbuf[0:TOKROWS, :].rearrange("p (u f) -> p u f", u=WIN)
        xwin = winbuf[0:TOKROWS, :].rearrange("p (g k) -> p g k", k=KWIN)
        xT = sb("xT", [KWIN, ROWG * CH, GRID, TOKROWS])
        wbuf = sb("wbuf", [128, 5 * ROWG * CH * D])
        wshift = wbuf[0:KWIN, :].rearrange("p (g a f) -> p g a f", g=5, a=ROWG)
        densew = sb("densew", [128, 128])
        X = sb("X", [128, TOK])
        X1 = sb("X1", [128, TOK])
        H0 = sb("H0", [128, TOK])
        xc = sb("xc", [128, TOK])
        sq = sb("sq", [128, TOK])
        hn = sb("hn", [128, TOK])
        ms = sb("ms", [CHUNK, 2, 4])
        rs = sb("rs", [CHUNK, 2, 4])
        rmsb = sb("rmsb", [128, 2, HALF])
        nqkvo = sb("nqkvo", [128, 4, 128])
        nW1 = sb("nW1", [128, MC, 128])
        nW2 = sb("nW2", [128, MC, 128])
        nWo2 = sb("nWo2", [128, 2, 4, 2, EDIM])
        tqkv = sb("tqkv", [128, 3, 128])
        tWo = sb("tWo", [128, 2, 2, 128])
        tW1 = sb("tW1", [128, MC, 128])
        tW2 = sb("tW2", [128, MC, 128])
        b1e = sb("b1e", [128, MC])
        qS = sb("qS", [128, 2, 2, HPAIR, SEQ])
        kSb = sb("kSb", [128, 2, 2, HPAIR, SEQ], BF16)
        qx = sb("qx", [128, PAIRS, 2, HSUB, SEQ])
        kxb = sb("kxb", [128, PAIRS, 2, HSUB, SEQ], BF16)
        kd = sb("kd", [128, PAIRS, 2, 2, 64])
        qdb = sb("qdb", [128, PAIRS, 2, 2, 64], BF16)
        vd = sb("vd", [128, PAIRS, HEADS, 2, EDIM])
        nmax = sb("nmax", [128, 2, 2 * HSUB], BF16)
        dmax = sb("dmax", [128, 2, 2 * HSUB, SEQ], BF16)
        pT = sb("pT", [128, 2, 2, HSUB * SEQ])
        rden = sb("rden", [128, 2, 2, 2, SEQ])
        on = sb("on", [128, 2, 2, 2, SEQ])
        o = sb("o", [128, 2, PAIRS, SEQ])
        osq = sb("osq", [128, 2, PAIRS, SEQ])
        xa = hn[:, :].rearrange("p (t n) -> p t n", t=2)
        gact = sb("gact", [128, 2, MC, HALF])
        swn = sb("swn", [EXPERTS, 128])
        swT = sb("swT", [128, EXPERTS])
        swb = sb("swb", [CHUNK, EXPERTS])
        ebn = sb("ebn", [EXPERTS, 128])
        nexp = imgbuf[:, 0:EXPERTS * 128].rearrange("p (e d) -> p e d", e=EXPERTS)
        texp = winbuf[:, 0:EXPERTS * 128].rearrange("p (e d) -> p e d", e=EXPERTS)
        NCH = TOK // CHUNK
        lg = sb("lg", [CHUNK, NCH, EXPERTS])
        eg = sb("eg", [CHUNK, NCH, EXPERTS])
        ohf = sb("ohf", [CHUNK, NCH, EXPERTS])
        ohb = sb("ohb", [CHUNK, NCH, EXPERTS], BF16)
        r1 = sb("r1", [CHUNK, 8, NCH])
        route = sb("route", [CHUNK, NCH, EXPERTS + 2])
        routeT = sb("routeT", [EXPERTS + 2, TOK])
        routeTb = sb("routeTb", [EXPERTS + 2, TOK], BF16)
        xm = wbuf[:, 0:3 * TOK].rearrange("p (b n) -> p b n", b=3)
        rpb = wbuf[:, 3 * TOK:4 * TOK]
        fin = wbuf[0:CHUNK, 4 * TOK:4 * TOK + NCH * 128].rearrange("p (c d) -> p c d", c=NCH)

        names = """in_x in_top in_bot in_w in_w4 in_c in_vec in_dense in_sw in_layer in_exp out_done
            halo_zero w_zero att_zero ximg_ok win_done xT_tr xT_cp_a xT_cp_v weff_done conv_done dense_done
            cstb_done vec_tr vcol_done params_done lp_done dvc
            ln_src ln_mean ln_cent ln_sq ln_stat ln_var ln_rs ln_rb h_done x_ready
            tr_qkv tr_wo tr_w1 tr_w2 wo_dup w_qkv w_o w_1 w_2 b1_ps b1_done
            qk_proj v_proj qk_ev v_ev q_sb k_sb qx_done kx_done sc_max sc_read dmax_done scores_done exp_done pv_done
            o_done osq_done wo_ps rms_ps rms_ms rms_r rms_rb rms_sb ffn1 gelu_done ffn2
            sw_tr swT_done exp_tr exp_cp_a exp_cp_v lg_ps lg_done eg_done oh_done cum_ps route_done route_tr routeT_done
            mask_ps xm_done exp_ps rp_ps rp_sb y_done y_tr fin_a fin_v acopy""".split()
        S = {n: sem(n) for n in names}

        def half(t):
            return slice(HALF * t, HALF * t + HALF)

        def of_image(tokens, j):
            return tokens.rearrange("p (a j q) -> p a j q", j=2, q=SEQ)[:, :, j, :]

        def cols(bank, n, rows=slice(0, 128), at=0):
            return ps[rows, bank, at:at + n]

        SHIFTS = [(1, 1), (1, 0), (1, 2), (0, 1), (2, 1)]
        BANK_QKV = [(0, 1, 6), (4, 5, 7)]
        BANK_UP = [2, 3, 4, 5, 0, 1, 2, 3]
        NTR = ROWG * CH * 2

        def load_shifted(eng, g, landed):
            du, dv = SHIFTS[g]
            for r in range(RHO):
                a0 = 1 if r < du else 0
                i0 = RHO * a0 + r - du
                n = (PATCH - 1 - i0) // RHO + 1
                dst = wshift[WIN * r + dv:WIN * r + dv + PATCH, g, a0:a0 + n, :]
                src = conv_w[i0::RHO, :, CH * g:CH * g + CH, :].rearrange("i j c d -> j i (c d)")
                eng.dma_start(dst, src).then_inc(landed, 16)

        block = ctx.enter_context(nc.Block())

        @block.sync
        def _(sp):
            rows = x.rearrange("b h w c -> (b h) (w c)")
            main = rows.rearrange("(n u) f -> n u f", u=PATCH)
            row = slice(CH, CH + SIDE * CH)
            sp.wait_ge(S["halo_zero"], 1)
            sp.dma_start(ximg[1:TOKROWS, 0, row], rows[PATCH - 1:IMGS * SIDE - 1:PATCH, :]).then_inc(S["in_top"], 16)
            sp.dma_start(ximg[:, 1:7, row], main[:, 0:6, :]).then_inc(S["in_x"], 16)
            sp.dma_start(ximg[:, 7:13, row], main[:, 6:12, :]).then_inc(S["in_x"], 16)
            sp.dma_start(ximg[:, 13:17, row], main[:, 12:16, :]).then_inc(S["in_x"], 16)
            sp.dma_start(ximg[0:TOKROWS - 1, WIN - 1, row], rows[PATCH:IMGS * SIDE:PATCH, :]).then_inc(S["in_bot"], 16)
            sp.wait_ge(S["w_zero"], 2)
            for g in range(4):
                load_shifted(sp, g, S["in_w"])

            def load_layer(l):
                for n, w in enumerate((Wq, Wk, Wv, Wo)):
                    sp.dma_start(nqkvo[:, n, :], w[bass.ds(l, 1), :, :].rearrange("l a b -> (l a) b")).then_inc(S["in_layer"], 16)
                sp.dma_start(nW1[:, :, :], W1[bass.ds(l, 1), :, :].rearrange("l (m p) d -> p (l m) d", p=128)).then_inc(S["in_layer"], 16)
                sp.dma_start(nW2[:, :, :], W2[bass.ds(l, 1), :, :].rearrange("l p (m k) -> p (l m) k", m=MC)).then_inc(S["in_layer"], 16)

            load_layer(0)
            with sp.Fori(1, LAYERS) as l:
                sp.wait_ge(S["tr_w2"], l)
                load_layer(l)
            sp.wait_ge(S["fin_a"], 1)
            sp.wait_ge(S["fin_v"], 1)
            sp.dma_start(out.rearrange("b s d -> (b s) d").rearrange("(c p) d -> p c d", p=CHUNK),
                         fin[:, :, :]).then_inc(S["out_done"], 16)
            sp.wait_ge(S["out_done"], 16)

        @block.gpsimd
        def _(pool):
            nc.gpsimd.memset(wshift[:, 3:5, :, :], 0.0).then_inc(S["w_zero"], 1)
            pool.dma_start(cst[:, :], consts).then_inc(S["in_c"], 16)
            for v, n, src in ((V_BO, 4, bo), (V_G, 4, g_ffn), (V_B, 4, b_ffn), (V_B2, 4, b2),
                              (V_B1, 16, b1.rearrange("l (m p) -> (l m) p", p=128))):
                pool.dma_start(vrow[v:v + n, :], src).then_inc(S["in_vec"], 16)
            for v, src in ((V_CONVB, conv_b), (V_GAMMA, gamma), (V_BETA, beta), (V_DENSEB, dense_b),
                           (V_GF, g_f), (V_BF, b_f)):
                pool.dma_start(vrow[v:v + 1, :], src.rearrange("(a d) -> a d", a=1)).then_inc(S["in_vec"], 16)
            pool.wait_ge(S["w_zero"], 2)
            load_shifted(pool, 4, S["in_w4"])
            for j in range(2):
                dst = vrow[V_RMS:V_RMS + 8, :].rearrange("p (c j e) -> p c j e", c=4, j=2)[:, :, j, :]
                pool.dma_start(dst, rms_w.rearrange("l (s c) e -> (l s) c e", s=2)).then_inc(S["in_vec"], 16)
            pool.dma_start(dwb[:, :], diffw.rearrange("(a l) -> a l", a=1).broadcast_to([128, LAYERS])).then_inc(S["in_vec"], 16)
            pool.dma_start(densew[:, :], dense_w).then_inc(S["in_dense"], 16)
            nc.gpsimd.memset(kd[:, :, :, :, :], 0.0).then_inc(S["att_zero"], 1)
            nc.gpsimd.memset(qdb[:, :, :, :, :], 0.0).then_inc(S["att_zero"], 1)
            nc.gpsimd.memset(vd[:, :, :, :, :], 0.0).then_inc(S["att_zero"], 1)
            pool.dma_start(swn[:, :], switch_w).then_inc(S["in_sw"], 16)
            pool.dma_start(swb[:, :], switch_b.rearrange("(a l) -> a l", a=1).broadcast_to([CHUNK, EXPERTS])).then_inc(S["in_sw"], 16)
            pool.dma_start(ebn[:, :], expert_b).then_inc(S["in_sw"], 16)
            pool.wait_ge(S["win_done"], ROWG * CH)
            pool.dma_start(nexp[:, :, :], expert_w.rearrange("e f d -> f e d")).then_inc(S["in_exp"], 16)

            def power(n, t):
                pool.wait_ge(S["ln_var"], 2 * n + t + 1)
                nc.gpsimd.tensor_tensor(rs[:, t, 0:HCH], ms[:, t, 0:HCH], cst[0:CHUNK, C_POW:C_POW + HCH],
                                        ALU.pow).then_inc(S["ln_rs"], 1)

            pool.wait_ge(S["in_c"], 16)
            for n in range(2):
                for t in range(2):
                    power(n, t)
            with pool.Fori(0, LAYERS) as l:
                pool.wait_ge(S["in_layer"], 96 * l + 96)
                ones_of_heads = cst[:, C_ONE:C_ONE + EDIM].rearrange("p (h e) -> p h e", h=1).broadcast_to([128, HEADS, EDIM])
                for j in range(2):
                    cols_of_heads = nqkvo[:, 3, :].rearrange("p (h e) -> p h e", e=EDIM)
                    nc.gpsimd.tensor_tensor(nWo2[:, :, :, j, :].rearrange("p s c e -> p (s c) e"),
                                            cols_of_heads, ones_of_heads, ALU.mult).then_inc(S["wo_dup"], 1)
                for t in range(2):
                    pool.wait_ge(S["rms_ms"], 2 * l + t + 1)
                    nc.gpsimd.tensor_tensor(rs[0:RCH, t, 0:4], ms[0:RCH, t, 0:4], cst[0:RCH, C_POW:C_POW + 4],
                                            ALU.pow).then_inc(S["rms_r"], 1)
                for t in range(2):
                    power(l + 2, t)
            for n in (LAYERS + 2, LAYERS + 3):
                for t in range(2):
                    power(n, t)

        @block.scalar
        def _(act):
            act.wait_ge(S["in_c"], 16)
            act.wait_ge(S["in_top"], 16)
            act.wait_ge(S["in_bot"], 16)
            nc.scalar.activation(ximg[:, 0, :], ximg[:, 0, :], ACT.Copy, scale=cst[0:TOKROWS, C_TOP:C_TOP + 1]).then_inc(S["ximg_ok"], 1)
            nc.scalar.activation(ximg[:, WIN - 1, :], ximg[:, WIN - 1, :], ACT.Copy, scale=cst[0:TOKROWS, C_BOT:C_BOT + 1]).then_inc(S["ximg_ok"], 1)
            for g in range(0, NTR, 2):
                act.wait_ge(S["xT_tr"], g + 1)
                nc.scalar.copy(xT[:, g // 2, 0:3, :], cols(g % 6, 3 * TOKROWS, slice(0, KWIN)).rearrange("p (w n) -> p w n", w=3)).then_inc(S["xT_cp_a"], 1)
            act.wait_ge(S["vec_tr"], 1)
            nc.scalar.copy(vcol[:, :], cols(6, V_END, at=400)).then_inc(S["vcol_done"], 1)

            def square(n, t):
                act.wait_ge(S["ln_cent"], 2 * n + t + 1)
                nc.scalar.activation(sq[:, half(t)], xc[:, half(t)], ACT.Square).then_inc(S["ln_sq"], 1)

            for n in range(2):
                for t in range(2):
                    square(n, t)
            act.wait_ge(S["att_zero"], 3)
            with act.Fori(0, LAYERS) as l:
                act.wait_ge(S["tr_qkv"], l + 1)
                nc.scalar.copy(tqkv[:, :, :], cols(4, 384)).then_inc(S["w_qkv"], 1)
                act.wait_ge(S["tr_w1"], l + 1)
                nc.scalar.copy(tW1[:, :, :], cols(2, 512)).then_inc(S["w_1"], 1)
                act.wait_ge(S["tr_w2"], l + 1)
                nc.scalar.copy(tW2[:, :, :], cols(3, 512)).then_inc(S["w_2"], 1)
                for t in range(2):
                    bq, bk, bv = BANK_QKV[t]
                    act.wait_ge(S["qk_proj"], 2 * l + t + 1)
                    q_v = cols(bq, HALF).rearrange("p (u a q) -> p u a q", u=2, q=SEQ)
                    k_v = cols(bk, HALF).rearrange("p (u a q) -> p u a q", u=2, q=SEQ)
                    nc.scalar.copy(qS[:, t, :, :, :], q_v).then_inc(S["q_sb"], 1)
                    pr = slice(HPAIR * t, HPAIR * t + HPAIR)
                    for j in range(2):
                        r = slice(64 * j, 64 * j + 64)
                        nc.scalar.copy(qdb[r, pr, :, j, 0:SEQ].rearrange("p a u q -> p u a q"), q_v[r])
                    act.wait_ge(S["k_sb"], 2 * l + t + 1)
                    for j in range(2):
                        r = slice(64 * j, 64 * j + 64)
                        last = nc.scalar.copy(kd[r, pr, :, j, 0:SEQ].rearrange("p a u q -> p u a q"), k_v[r])
                    last.then_inc(S["qk_ev"], 1)
                    act.wait_ge(S["v_proj"], 2 * l + t + 1)
                    for j in range(2):
                        r = slice(64 * j, 64 * j + SEQ)
                        last = nc.scalar.copy(vd[r, pr, :, j, :], cols(bv, 512, r).rearrange("p (a h e) -> p a h e", a=HPAIR, h=HEADS))
                    last.then_inc(S["v_ev"], 1)
                for p in range(PAIRS):
                    b = 2 + 2 * (p % 2)
                    act.wait_ge(S["scores_done"], PAIRS * l + p + 1)
                    if p >= 2:
                        act.wait_ge(S["pv_done"], PAIRS * l + p - 1)
                    nc.scalar.activation(pT[:, p % 2, :, :], ps[:, b:b + 2, 0:HALF], ACT.Exp,
                                         scale=float(FDIM) ** -0.5).then_inc(S["exp_done"], 1)
                    if p >= 2:
                        act.wait_ge(S["o_done"], PAIRS * l + p - 1)
                        nc.scalar.activation(osq[:, :, p - 2, :], o[:, :, p - 2, :], ACT.Square).then_inc(S["osq_done"], 1)
                for p in (PAIRS - 2, PAIRS - 1):
                    act.wait_ge(S["o_done"], PAIRS * l + p + 1)
                    nc.scalar.activation(osq[:, :, p, :], o[:, :, p, :], ACT.Square).then_inc(S["osq_done"], 1)
                for t in range(2):
                    act.wait_ge(S["rms_rb"], 2 * l + t + 1)
                    nc.scalar.copy(rmsb[:, t, :], cols(2 + t, HALF)).then_inc(S["rms_sb"], 1)
                for t in range(2):
                    square(l + 2, t)
                act.wait_ge(S["b1_done"], l + 1)
                for t in range(2):
                    for m in range(MC):
                        act.wait_ge(S["ffn1"], 2 * MC * l + MC * t + m + 1)
                        nc.scalar.activation(gact[:, t, m, :], cols(BANK_UP[MC * t + m], HALF), ACT.Gelu,
                                             bias=b1e[:, m:m + 1]).then_inc(S["gelu_done"], 1)
            for t in range(2):
                square(LAYERS + 2, t)
            act.wait_ge(S["sw_tr"], 1)
            nc.scalar.copy(swT[:, :], cols(0, EXPERTS)).then_inc(S["swT_done"], 1)
            for g in range(0, 4, 2):
                act.wait_ge(S["exp_tr"], g + 1)
                nc.scalar.copy(texp[:, 4 * g:4 * g + 4, :], cols(2 + g, 512)).then_inc(S["exp_cp_a"], 1)
            for t in range(2):
                square(LAYERS + 3, t)
            act.wait_ge(S["lg_done"], 1)
            nc.scalar.activation(eg[:, :, :], lg[:, :, :], ACT.Exp).then_inc(S["eg_done"], 1)
            act.wait_ge(S["rp_ps"], 1)
            nc.scalar.copy(rpb[:, :].rearrange("p (t n) -> p t n", t=2), ps[:, 0:2, 0:HALF]).then_inc(S["rp_sb"], 1)
            act.wait_ge(S["y_tr"], 1)
            nc.scalar.copy(fin[:, 0:HCH, :], cols(2, HCH * 128, slice(0, CHUNK))).then_inc(S["fin_a"], 1)

        @block.vector
        def _(dve):
            chain = Chain(dve, S["dvc"])
            nc.vector.memset(ximg[:, 0, :], 0.0)
            nc.vector.memset(ximg[:, WIN - 1, :], 0.0)
            nc.vector.memset(ximg[:, 1:WIN - 1, 0:CH], 0.0)
            nc.vector.memset(ximg[:, 1:WIN - 1, CH + SIDE * CH:ROWPITCH], 0.0).then_inc(S["halo_zero"], 1)
            nc.vector.memset(wshift[:, 0:3, :, :], 0.0).then_inc(S["w_zero"], 1)
            dve.wait_ge(S["in_c"], 16)
            nc.vector.tensor_copy(cstb[:, :], cst[:, 0:C_RANK]).then_inc(S["cstb_done"], 1)
            dve.wait_ge(S["in_x"], 48)
            dve.wait_ge(S["ximg_ok"], 2)

            for a in range(ROWG):
                for c in range(CH):
                    dst = xwin[:, (a * CH + c) * GRID:(a * CH + c + 1) * GRID, :].rearrange("n w (r v) -> n w r v", v=WIN)
                    rws = ximg[:, RHO * a:RHO * a + RHO, :]
                    body = rws[:, :, 0:GRID * 48].rearrange("n r (w v c) -> n w r v c", w=GRID, c=CH)[:, :, :, :, c]
                    tail = rws[:, :, 48:48 + GRID * 48].rearrange("n r (w v c) -> n w r v c", w=GRID, c=CH)[:, :, :, 0:2, c]
                    nc.vector.tensor_copy(dst[:, :, :, 0:PATCH], body)
                    nc.vector.tensor_copy(dst[:, :, :, PATCH:WIN], tail).then_inc(S["win_done"], 1)
            for g in range(1, NTR, 2):
                dve.wait_ge(S["xT_tr"], g + 1)
                nc.vector.tensor_copy(xT[:, g // 2, 3:6, :], cols(g % 6, 3 * TOKROWS, slice(0, KWIN)).rearrange("p (w n) -> p w n", w=3)).then_inc(S["xT_cp_v"], 1)
            dve.wait_ge(S["in_w"], 16 * 4 * RHO)
            dve.wait_ge(S["in_w4"], 16 * RHO)
            for g in range(1, 5):
                ins = nc.vector.tensor_tensor(wshift[:, 0, :, :], wshift[:, 0, :, :], wshift[:, g, :, :], ALU.add)
                if g < 4:
                    chain.step(ins)
            ins.then_inc(S["weff_done"], 1)
            dve.wait_ge(S["vcol_done"], 1)
            for t in range(2):
                dve.wait_ge(S["conv_done"], t + 1)
                nc.vector.tensor_scalar(X1[:, half(t)], cols(6 + t, HALF), vcol[:, V_CONVB:V_CONVB + 1], None, ALU.add).then_inc(S["ln_src"], 1)

            def center(n, t, src):
                dve.wait_ge(S["ln_mean"], 2 * n + t + 1)
                nc.vector.tensor_tensor(xc[:, half(t)], src[:, half(t)], cols(6 + t, HALF), ALU.subtract).then_inc(S["ln_cent"], 1)

            def variance(n, t, eps):
                dve.wait_ge(S["ln_stat"], 2 * n + t + 1)
                nc.vector.tensor_scalar(ms[:, t, 0:HCH], cols(6 + t, HCH, slice(0, CHUNK), 300), eps, None, ALU.add).then_inc(S["ln_var"], 1)

            for t in range(2):
                center(0, t, X1)
            for t in range(2):
                variance(0, t, EPS_TOK)
            for t in range(2):
                dve.wait_ge(S["ln_rb"], t + 1)
                chain.step(nc.vector.scalar_tensor_tensor(hn[:, half(t)], xc[:, half(t)], vcol[:, V_GAMMA:V_GAMMA + 1],
                                                          cols(6 + t, HALF), ALU.mult, ALU.mult))
                nc.vector.tensor_scalar(hn[:, half(t)], hn[:, half(t)], vcol[:, V_BETA:V_BETA + 1], None, ALU.add).then_inc(S["h_done"], 1)
            for t in range(2):
                dve.wait_ge(S["dense_done"], t + 1)
                nc.vector.tensor_scalar(H0[:, half(t)], cols(t, HALF), vcol[:, V_DENSEB:V_DENSEB + 1], None, ALU.add).then_inc(S["ln_src"], 1)
            nc.vector.tensor_copy(params[:, :, 0:4].rearrange("p l k -> p k l"), vcol[:, 0:16].rearrange("p (k l) -> p k l", k=4))
            nc.vector.tensor_copy(params[:, :, L_B1:L_B1 + MC], vcol[:, V_B1:V_B1 + 16].rearrange("p (l m) -> p l m", l=LAYERS))
            for s in range(2):
                for j in range(2):
                    k = L_RMS + 2 * s + j
                    nc.vector.tensor_scalar(params[:, :, k], vcol[:, V_RMS:V_RMS + 8].rearrange("p (l s) -> p l s", s=2)[:, :, s],
                                            cst[:, C_RMS + j:C_RMS + j + 1], float(D), ALU.mult, ALU.mult)
            nc.vector.tensor_scalar(params[:, :, L_NDW], dwb[:, :], -1.0, None, ALU.mult)
            chain.step(nc.vector.tensor_scalar(params[:, :, L_OMD], dwb[:, :], -1.0, 1.0, ALU.mult, ALU.add))
            nc.vector.tensor_tensor(params[:, :, L_BO], params[:, :, L_BO], params[:, :, L_OMD], ALU.mult).then_inc(S["params_done"], 1)
            for t in range(2):
                center(1, t, H0)
            for t in range(2):
                variance(1, t, EPS_LN)
            for t in range(2):
                dve.wait_ge(S["ln_rb"], 2 + t + 1)
                nc.vector.tensor_tensor(X[:, half(t)], xc[:, half(t)], cols(6 + t, HALF), ALU.mult).then_inc(S["x_ready"], 1)
            assert chain.n == DVE_BEFORE, chain.n
            dve.wait_ge(S["params_done"], 1)
            with dve.Fori(0, LAYERS) as l:
                chain.rebase(DVE_LAYER * l + DVE_BEFORE)
                dve.wait_ge(S["x_ready"], 2 * l + 2)
                chain.step(nc.vector.tensor_copy(lp[:, :], params[:, bass.ds(l, 1), :].rearrange("p l k -> p (l k)")))
                dve.wait_ge(S["tr_wo"], l + 1)
                for s in range(2):
                    for j in range(2):
                        k = L_RMS + 2 * s + j
                        last = nc.vector.tensor_scalar(tWo[:, s, j, :], cols(5, 128, at=128 * s), lp[:, k:k + 1], None, ALU.mult)
                last.then_inc(S["w_o"], 1)

                def spread(t, queries, keys):
                    pr = slice(HPAIR * t, HPAIR * t + HPAIR)
                    for buf, src, done in ((qx, qS, queries), (kxb, kSb, keys)):
                        for a in done:
                            last = nc.vector.tensor_scalar(buf[:, pr, :, a, :].rearrange("p a u q -> p u a q"), src[:, t, :, :, :],
                                                           cst[:, C_SUB + a:C_SUB + a + 1], None, ALU.mult)
                            if a == HSUB - 1:
                                last.then_inc(S["qx_done" if buf is qx else "kx_done"], 1)

                def keys_bf16(t):
                    dve.wait_ge(S["qk_proj"], 2 * l + t + 1)
                    nc.vector.tensor_copy(kSb[:, t, :, :, :], cols(BANK_QKV[t][1], HALF).rearrange("p (u a q) -> p u a q", u=2, q=SEQ)).then_inc(S["k_sb"], 1)
                    dve.wait_ge(S["k_sb"], 2 * l + t + 1)

                def maxima(p):
                    dve.wait_ge(S["sc_max"], PAIRS * l + p + 1)
                    ins = nc.vector.tensor_reduce(nmax[:, p % 2, :], ps[:, 0:2, 0:HALF].rearrange("p u (a k) -> p u a k", k=SEQ),
                                                  AX_X, ALU.max, negate=True)
                    chain.step(ins)
                    if p >= 2:
                        dve.wait_ge(S["scores_done"], PAIRS * l + p - 1)
                    nc.vector.tensor_tensor(dmax[:, p % 2, :, :], selq_b.rearrange("p (a q) -> p a q", a=1).broadcast_to([128, 2 * HSUB, SEQ]),
                                            nmax[:, p % 2, :].rearrange("p (a q) -> p a q", q=1).broadcast_to([128, 2 * HSUB, SEQ]),
                                            ALU.mult).then_inc(S["dmax_done"], 1)

                def normalize(p):
                    b = 6 + p % 2
                    dve.wait_ge(S["pv_done"], PAIRS * l + p + 1)
                    sums = cols(b, 144, at=144).rearrange("p (s i q) -> p s i q", s=2, i=2)
                    vals = cols(b, 144).rearrange("p (s i q) -> p s i q", s=2, i=2)
                    r, w = rden[:, p % 2], on[:, p % 2]
                    chain.step(nc.vector.reciprocal(r, sums))
                    chain.step(nc.vector.tensor_tensor(w, vals, r, ALU.mult))
                    nc.vector.scalar_tensor_tensor(o[:, :, p, :], w[:, :, 1, :], lp[:, L_NDW:L_NDW + 1], w[:, :, 0, :],
                                                   ALU.mult, ALU.add).then_inc(S["o_done"], 1)

                every = range(HSUB)
                keys_bf16(0)
                spread(0, (), every)
                dve.wait_ge(S["q_sb"], 2 * l + 1)
                spread(0, every, ())
                maxima(0)
                keys_bf16(1)
                dve.wait_ge(S["q_sb"], 2 * l + 2)
                spread(1, range(0, 2), range(0, 4))
                maxima(1)
                spread(1, range(2, 4), range(4, 8))
                normalize(0)
                maxima(2)
                spread(1, range(4, 6), ())
                normalize(1)
                maxima(3)
                spread(1, range(6, 8), ())
                normalize(2)
                for p in range(4, PAIRS):
                    maxima(p)
                    normalize(p - 1)
                normalize(PAIRS - 1)

                for t in range(2):
                    dve.wait_ge(S["rms_ps"], 2 * l + t + 1)
                    nc.vector.tensor_scalar(ms[0:RCH, t, :], cols(t, 4, slice(0, RCH), 300), EPS_RMS, None, ALU.add).then_inc(S["rms_ms"], 1)
                dve.wait_ge(S["b1_ps"], l + 1)
                nc.vector.tensor_tensor(b1e[:, :], lp[:, L_B1:L_B1 + MC], cols(7, MC, at=400), ALU.add).then_inc(S["b1_done"], 1)
                for t in range(2):
                    dve.wait_ge(S["rms_sb"], 2 * l + t + 1)
                    dve.wait_ge(S["wo_ps"], 2 * l + t + 1)
                    chain.step(nc.vector.scalar_tensor_tensor(xa[:, t, :], rmsb[:, t, :], lp[:, L_OMD:L_OMD + 1], cols(t, HALF), ALU.mult, ALU.mult))
                    nc.vector.scalar_tensor_tensor(X1[:, half(t)], xa[:, t, :], lp[:, L_BO:L_BO + 1], X[:, half(t)],
                                                   ALU.add, ALU.add).then_inc(S["ln_src"], 1)
                for t in range(2):
                    center(l + 2, t, X1)
                for t in range(2):
                    variance(l + 2, t, EPS_LN)
                for t in range(2):
                    dve.wait_ge(S["ln_rb"], 2 * l + 4 + t + 1)
                    nc.vector.scalar_tensor_tensor(hn[:, half(t)], xc[:, half(t)], lp[:, L_G:L_G + 1], cols(6 + t, HALF),
                                                   ALU.mult, ALU.mult).then_inc(S["h_done"], 1)
                for t in range(2):
                    dve.wait_ge(S["ffn2"], 2 * l + t + 1)
                    ins = nc.vector.scalar_tensor_tensor(X[:, half(t)], cols(6 + t, HALF), lp[:, L_B2:L_B2 + 1], X1[:, half(t)],
                                                         ALU.add, ALU.add)
                    ins.then_inc(S["x_ready"], 1)
                assert chain.n == DVE_LAYER, chain.n

            chain.rebase(DVE_LAYER * LAYERS + DVE_BEFORE)
            n = LAYERS + 2
            for t in range(2):
                center(n, t, X)
            for t in range(2):
                variance(n, t, EPS_LN)
            for t in range(2):
                dve.wait_ge(S["ln_rb"], 2 * n + t + 1)
                chain.step(nc.vector.scalar_tensor_tensor(hn[:, half(t)], xc[:, half(t)], vcol[:, V_GF:V_GF + 1], cols(6 + t, HALF),
                                                          ALU.mult, ALU.mult))
                nc.vector.scalar_tensor_tensor(X1[:, half(t)], hn[:, half(t)], vcol[:, V_BF:V_BF + 1], H0[:, half(t)],
                                               ALU.add, ALU.add).then_inc(S["ln_src"], 1)
            for g in range(1, 4, 2):
                dve.wait_ge(S["exp_tr"], g + 1)
                nc.vector.tensor_copy(texp[:, 4 * g:4 * g + 4, :], cols(2 + g, 512)).then_inc(S["exp_cp_v"], 1)
            n = LAYERS + 3
            for t in range(2):
                center(n, t, X1)
            for t in range(2):
                variance(n, t, EPS_LN)
            for t in range(2):
                dve.wait_ge(S["ln_rb"], 2 * n + t + 1)
                nc.vector.tensor_tensor(X[:, half(t)], xc[:, half(t)], cols(6 + t, HALF), ALU.mult).then_inc(S["x_ready"], 1)
            dve.wait_ge(S["lg_ps"], 1)
            dve.wait_ge(S["in_sw"], 48)

            def over(v):
                return v.rearrange("p (c e) -> p c e", e=1).broadcast_to([CHUNK, NCH, EXPERTS])

            chain.step(nc.vector.tensor_tensor(lg[:, :, :], cols(0, NCH * EXPERTS, slice(0, CHUNK)).rearrange("p (c e) -> p c e", e=EXPERTS),
                                               swb[:, :].rearrange("p (c e) -> p c e", c=1).broadcast_to([CHUNK, NCH, EXPERTS]), ALU.add))
            chain.step(nc.vector.tensor_reduce(r1[:, 0, :], lg[:, :, :], AX_X, ALU.max))
            nc.vector.tensor_tensor(lg[:, :, :], lg[:, :, :], over(r1[:, 0, :]), ALU.subtract).then_inc(S["lg_done"], 1)
            dve.wait_ge(S["eg_done"], 1)
            chain.step(nc.vector.tensor_reduce(r1[:, 1, :], eg[:, :, :], AX_X, ALU.max))
            chain.step(nc.vector.tensor_tensor(lg[:, :, :], eg[:, :, :], over(r1[:, 1, :]), ALU.is_equal))
            chain.step(nc.vector.tensor_tensor(lg[:, :, :], lg[:, :, :],
                                               cst[0:CHUNK, C_RANK:C_RANK + EXPERTS].rearrange("p (c e) -> p c e", c=1).broadcast_to([CHUNK, NCH, EXPERTS]),
                                               ALU.mult))
            chain.step(nc.vector.tensor_reduce(r1[:, 2, :], lg[:, :, :], AX_X, ALU.max))
            nc.vector.tensor_tensor(ohb[:, :, :], lg[:, :, :], over(r1[:, 2, :]), ALU.is_equal).then_inc(S["oh_done"], 1)
            chain.step(nc.vector.tensor_tensor(ohf[:, :, :], lg[:, :, :], over(r1[:, 2, :]), ALU.is_equal))
            chain.step(nc.vector.tensor_reduce(r1[:, 3, :], eg[:, :, :], AX_X, ALU.add))
            chain.step(nc.vector.reciprocal(r1[:, 4, :], r1[:, 3, :]))
            nc.vector.tensor_tensor(route[:, :, EXPERTS + 1], r1[:, 1, :], r1[:, 4, :], ALU.mult)
            dve.wait_ge(S["cum_ps"], 1)
            chain.step(nc.vector.tensor_tensor(lg[:, :, :], ohf[:, :, :], cols(1, NCH * EXPERTS, slice(0, CHUNK)).rearrange("p (c e) -> p c e", e=EXPERTS), ALU.mult))
            chain.step(nc.vector.tensor_reduce(r1[:, 5, :], lg[:, :, :], AX_X, ALU.add))
            nc.vector.tensor_scalar(route[:, :, EXPERTS], r1[:, 5, :], float(CAPACITY), None, ALU.is_gt)
            chain.step(nc.vector.tensor_scalar(r1[:, 6, :], r1[:, 5, :], float(CAPACITY), None, ALU.is_le))
            nc.vector.tensor_tensor(route[:, :, 0:EXPERTS], ohf[:, :, :], over(r1[:, 6, :]), ALU.mult).then_inc(S["route_done"], 1)
            dve.wait_ge(S["route_tr"], 1)
            rT = ps[0:EXPERTS + 2, 2:4, 0:HALF]
            nc.vector.tensor_copy(routeTb[:, :].rearrange("p (t n) -> p t n", t=2), rT)
            nc.vector.tensor_copy(routeT[:, :].rearrange("p (t n) -> p t n", t=2), rT).then_inc(S["routeT_done"], 1)
            for e in range(EXPERTS + 1):
                dve.wait_ge(S["mask_ps"], e + 1)
                if e >= 3:
                    dve.wait_ge(S["exp_ps"], e - 2)
                b = 2 + 2 * (e % 2)
                nc.vector.tensor_tensor(xm[:, e % 3, :].rearrange("p (t n) -> p t n", t=2), X[:, :].rearrange("p (t n) -> p t n", t=2),
                                        ps[:, b:b + 2, 0:HALF], ALU.mult).then_inc(S["xm_done"], 1)
            dve.wait_ge(S["rp_sb"], 1)
            dve.wait_ge(S["exp_ps"], EXPERTS + 1)
            for t in range(2):
                chain.step(nc.vector.tensor_tensor(hn[:, half(t)], rpb[:, half(t)], cols(6 + t, HALF), ALU.mult))
                nc.vector.tensor_tensor(hn[:, half(t)], hn[:, half(t)], X1[:, half(t)], ALU.add).then_inc(S["y_done"], 1)
            dve.wait_ge(S["y_tr"], 2)
            nc.vector.tensor_copy(fin[:, HCH:NCH, :], cols(3, HCH * 128, slice(0, CHUNK))).then_inc(S["fin_v"], 1)

        @block.tensor
        def _(pe):
            mm = nc.tensor.matmul

            def turn(dst, src, k):
                return nc.tensor.transpose(dst, src, ident[0:k, 0:k])

            pe.wait_ge(S["in_c"], 16)
            pe.wait_ge(S["in_vec"], 16 * 14)
            turn(cols(6, V_END, at=400), vrow[:, :], V_END).then_inc(S["vec_tr"], 1)
            for g in range(NTR):
                pe.wait_ge(S["win_done"], g // 2 + 1)
                if g >= 6:
                    pe.wait_ge(S["xT_cp_v" if g % 2 else "xT_cp_a"], (g - 6) // 2 + 1)
                for w in range(3):
                    ins = turn(cols(g % 6, TOKROWS, slice(0, KWIN), TOKROWS * w), xwin[:, 3 * g + w, :], TOKROWS)
                ins.then_inc(S["xT_tr"], 1)
            pe.wait_ge(S["xT_cp_a"], NTR // 2)
            pe.wait_ge(S["xT_cp_v"], NTR // 2)
            pe.wait_ge(S["weff_done"], 1)
            pe.wait_ge(S["vcol_done"], 1)
            for t in range(2):
                for k in range(ROWG * CH):
                    ins = mm(cols(6 + t, HALF), wshift[:, 0, k // CH, D * (k % CH):D * (k % CH) + D],
                             xT[:, k, :, 48 * t:48 * t + 48].rearrange("p w n -> p n w"), start=(k == 0), stop=(k == ROWG * CH - 1))
                ins.then_inc(S["conv_done"], 1)

            def mean(n, t, src, ready, value):
                pe.wait_ge(ready, value)
                mm(cols(6 + t, HALF), meanw, src[:, half(t)], start=True, stop=True).then_inc(S["ln_mean"], 1)

            def stat(n, t):
                pe.wait_ge(S["ln_sq"], 2 * n + t + 1)
                for c in range(HCH):
                    ins = mm(cols(6 + t, 1, slice(0, CHUNK), 300 + c), sq[:, HALF * t + CHUNK * c:HALF * t + CHUNK * c + CHUNK],
                             meanw[:, 0:1], start=True, stop=True)
                ins.then_inc(S["ln_stat"], 1)

            def bcast(n, t):
                pe.wait_ge(S["ln_rs"], 2 * n + t + 1)
                for c in range(HCH):
                    ins = mm(cols(6 + t, CHUNK, at=CHUNK * c), rs[:, t, c:c + 1].broadcast_to([CHUNK, 128]), ident[0:CHUNK, 0:CHUNK],
                             start=True, stop=True)
                ins.then_inc(S["ln_rb"], 1)

            def norm(n, src, ready, value):
                for t in range(2):
                    mean(n, t, src, ready, value + t)
                for t in range(2):
                    stat(n, t)
                for t in range(2):
                    bcast(n, t)

            norm(0, X1, S["ln_src"], 1)
            pe.wait_ge(S["in_dense"], 16)
            for t in range(2):
                pe.wait_ge(S["h_done"], t + 1)
                mm(cols(t, HALF), densew[:, :], hn[:, half(t)], start=True, stop=True).then_inc(S["dense_done"], 1)
            norm(1, H0, S["ln_src"], 3)
            pe.wait_ge(S["att_zero"], 3)
            pe.wait_ge(S["cstb_done"], 1)

            with pe.Fori(0, LAYERS) as l:
                pe.wait_ge(S["in_layer"], 96 * l + 96)
                for n in range(3):
                    ins = turn(cols(4, 128, at=128 * n), nqkvo[:, n, :], 128)
                ins.then_inc(S["tr_qkv"], 1)
                pe.wait_ge(S["wo_dup"], 2 * l + 2)
                for s in range(2):
                    ins = turn(cols(5, 128, at=128 * s), nWo2[:, s, :, :, :].rearrange("p c j e -> p (c j e)"), 128)
                ins.then_inc(S["tr_wo"], 1)
                for m in range(MC):
                    ins = turn(cols(2, 128, at=128 * m), nW1[:, m, :], 128)
                ins.then_inc(S["tr_w1"], 1)
                for m in range(MC):
                    ins = turn(cols(3, 128, at=128 * m), nW2[:, m, :], 128)
                ins.then_inc(S["tr_w2"], 1)
                pe.wait_ge(S["w_qkv"], l + 1)
                for t in range(2):
                    bq, bk, bv = BANK_QKV[t]
                    pe.wait_ge(S["x_ready"], 2 * l + t + 1)
                    if t == 1:
                        pe.wait_ge(S["w_o"], l + 1)
                    for b, n in ((bq, 0), (bk, 1)):
                        for u in range(2):
                            for j in range(2):
                                ins = mm(cols(b, HALF // 2, slice(64 * j, 64 * j + 64), HALF // 2 * u), tqkv[:, n, 64 * u:64 * u + 64],
                                         of_image(X[:, half(t)], j), start=True, stop=True)
                    ins.then_inc(S["qk_proj"], 1)
                    for a in range(HPAIR):
                        for j in range(2):
                            at = HALF * t + 2 * SEQ * a + SEQ * j
                            ins = mm(cols(bv, 128, slice(64 * j, 64 * j + SEQ), 128 * a), X[:, at:at + SEQ], tqkv[:, 2, :], start=True, stop=True)
                    ins.then_inc(S["v_proj"], 1)

                def approx(p):
                    t = p // HPAIR
                    pe.wait_ge(S["qk_ev"], 2 * l + t + 1)
                    pe.wait_ge(S["kx_done"], 2 * l + t + 1)
                    if p >= 1:
                        pe.wait_ge(S["dmax_done"], PAIRS * l + p)
                    for u in range(2):
                        ins = mm(cols(u, HALF), qdb[:, p, u, :, :].rearrange("p j q -> p (j q)"), kxb[:, p, u, :, :], start=True, stop=True)
                    ins.then_inc(S["sc_max"], 1)

                def scores(p):
                    b = 2 + 2 * (p % 2)
                    pe.wait_ge(S["qx_done"], 2 * l + p // HPAIR + 1)
                    if p == 0:
                        pe.wait_ge(S["w_1"], l + 1)
                        pe.wait_ge(S["w_2"], l + 1)
                    if p == 1:
                        pe.wait_ge(S["qk_ev"], 2 * l + 2)
                    if p >= 2:
                        pe.wait_ge(S["exp_done"], PAIRS * l + p - 1)
                    for u in range(2):
                        mm(cols(b + u, HALF), kd[:, p, u, :, :].rearrange("p j q -> p (j q)"), qx[:, p, u, :, :], start=True, stop=False)

                def less_max(p):
                    b = 2 + 2 * (p % 2)
                    pe.wait_ge(S["dmax_done"], PAIRS * l + p + 1)
                    for u in range(2):
                        ins = mm(cols(b + u, HALF), sameimg_b, dmax[:, p % 2, HSUB * u:HSUB * u + HSUB, :], start=False, stop=True)
                    ins.then_inc(S["scores_done"], 1)

                def values(p):
                    b = 6 + p % 2
                    pe.wait_ge(S["exp_done"], PAIRS * l + p + 1)
                    if p < 2:
                        pe.wait_ge(S["v_ev"], 2 * l + 2)
                    if p >= 2:
                        pe.wait_ge(S["o_done"], PAIRS * l + p - 1)
                    for h in range(HEADS):
                        u, c = h // 4, h % 4
                        w = pT[:, p % 2, u, 2 * SEQ * c:2 * SEQ * c + 2 * SEQ]
                        r = slice(32 * c, 32 * c + 32)
                        mm(cols(b, 2 * SEQ, r, 2 * SEQ * u), vd[:, p, h, :, :].rearrange("p j e -> p (j e)"), w, start=True, stop=True)
                        ins = mm(cols(b, 2 * SEQ, r, 144 + 2 * SEQ * u), cst[:, C_SUMIMG:C_SUMIMG + 32], w, start=True, stop=True)
                    ins.then_inc(S["pv_done"], 1)

                approx(0)
                for p in range(PAIRS):
                    scores(p)
                    if p >= 1:
                        values(p - 1)
                    less_max(p)
                    if p + 1 < PAIRS:
                        approx(p + 1)
                values(PAIRS - 1)

                for t in range(2):
                    pe.wait_ge(S["o_done"], PAIRS * l + HPAIR * t + HPAIR)
                    if t == 0:
                        pe.wait_ge(S["w_o"], l + 1)
                    for j in range(2):
                        for s in range(2):
                            ins = mm(of_image(cols(t, HALF), j), tWo[:, s, j, :],
                                     o[:, s, HPAIR * t:HPAIR * t + HPAIR, :].rearrange("p a q -> p (a q)"), start=(s == 0), stop=(s == 1))
                    ins.then_inc(S["wo_ps"], 1)
                    pe.wait_ge(S["osq_done"], PAIRS * l + HPAIR * t + HPAIR)
                    for c in range(2):
                        for s in range(2):
                            a = HPAIR * t + 2 * c
                            ins = mm(cols(t, 2, slice(0, RCH), 300 + 2 * c), osq[:, s, a:a + 2, :].rearrange("p a q -> p (a q)"),
                                     cst[:, C_RMS:C_RMS + 2], start=(s == 0), stop=(s == 1))
                    ins.then_inc(S["rms_ps"], 1)
                for m in range(MC):
                    ins = mm(cols(7, 1, at=400 + m), tW1[:, m, :], lp[:, L_B:L_B + 1], start=True, stop=True)
                ins.then_inc(S["b1_ps"], 1)
                for t in range(2):
                    pe.wait_ge(S["rms_r"], 2 * l + t + 1)
                    for j in range(2):
                        for c in range(2):
                            ins = mm(of_image(cols(2 + t, HALF), j)[:, 2 * c:2 * c + 2, :], rs[0:RCH, t, 2 * c + j:2 * c + j + 1].broadcast_to([RCH, 128]),
                                     ident[0:RCH, 0:RCH], start=True, stop=True)
                    ins.then_inc(S["rms_rb"], 1)
                pe.wait_ge(S["b1_done"], l + 1)
                norm(l + 2, X1, S["ln_src"], 2 * l + 5)
                for t in range(2):
                    pe.wait_ge(S["h_done"], 2 * l + 2 + t + 1)
                    for m in range(MC):
                        if t == 1 and m >= 2:
                            pe.wait_ge(S["gelu_done"], 2 * MC * l + m - 1)
                        mm(cols(BANK_UP[MC * t + m], HALF), tW1[:, m, :], hn[:, half(t)], start=True, stop=True).then_inc(S["ffn1"], 1)
                for t in range(2):
                    for m in range(MC):
                        pe.wait_ge(S["gelu_done"], 2 * MC * l + MC * t + m + 1)
                        ins = mm(cols(6 + t, HALF), tW2[:, m, :], gact[:, t, m, :], start=(m == 0), stop=(m == MC - 1))
                    ins.then_inc(S["ffn2"], 1)

            pe.wait_ge(S["in_exp"], 16)
            pe.wait_ge(S["in_sw"], 48)
            n = LAYERS + 2
            for t in range(2):
                mean(n, t, X, S["x_ready"], 2 * LAYERS + t + 1)
            turn(cols(0, EXPERTS), swn[:, :], EXPERTS).then_inc(S["sw_tr"], 1)
            for t in range(2):
                stat(n, t)
            for g in range(2):
                for k in range(4):
                    ins = turn(cols(2 + g, 128, at=128 * k), nexp[:, 4 * g + k, :], 128)
                ins.then_inc(S["exp_tr"], 1)
            for t in range(2):
                bcast(n, t)
            for g in range(2, 4):
                for k in range(4):
                    ins = turn(cols(2 + g, 128, at=128 * k), nexp[:, 4 * g + k, :], 128)
                ins.then_inc(S["exp_tr"], 1)
            norm(LAYERS + 3, X1, S["ln_src"], 2 * LAYERS + 5)
            pe.wait_ge(S["swT_done"], 1)
            for c in range(NCH):
                if c % HCH == 0:
                    pe.wait_ge(S["x_ready"], 2 * LAYERS + 2 + c // HCH + 1)
                ins = mm(cols(0, EXPERTS, slice(0, CHUNK), EXPERTS * c), X[:, CHUNK * c:CHUNK * c + CHUNK], swT[:, :], start=True, stop=True)
            ins.then_inc(S["lg_ps"], 1)
            pe.wait_ge(S["oh_done"], 1)
            for c in range(NCH):
                dst = cols(1, EXPERTS, slice(0, CHUNK), EXPERTS * c)
                for k in range(c):
                    mm(dst, cstb[0:CHUNK, C_ONE:C_ONE + CHUNK], ohb[:, k, :], start=(k == 0), stop=False)
                ins = mm(dst, cstb[0:CHUNK, C_CUM:C_CUM + CHUNK], ohb[:, c, :], start=(c == 0), stop=True)
            ins.then_inc(S["cum_ps"], 1)
            pe.wait_ge(S["route_done"], 1)
            pe.wait_ge(S["exp_cp_a"], 2)
            pe.wait_ge(S["exp_cp_v"], 2)
            for c in range(NCH):
                ins = turn(cols(2 + c // HCH, CHUNK, slice(0, EXPERTS + 2), CHUNK * (c % HCH)), route[:, c, :], CHUNK)
            ins.then_inc(S["route_tr"], 1)
            pe.wait_ge(S["routeT_done"], 1)

            def mask(e):
                b = 2 + 2 * (e % 2)
                if e >= 2:
                    pe.wait_ge(S["xm_done"], e - 1)
                for t in range(2):
                    ins = mm(cols(b + t, HALF), identb[0:EXPERTS + 2, e:e + 1].broadcast_to([EXPERTS + 2, 128]), routeTb[:, half(t)],
                             start=True, stop=True)
                ins.then_inc(S["mask_ps"], 1)

            mask(0)
            mask(1)
            for t in range(2):
                mm(cols(t, HALF), ident[0:EXPERTS + 2, EXPERTS + 1:EXPERTS + 2].broadcast_to([EXPERTS + 2, 128]), routeT[:, half(t)],
                   start=True, stop=True).then_inc(S["rp_ps"], 1) if t == 1 else mm(
                       cols(t, HALF), ident[0:EXPERTS + 2, EXPERTS + 1:EXPERTS + 2].broadcast_to([EXPERTS + 2, 128]), routeT[:, half(t)],
                       start=True, stop=True)
            for t in range(2):
                mm(cols(6 + t, HALF), ebn[:, :], routeT[0:EXPERTS, half(t)], start=True, stop=False)
            for e in range(EXPERTS + 1):
                pe.wait_ge(S["xm_done"], e + 1)
                for t in range(2):
                    ins = mm(cols(6 + t, HALF), texp[:, e, :] if e < EXPERTS else ident, xm[:, e % 3, half(t)],
                             start=False, stop=(e == EXPERTS))
                ins.then_inc(S["exp_ps"], 1)
                if e + 2 <= EXPERTS:
                    mask(e + 2)
            for t in range(2):
                pe.wait_ge(S["y_done"], t + 1)
                for c in range(HCH):
                    ins = turn(cols(2 + t, 128, slice(0, CHUNK), 128 * c), hn[:, HALF * t + CHUNK * c:HALF * t + CHUNK * c + CHUNK], 128)
                ins.then_inc(S["y_tr"], 1)


_ORDER = ['x', 'L0_tok_conv_w', 'L0_tok_conv_b', 'L0_tok_gamma', 'L0_tok_beta', 'L0_tok_dense_w', 'L0_tok_dense_b',
          'L0_attn_Wq', 'L0_attn_Wk', 'L0_attn_Wv', 'L0_attn_rms_w', 'L0_attn_Wo', 'L0_attn_bo', 'L0_attn_diffw',
          'L0_attn_g_ffn', 'L0_attn_b_ffn', 'L0_attn_W1', 'L0_attn_b1', 'L0_attn_W2', 'L0_attn_b2', 'L0_attn_g_f',
          'L0_attn_b_f', 'L0_ffn_switch_w', 'L0_ffn_switch_b', 'L0_ffn_expert_w', 'L0_ffn_expert_b']


def kernel(**inputs):
    import concourse.bacc as bacc
    from concourse.bass_utils import run_bass_kernel_spmd

    nc = bacc.Bacc("TRN2", target_bir_lowering=False, num_devices=1)
    arrays, args = {}, []
    for name in _ORDER + ['consts']:
        a = constants() if name == 'consts' else np.ascontiguousarray(inputs[name])
        arrays[f"in_{name}_dram"] = a
        args.append(nc.dram_tensor(f"in_{name}_dram", a.shape, mybir.dt.from_np(a.dtype), kind="ExternalInput").ap())
    args.append(nc.dram_tensor("out_0_dram", (IMGS, SEQ, D), F32, kind="ExternalOutput").ap())
    vit_tower(nc, *args)
    r = run_bass_kernel_spmd(nc, [arrays], core_ids=[0])
    return r.results[0]["out_0_dram"]
```

```python
from contextlib import ExitStack

import numpy as np

import concourse.bass as bass
from concourse import mybir

F32 = mybir.dt.float32
BF16 = mybir.dt.bfloat16
ALU = mybir.AluOpType
ACT = mybir.ActivationFunctionType
AX_X = mybir.AxisListType.X

IMGS, SIDE, CH, PATCH = 16, 96, 3, 16
GRID = SIDE // PATCH
SEQ = GRID * GRID
TOK = IMGS * SEQ
D = 128
LAYERS, HEADS, MLP, EXPERTS = 4, 8, 512, 16
EDIM = D // HEADS
FDIM = EDIM // 2
CAPACITY = int(1.2 * TOK / EXPERTS)
EPS_TOK, EPS_LN, EPS_RMS = 1e-3, 1e-5, 1.1920929e-07

PAIRS = IMGS // 2
HALF = TOK // 2
HPAIR = PAIRS // 2
CHUNK = 96
HCH = HALF // CHUNK
RCH = 2 * SEQ
HSUB = HEADS * 2 // 2
MC = MLP // D
WIN = PATCH + 2
RHO = 6
ROWG = WIN // RHO
KWIN = RHO * WIN
ROWPITCH = SIDE * CH + 48
TOKROWS = IMGS * GRID

C_IDENT, C_MEAN, C_SAMEIMG, C_SUMIMG = 0, 128, 256, 384
C_RMS, C_SUB, C_SELQ, C_CUM, C_ONE = 416, 418, 426, 462, 558
C_RANK, C_TOP, C_BOT, C_POW, C_END = 654, 670, 671, 672, 676

V_BO, V_G, V_B, V_B2, V_B1, V_RMS = 0, 4, 8, 12, 16, 32
V_CONVB, V_GAMMA, V_BETA, V_DENSEB, V_GF, V_BF, V_END = 40, 41, 42, 43, 44, 45, 46
L_BO, L_G, L_B, L_B2, L_B1, L_RMS, L_NDW, L_OMD, L_END = 0, 1, 2, 3, 4, 8, 12, 13, 14


def constants():
    c = np.zeros((128, C_END), np.float32)
    p = np.arange(128)
    c[:, C_IDENT:C_IDENT + 128] = np.eye(128)
    c[:, C_MEAN:C_MEAN + 128] = 1.0 / D
    f = np.arange(128)
    c[:, C_SAMEIMG:C_SAMEIMG + 128] = (p[:, None] // 64 == f[None] // 64) & (f[None] % 64 < SEQ)
    f = np.arange(32)
    c[:, C_SUMIMG:C_SUMIMG + 32] = (p[:, None] // 64 == f[None] // 16) & (p[:, None] % 64 < SEQ)
    c[:, C_RMS:C_RMS + 2] = (p[:, None] // 16 % 2 == np.arange(2)[None]) / D
    c[:, C_SUB:C_SUB + HSUB] = p[:, None] // FDIM % HSUB == np.arange(HSUB)[None]
    c[:, C_SELQ:C_SELQ + SEQ] = p[:, None] % 64 == np.arange(SEQ)[None]
    c[:, C_CUM:C_CUM + CHUNK] = p[:, None] <= np.arange(CHUNK)[None]
    c[:, C_ONE:C_ONE + CHUNK] = 1.0
    c[:, C_RANK:C_RANK + EXPERTS] = EXPERTS - np.arange(EXPERTS)[None]
    c[:, C_TOP] = p % GRID != 0
    c[:, C_BOT] = p % GRID != GRID - 1
    c[:, C_POW:C_POW + 4] = -0.5
    return c


class Chain:

    def __init__(self, eng, sem):
        self.eng, self.sem, self.base, self.n = eng, sem, 0, 0

    def step(self, ins, meanwhile=None):
        self.n += 1
        ins.then_inc(self.sem, 1)
        if meanwhile:
            meanwhile()
        self.eng.wait_ge(self.sem, self.base + self.n)

    def rebase(self, base):
        self.base, self.n = base, 0


DVE_BEFORE, DVE_LAYER = 6, 19


def vit_tower(nc, x, conv_w, conv_b, gamma, beta, dense_w, dense_b, Wq, Wk, Wv, rms_w, Wo, bo, diffw,
              g_ffn, b_ffn, W1, b1, W2, b2, g_f, b_f, switch_w, switch_b, expert_w, expert_b, consts, out):
    ctx = ExitStack()
    with ctx:
        def sb(name, shape, dt=F32):
            return ctx.enter_context(nc.sbuf_tensor(name, shape, dt))

        def sem(name):
            return ctx.enter_context(nc.semaphore(name))

        ps = ctx.enter_context(nc.psum_tensor("ps", [128, 8, 512], F32))

        cst = sb("cst", [128, C_END])
        ident = cst[:, C_IDENT:C_IDENT + 128]
        meanw = cst[:, C_MEAN:C_MEAN + 128]
        cstb = sb("cstb", [128, C_RANK], BF16)
        identb = cstb[:, C_IDENT:C_IDENT + 128]
        sameimg_b = cstb[:, C_SAMEIMG:C_SAMEIMG + 128]
        selq_b = cstb[:, C_SELQ:C_SELQ + SEQ]
        vrow = sb("vrow", [V_END, 128])
        vcol = sb("vcol", [128, V_END])
        dwb = sb("dwb", [128, LAYERS])
        params = sb("params", [128, LAYERS, L_END])
        lp = sb("lp", [128, L_END])
        imgbuf = sb("imgbuf", [128, WIN * ROWPITCH])
        winbuf = sb("winbuf", [128, ROWG * CH * GRID * KWIN])
        ximg = imgbuf[0:TOKROWS, :].rearrange("p (u f) -> p u f", u=WIN)
        xwin = winbuf[0:TOKROWS, :].rearrange("p (g k) -> p g k", k=KWIN)
        xT = sb("xT", [KWIN, ROWG * CH, GRID, TOKROWS])
        wbuf = sb("wbuf", [128, 5 * ROWG * CH * D])
        wshift = wbuf[0:KWIN, :].rearrange("p (g a f) -> p g a f", g=5, a=ROWG)
        densew = sb("densew", [128, 128])
        X = sb("X", [128, TOK])
        X1 = sb("X1", [128, TOK])
        H0 = sb("H0", [128, TOK])
        xc = sb("xc", [128, TOK])
        sq = sb("sq", [128, TOK])
        hn = sb("hn", [128, TOK])
        ms = sb("ms", [CHUNK, 2, 4])
        rs = sb("rs", [CHUNK, 2, 4])
        ao = sb("ao", [128, 2, HALF])
        nqkvo = sb("nqkvo", [128, 4, 128])
        nW1 = sb("nW1", [128, MC, 128])
        nW2 = sb("nW2", [128, MC, 128])
        nWo2 = sb("nWo2", [128, 2, 4, 2, EDIM])
        tqkv = sb("tqkv", [128, 3, 128])
        tWo = sb("tWo", [128, 2, 2, 128])
        tW1 = sb("tW1", [128, MC, 128])
        tW2 = sb("tW2", [128, MC, 128])
        b1e = sb("b1e", [128, MC])
        qS = sb("qS", [128, 2, 2, HPAIR, SEQ])
        kSb = sb("kSb", [128, 2, 2, HPAIR, SEQ], BF16)
        qx = sb("qx", [128, PAIRS, 2, HSUB, SEQ])
        kxb = sb("kxb", [128, PAIRS, 2, HSUB, SEQ], BF16)
        kd = sb("kd", [128, PAIRS, 2, 2, 64])
        qdb = sb("qdb", [128, PAIRS, 2, 2, 64], BF16)
        vd = sb("vd", [128, PAIRS, HEADS, 2, EDIM])
        nmax = sb("nmax", [128, 2, 2 * HSUB], BF16)
        dmax = sb("dmax", [128, 2, 2 * HSUB, SEQ], BF16)
        pT = sb("pT", [128, 2, 2, HSUB * SEQ])
        rden = sb("rden", [128, 2, 2, 2, SEQ])
        on = sb("on", [128, 2, 2, 2, SEQ])
        o = sb("o", [128, 2, PAIRS, SEQ])
        osq = sb("osq", [128, 2, PAIRS, SEQ])
        xa = hn[:, :].rearrange("p (t n) -> p t n", t=2)
        table = sb("table", [1, 1])
        gact = sb("gact", [128, 2, MC, HALF])
        swn = sb("swn", [EXPERTS, 128])
        swT = sb("swT", [128, EXPERTS])
        swb = sb("swb", [CHUNK, EXPERTS])
        ebn = sb("ebn", [EXPERTS, 128])
        nexp = imgbuf[:, 0:EXPERTS * 128].rearrange("p (e d) -> p e d", e=EXPERTS)
        texp = winbuf[:, 0:EXPERTS * 128].rearrange("p (e d) -> p e d", e=EXPERTS)
        NCH = TOK // CHUNK
        lg = sb("lg", [CHUNK, NCH, EXPERTS])
        eg = sb("eg", [CHUNK, NCH, EXPERTS])
        ohf = sb("ohf", [CHUNK, NCH, EXPERTS])
        ohb = sb("ohb", [CHUNK, NCH, EXPERTS], BF16)
        r1 = sb("r1", [CHUNK, 8, NCH])
        route = sb("route", [CHUNK, NCH, EXPERTS + 2])
        routeT = sb("routeT", [EXPERTS + 2, TOK])
        routeTb = sb("routeTb", [EXPERTS + 2, TOK], BF16)
        xm = wbuf[:, 0:3 * TOK].rearrange("p (b n) -> p b n", b=3)
        rpb = wbuf[:, 3 * TOK:4 * TOK]
        fin = wbuf[0:CHUNK, 4 * TOK:4 * TOK + NCH * 128].rearrange("p (c d) -> p c d", c=NCH)

        names = """in_x0 in_x1 in_x2 in_top in_bot in_w0 in_w1 in_w2 in_w3 in_w4 in_c in_vec in_rms in_dense in_sw in_layer in_exp out_done
            halo_zero w_zero w_zero_p att_zero ximg_ok win_done xT_tr xT_cp weff_done conv_done dense_done
            cstb_done vec_tr vcol_done params_done lp_done dvc
            ln_src ln_mean ln_cent ln_sq ln_stat ln_var ln_rs ln_rb h_done x_ready
            tr_qkv tr_wo tr_w1 tr_w2 wo_dup w_qkv w_o w_1 w_2 b1_done
            qk_proj v_proj qk_ev v_ev q_sb k_sb qx_done qx_act kx_done sc_max sc_read nmax_done dmax_done scores_done exp_done pv_done
            o_done osq_done wo_ps rms_ps rms_ms rms_r rms_rb wo_sb ffn1 gelu_done ffn2
            sw_tr swT_done exp_tr exp_cp_a exp_cp_v lg_ps lg_done eg_done oh_done cum_ps route_done route_tr routeT_done
            mask_ps xm_done exp_ps rp_ps rp_sb y_done y_tr fin_a fin_v acopy""".split()
        S = {n: sem(n) for n in names}

        def half(t):
            return slice(HALF * t, HALF * t + HALF)

        def of_image(tokens, j):
            return tokens.rearrange("p (a j q) -> p a j q", j=2, q=SEQ)[:, :, j, :]

        def cols(bank, n, rows=slice(0, 128), at=0):
            return ps[rows, bank, at:at + n]

        SHIFTS = [(1, 1), (1, 0), (1, 2), (0, 1), (2, 1)]
        BANK_QKV = [(0, 1, 6), (4, 5, 7)]
        BANK_VALUE = [6, 7, 6, 7, 6, 6, 6, 1]
        BANK_NORM = [6, 7]
        BANK_POST = [7, 0]
        BANK_WO = [7, 1]
        BANK_UP = [2, 3, 4, 5, 1, 2, 3, 4]
        SPREAD_DVE = [6, 4]
        NTR = ROWG * CH * 2

        def load_shifted(eng, g, landed):
            du, dv = SHIFTS[g]
            for r in range(RHO):
                a0 = 1 if r < du else 0
                i0 = RHO * a0 + r - du
                n = (PATCH - 1 - i0) // RHO + 1
                dst = wshift[WIN * r + dv:WIN * r + dv + PATCH, g, a0:a0 + n, :]
                src = conv_w[i0::RHO, :, CH * g:CH * g + CH, :].rearrange("i j c d -> j i (c d)")
                eng.dma_start(dst, src).then_inc(landed, 16)

        block = ctx.enter_context(nc.Block())

        @block.sync
        def _(sp):
            rows = x.rearrange("b h w c -> (b h) (w c)")
            main = rows.rearrange("(n u) f -> n u f", u=PATCH)
            row = slice(CH, CH + SIDE * CH)
            sp.dma_start(ximg[:, 1:6, row], main[:, 0:5, :]).then_inc(S["in_x0"], 16)
            sp.dma_start(cst[:, :], consts).then_inc(S["in_c"], 16)
            sp.wait_ge(S["halo_zero"], 1)
            sp.dma_start(ximg[1:TOKROWS, 0, row], rows[PATCH - 1:IMGS * SIDE - 1:PATCH, :]).then_inc(S["in_top"], 16)
            sp.dma_start(ximg[:, 6:12, row], main[:, 5:11, :]).then_inc(S["in_x1"], 16)
            sp.dma_start(ximg[:, 12:17, row], main[:, 11:16, :]).then_inc(S["in_x2"], 16)
            sp.dma_start(ximg[0:TOKROWS - 1, WIN - 1, row], rows[PATCH:IMGS * SIDE:PATCH, :]).then_inc(S["in_bot"], 16)
            for g in range(4):
                if g < 3:
                    sp.wait_ge(S["w_zero"], g + 1)
                else:
                    sp.wait_ge(S["w_zero_p"], 1)
                load_shifted(sp, g, S[f"in_w{g}"])
            for v, n, src in ((V_BO, 4, bo), (V_G, 4, g_ffn), (V_B, 4, b_ffn), (V_B2, 4, b2),
                              (V_B1, 16, b1.rearrange("l (m p) -> (l m) p", p=128))):
                sp.dma_start(vrow[v:v + n, :], src).then_inc(S["in_vec"], 16)
            for v, src in ((V_CONVB, conv_b), (V_GAMMA, gamma), (V_BETA, beta), (V_DENSEB, dense_b),
                           (V_GF, g_f), (V_BF, b_f)):
                sp.dma_start(vrow[v:v + 1, :], src.rearrange("(a d) -> a d", a=1)).then_inc(S["in_vec"], 16)

            def load_layer(l):
                for n, w in enumerate((Wq, Wk, Wv, Wo)):
                    sp.dma_start(nqkvo[:, n, :], w[bass.ds(l, 1), :, :].rearrange("l a b -> (l a) b")).then_inc(S["in_layer"], 16)
                sp.dma_start(nW1[:, :, :], W1[bass.ds(l, 1), :, :].rearrange("l (m p) d -> p (l m) d", p=128)).then_inc(S["in_layer"], 16)
                sp.dma_start(nW2[:, :, :], W2[bass.ds(l, 1), :, :].rearrange("l p (m k) -> p (l m) k", m=MC)).then_inc(S["in_layer"], 16)

            load_layer(0)
            with sp.Fori(1, LAYERS) as l:
                sp.wait_ge(S["tr_w2"], l)
                load_layer(l)
            sp.wait_ge(S["fin_a"], 1)
            sp.wait_ge(S["fin_v"], 1)
            sp.dma_start(out.rearrange("b s d -> (b s) d").rearrange("(c p) d -> p c d", p=CHUNK),
                         fin[:, :, :]).then_inc(S["out_done"], 16)
            sp.wait_ge(S["out_done"], 16)

        @block.gpsimd
        def _(pool):
            nc.gpsimd.memset(wshift[:, 3:5, :, :], 0.0).then_inc(S["w_zero_p"], 1)
            pool.wait_ge(S["w_zero_p"], 1)
            load_shifted(pool, 4, S["in_w4"])
            for j in range(2):
                dst = vrow[V_RMS:V_RMS + 8, :].rearrange("p (c j e) -> p c j e", c=4, j=2)[:, :, j, :]
                pool.dma_start(dst, rms_w.rearrange("l (s c) e -> (l s) c e", s=2)).then_inc(S["in_rms"], 16)
            pool.dma_start(dwb[:, :], diffw.rearrange("(a l) -> a l", a=1).broadcast_to([128, LAYERS])).then_inc(S["in_rms"], 16)
            pool.dma_start(densew[:, :], dense_w).then_inc(S["in_dense"], 16)
            nc.gpsimd.memset(kd[:, :, :, :, :], 0.0).then_inc(S["att_zero"], 1)
            nc.gpsimd.memset(qdb[:, :, :, :, :], 0.0).then_inc(S["att_zero"], 1)
            nc.gpsimd.memset(vd[:, :, :, :, :], 0.0).then_inc(S["att_zero"], 1)
            pool.dma_start(swn[:, :], switch_w).then_inc(S["in_sw"], 16)
            pool.dma_start(swb[:, :], switch_b.rearrange("(a l) -> a l", a=1).broadcast_to([CHUNK, EXPERTS])).then_inc(S["in_sw"], 16)
            pool.dma_start(ebn[:, :], expert_b).then_inc(S["in_sw"], 16)
            pool.wait_ge(S["win_done"], ROWG * CH)
            pool.dma_start(nexp[:, :, :], expert_w.rearrange("e f d -> f e d")).then_inc(S["in_exp"], 16)

            def power(n, t):
                pool.wait_ge(S["ln_var"], 2 * n + t + 1)
                nc.gpsimd.tensor_tensor(rs[:, t, 0:HCH], ms[:, t, 0:HCH], cst[0:CHUNK, C_POW:C_POW + HCH],
                                        ALU.pow).then_inc(S["ln_rs"], 1)

            pool.wait_ge(S["in_c"], 16)
            for n in range(2):
                for t in range(2):
                    power(n, t)
            with pool.Fori(0, LAYERS) as l:
                pool.wait_ge(S["in_layer"], 96 * l + 96)
                ones_of_heads = cst[:, C_ONE:C_ONE + EDIM].rearrange("p (h e) -> p h e", h=1).broadcast_to([128, HEADS, EDIM])
                for j in range(2):
                    cols_of_heads = nqkvo[:, 3, :].rearrange("p (h e) -> p h e", e=EDIM)
                    nc.gpsimd.tensor_tensor(nWo2[:, :, :, j, :].rearrange("p s c e -> p (s c) e"),
                                            cols_of_heads, ones_of_heads, ALU.mult).then_inc(S["wo_dup"], 1)

                def diagonal(p):
                    pool.wait_ge(S["nmax_done"], PAIRS * l + p + 1)
                    if p >= 2:
                        pool.wait_ge(S["scores_done"], PAIRS * l + p - 1)
                    nc.gpsimd.tensor_tensor(dmax[:, p % 2, :, :], selq_b.rearrange("p (a q) -> p a q", a=1).broadcast_to([128, 2 * HSUB, SEQ]),
                                            nmax[:, p % 2, :].rearrange("p (a q) -> p a q", q=1).broadcast_to([128, 2 * HSUB, SEQ]),
                                            ALU.mult).then_inc(S["dmax_done"], 1)

                def inverse_rms(t):
                    pool.wait_ge(S["rms_ms"], 2 * l + t + 1)
                    nc.gpsimd.tensor_tensor(rs[0:RCH, t, 0:4], ms[0:RCH, t, 0:4], cst[0:RCH, C_POW:C_POW + 4],
                                            ALU.pow).then_inc(S["rms_r"], 1)

                for p in range(PAIRS - 1):
                    diagonal(p)
                inverse_rms(0)
                diagonal(PAIRS - 1)
                power(l + 2, 0)
                inverse_rms(1)
                power(l + 2, 1)
            for n in (LAYERS + 2, LAYERS + 3):
                for t in range(2):
                    power(n, t)

        @block.scalar
        def _(act):
            act.wait_ge(S["in_c"], 16)
            act.wait_ge(S["halo_zero"], 1)
            act.wait_ge(S["in_top"], 16)
            nc.scalar.activation(ximg[:, 0, :], ximg[:, 0, :], ACT.Copy, scale=cst[0:TOKROWS, C_TOP:C_TOP + 1]).then_inc(S["ximg_ok"], 1)
            act.wait_ge(S["in_bot"], 16)
            nc.scalar.activation(ximg[:, WIN - 1, :], ximg[:, WIN - 1, :], ACT.Copy, scale=cst[0:TOKROWS, C_BOT:C_BOT + 1]).then_inc(S["ximg_ok"], 1)
            for g in range(NTR):
                act.wait_ge(S["xT_tr"], g + 1)
                nc.scalar.copy(xT[:, g // 2, 3 * (g % 2):3 * (g % 2) + 3, :],
                               cols(g % 6, 3 * TOKROWS, slice(0, KWIN)).rearrange("p (w n) -> p w n", w=3)).then_inc(S["xT_cp"], 1)
            act.wait_ge(S["vec_tr"], 1)
            nc.scalar.copy(vcol[:, :], cols(5, V_END)).then_inc(S["vcol_done"], 1)

            def square(n, t):
                act.wait_ge(S["ln_cent"], 2 * n + t + 1)
                nc.scalar.activation(sq[:, half(t)], xc[:, half(t)], ACT.Square).then_inc(S["ln_sq"], 1)

            for n in range(2):
                for t in range(2):
                    square(n, t)
            act.wait_ge(S["att_zero"], 3)
            with act.Fori(0, LAYERS) as l:
                act.wait_ge(S["tr_qkv"], l + 1)
                nc.scalar.copy(tqkv[:, :, :], cols(4, 384)).then_inc(S["w_qkv"], 1)
                act.wait_ge(S["tr_w1"], l + 1)
                nc.scalar.copy(tW1[:, :, :], cols(2, 512)).then_inc(S["w_1"], 1)
                act.wait_ge(S["tr_w2"], l + 1)
                nc.scalar.copy(tW2[:, :, :], cols(3, 512)).then_inc(S["w_2"], 1)

                def spread_act(t):
                    act.wait_ge(S["q_sb"], 2 * l + t + 1)
                    pr = slice(HPAIR * t, HPAIR * t + HPAIR)
                    for a in range(SPREAD_DVE[t], HSUB):
                        last = nc.scalar.activation(qx[:, pr, :, a, :].rearrange("p a u q -> p u a q"), qS[:, t, :, :, :],
                                                    ACT.Copy, scale=cst[:, C_SUB + a:C_SUB + a + 1])
                    last.then_inc(S["qx_act"], 1)

                for t in range(2):
                    bq, bk, bv = BANK_QKV[t]
                    act.wait_ge(S["qk_proj"], 2 * l + t + 1)
                    q_v = cols(bq, HALF).rearrange("p (u a q) -> p u a q", u=2, q=SEQ)
                    k_v = cols(bk, HALF).rearrange("p (u a q) -> p u a q", u=2, q=SEQ)
                    nc.scalar.copy(qS[:, t, :, :, :], q_v).then_inc(S["q_sb"], 1)
                    pr = slice(HPAIR * t, HPAIR * t + HPAIR)
                    for j in range(2):
                        r = slice(64 * j, 64 * j + 64)
                        nc.scalar.copy(qdb[r, pr, :, j, 0:SEQ].rearrange("p a u q -> p u a q"), q_v[r])
                    act.wait_ge(S["k_sb"], 2 * l + t + 1)
                    for j in range(2):
                        r = slice(64 * j, 64 * j + 64)
                        last = nc.scalar.copy(kd[r, pr, :, j, 0:SEQ].rearrange("p a u q -> p u a q"), k_v[r])
                    last.then_inc(S["qk_ev"], 1)
                    if t == 0:
                        spread_act(0)
                    act.wait_ge(S["v_proj"], 2 * l + t + 1)
                    for j in range(2):
                        r = slice(64 * j, 64 * j + SEQ)
                        last = nc.scalar.copy(vd[r, pr, :, j, :], cols(bv, 512, r).rearrange("p (a h e) -> p a h e", a=HPAIR, h=HEADS))
                    last.then_inc(S["v_ev"], 1)

                def exps(p):
                    b = 2 + 2 * (p % 2)
                    act.wait_ge(S["scores_done"], PAIRS * l + p + 1)
                    if p >= 2:
                        act.wait_ge(S["pv_done"], PAIRS * l + p - 1)
                    nc.scalar.activation(pT[:, p % 2, :, :], ps[:, b:b + 2, 0:HALF], ACT.Exp,
                                         scale=float(FDIM) ** -0.5).then_inc(S["exp_done"], 1)

                def square_heads(p):
                    act.wait_ge(S["o_done"], PAIRS * l + p + 1)
                    nc.scalar.activation(osq[:, :, p, :], o[:, :, p, :], ACT.Square).then_inc(S["osq_done"], 1)

                def copy_out(t):
                    act.wait_ge(S["wo_ps"], 2 * l + t + 1)
                    nc.scalar.activation(ao[:, t, :], cols(BANK_WO[t], HALF), ACT.Copy, scale=lp[:, L_OMD:L_OMD + 1]).then_inc(S["wo_sb"], 1)

                def gelu(t, m):
                    act.wait_ge(S["ffn1"], 2 * MC * l + MC * t + m + 1)
                    nc.scalar.activation(gact[:, t, m, :], cols(BANK_UP[MC * t + m], HALF), ACT.Gelu,
                                         bias=b1e[:, m:m + 1]).then_inc(S["gelu_done"], 1)

                exps(0)
                spread_act(1)
                exps(1)
                for p in range(2, 5):
                    exps(p)
                    square_heads(p - 2)
                square_heads(3)
                exps(5)
                square_heads(4)
                copy_out(0)
                exps(6)
                square_heads(5)
                exps(7)
                square(l + 2, 0)
                square_heads(6)
                square_heads(7)
                nc.scalar.activation(table[:, :], cst[0:1, 0:1], ACT.Gelu)
                copy_out(1)
                act.wait_ge(S["b1_done"], l + 1)
                gelu(0, 0)
                gelu(0, 1)
                square(l + 2, 1)
                gelu(0, 2)
                gelu(0, 3)
                for m in range(MC):
                    gelu(1, m)
            for t in range(2):
                square(LAYERS + 2, t)
            act.wait_ge(S["sw_tr"], 1)
            nc.scalar.copy(swT[:, :], cols(0, EXPERTS)).then_inc(S["swT_done"], 1)
            for g in range(0, 4, 2):
                act.wait_ge(S["exp_tr"], g + 1)
                nc.scalar.copy(texp[:, 4 * g:4 * g + 4, :], cols(2 + g, 512)).then_inc(S["exp_cp_a"], 1)
            for t in range(2):
                square(LAYERS + 3, t)
            act.wait_ge(S["lg_done"], 1)
            nc.scalar.activation(eg[:, :, :], lg[:, :, :], ACT.Exp).then_inc(S["eg_done"], 1)
            act.wait_ge(S["rp_ps"], 1)
            nc.scalar.copy(rpb[:, :].rearrange("p (t n) -> p t n", t=2), ps[:, 0:2, 0:HALF]).then_inc(S["rp_sb"], 1)
            act.wait_ge(S["y_tr"], 1)
            nc.scalar.copy(fin[:, 0:HCH, :], cols(2, HCH * 128, slice(0, CHUNK))).then_inc(S["fin_a"], 1)

        @block.vector
        def _(dve):
            chain = Chain(dve, S["dvc"])
            nc.vector.memset(ximg[:, 0, :], 0.0)
            nc.vector.memset(ximg[:, WIN - 1, :], 0.0)
            nc.vector.memset(ximg[:, 1:WIN - 1, 0:CH], 0.0)
            nc.vector.memset(ximg[:, 1:WIN - 1, CH + SIDE * CH:SIDE * CH + 2 * CH], 0.0).then_inc(S["halo_zero"], 1)
            for g in range(3):
                nc.vector.memset(wshift[:, g, :, :], 0.0).then_inc(S["w_zero"], 1)

            dve.wait_ge(S["halo_zero"], 1)
            for a in range(ROWG):
                dve.wait_ge(S[f"in_x{a}"], 16)
                if a == 0:
                    dve.wait_ge(S["ximg_ok"], 1)
                if a == ROWG - 1:
                    dve.wait_ge(S["ximg_ok"], 2)
                for c in range(CH):
                    dst = xwin[:, (a * CH + c) * GRID:(a * CH + c + 1) * GRID, :].rearrange("n w (r v) -> n w r v", v=WIN)
                    rws = ximg[:, RHO * a:RHO * a + RHO, :]
                    body = rws[:, :, 0:GRID * 48].rearrange("n r (w v c) -> n w r v c", w=GRID, c=CH)[:, :, :, :, c]
                    tail = rws[:, :, 48:48 + GRID * 48].rearrange("n r (w v c) -> n w r v c", w=GRID, c=CH)[:, :, :, 0:2, c]
                    nc.vector.tensor_copy(dst[:, :, :, 0:PATCH], body)
                    nc.vector.tensor_copy(dst[:, :, :, PATCH:WIN], tail).then_inc(S["win_done"], 1)
            dve.wait_ge(S["in_c"], 16)
            nc.vector.tensor_copy(cstb[:, :], cst[:, 0:C_RANK]).then_inc(S["cstb_done"], 1)
            dve.wait_ge(S["in_w0"], 16 * RHO)
            for g in range(1, 5):
                dve.wait_ge(S[f"in_w{g}"], 16 * RHO)
                if g < 4:
                    chain.step(nc.vector.tensor_tensor(wshift[:, 0, :, :], wshift[:, 0, :, :], wshift[:, g, :, :], ALU.add))
            for a in range(ROWG):
                nc.vector.tensor_tensor(wshift[:, 0, a, :], wshift[:, 0, a, :], wshift[:, 4, a, :], ALU.add).then_inc(S["weff_done"], 1)
            dve.wait_ge(S["vcol_done"], 1)

            def center(n, t, src, bank=BANK_NORM):
                dve.wait_ge(S["ln_mean"], 2 * n + t + 1)
                nc.vector.tensor_tensor(xc[:, half(t)], src[:, half(t)], cols(bank[t], HALF), ALU.subtract).then_inc(S["ln_cent"], 1)

            def variance(n, t, eps, bank=BANK_NORM):
                dve.wait_ge(S["ln_stat"], 2 * n + t + 1)
                nc.vector.tensor_scalar(ms[:, t, 0:HCH], cols(bank[t], HCH, slice(0, CHUNK), 300), eps, None, ALU.add).then_inc(S["ln_var"], 1)

            def token_norm(t):
                dve.wait_ge(S["ln_rb"], t + 1)
                chain.step(nc.vector.scalar_tensor_tensor(hn[:, half(t)], xc[:, half(t)], vcol[:, V_GAMMA:V_GAMMA + 1],
                                                          cols(6 + t, HALF), ALU.mult, ALU.mult))
                nc.vector.tensor_scalar(hn[:, half(t)], hn[:, half(t)], vcol[:, V_BETA:V_BETA + 1], None, ALU.add).then_inc(S["h_done"], 1)

            def conv_bias(t):
                dve.wait_ge(S["conv_done"], t + 1)
                nc.vector.tensor_scalar(X1[:, half(t)], cols(6 + t, HALF), vcol[:, V_CONVB:V_CONVB + 1], None, ALU.add).then_inc(S["ln_src"], 1)

            def dense_bias(t):
                dve.wait_ge(S["dense_done"], t + 1)
                nc.vector.tensor_scalar(H0[:, half(t)], cols(t, HALF), vcol[:, V_DENSEB:V_DENSEB + 1], None, ALU.add).then_inc(S["ln_src"], 1)

            def scale_only(t):
                dve.wait_ge(S["ln_rb"], 2 + t + 1)
                nc.vector.tensor_tensor(X[:, half(t)], xc[:, half(t)], cols(6 + t, HALF), ALU.mult).then_inc(S["x_ready"], 1)

            conv_bias(0)
            center(0, 0, X1)
            variance(0, 0, EPS_TOK)
            conv_bias(1)
            token_norm(0)
            center(0, 1, X1)
            dense_bias(0)
            variance(0, 1, EPS_TOK)
            center(1, 0, H0)
            token_norm(1)
            variance(1, 0, EPS_LN)
            dense_bias(1)
            scale_only(0)
            center(1, 1, H0)
            dve.wait_ge(S["in_rms"], 48)
            nc.vector.tensor_copy(params[:, :, 0:4].rearrange("p l k -> p k l"), vcol[:, 0:16].rearrange("p (k l) -> p k l", k=4))
            nc.vector.tensor_copy(params[:, :, L_B1:L_B1 + MC], vcol[:, V_B1:V_B1 + 16].rearrange("p (l m) -> p l m", l=LAYERS))
            for s in range(2):
                for j in range(2):
                    k = L_RMS + 2 * s + j
                    nc.vector.tensor_scalar(params[:, :, k], vcol[:, V_RMS:V_RMS + 8].rearrange("p (l s) -> p l s", s=2)[:, :, s],
                                            cst[:, C_RMS + j:C_RMS + j + 1], float(D), ALU.mult, ALU.mult)
            nc.vector.tensor_scalar(params[:, :, L_NDW], dwb[:, :], -1.0, None, ALU.mult)
            chain.step(nc.vector.tensor_scalar(params[:, :, L_OMD], dwb[:, :], -1.0, 1.0, ALU.mult, ALU.add))
            nc.vector.tensor_tensor(params[:, :, L_BO], params[:, :, L_BO], params[:, :, L_OMD], ALU.mult).then_inc(S["params_done"], 1)
            variance(1, 1, EPS_LN)
            scale_only(1)
            assert chain.n == DVE_BEFORE, chain.n
            dve.wait_ge(S["params_done"], 1)
            with dve.Fori(0, LAYERS) as l:
                chain.rebase(DVE_LAYER * l + DVE_BEFORE)
                dve.wait_ge(S["x_ready"], 2 * l + 2)
                chain.step(nc.vector.tensor_copy(lp[:, :], params[:, bass.ds(l, 1), :].rearrange("p l k -> p (l k)")))
                dve.wait_ge(S["tr_wo"], l + 1)
                for s in range(2):
                    for j in range(2):
                        k = L_RMS + 2 * s + j
                        last = nc.vector.tensor_scalar(tWo[:, s, j, :], cols(5, 128, at=128 * s), lp[:, k:k + 1], None, ALU.mult)
                last.then_inc(S["w_o"], 1)

                def spread(t, queries, keys):
                    pr = slice(HPAIR * t, HPAIR * t + HPAIR)
                    for buf, src, done, end in ((qx, qS, queries, SPREAD_DVE[t]), (kxb, kSb, keys, HSUB)):
                        for a in done:
                            last = nc.vector.tensor_scalar(buf[:, pr, :, a, :].rearrange("p a u q -> p u a q"), src[:, t, :, :, :],
                                                           cst[:, C_SUB + a:C_SUB + a + 1], None, ALU.mult)
                            if a == end - 1:
                                last.then_inc(S["qx_done" if buf is qx else "kx_done"], 1)

                def keys_bf16(t):
                    dve.wait_ge(S["qk_proj"], 2 * l + t + 1)
                    nc.vector.tensor_copy(kSb[:, t, :, :, :], cols(BANK_QKV[t][1], HALF).rearrange("p (u a q) -> p u a q", u=2, q=SEQ)).then_inc(S["k_sb"], 1)
                    dve.wait_ge(S["k_sb"], 2 * l + t + 1)

                def maxima(p):
                    dve.wait_ge(S["sc_max"], PAIRS * l + p + 1)
                    if p >= 2:
                        dve.wait_ge(S["dmax_done"], PAIRS * l + p - 1)
                    nc.vector.tensor_reduce(nmax[:, p % 2, :], ps[:, 0:2, 0:HALF].rearrange("p u (a k) -> p u a k", k=SEQ),
                                            AX_X, ALU.max, negate=True).then_inc(S["nmax_done"], 1)

                def normalize(p, meanwhile=None):
                    b = BANK_VALUE[p]
                    dve.wait_ge(S["pv_done"], PAIRS * l + p + 1)
                    sums = cols(b, 144, at=144).rearrange("p (s i q) -> p s i q", s=2, i=2)
                    vals = cols(b, 144).rearrange("p (s i q) -> p s i q", s=2, i=2)
                    r, w = rden[:, p % 2], on[:, p % 2]
                    chain.step(nc.vector.reciprocal(r, sums), meanwhile)
                    chain.step(nc.vector.tensor_tensor(w, vals, r, ALU.mult))
                    nc.vector.scalar_tensor_tensor(o[:, :, p, :], w[:, :, 1, :], lp[:, L_NDW:L_NDW + 1], w[:, :, 0, :],
                                                   ALU.mult, ALU.add).then_inc(S["o_done"], 1)

                def mean_square(t):
                    dve.wait_ge(S["rms_ps"], 2 * l + t + 1)
                    nc.vector.tensor_scalar(ms[0:RCH, t, :], cols(BANK_POST[t], 4, slice(0, RCH), 300), EPS_RMS, None, ALU.add).then_inc(S["rms_ms"], 1)

                def add_attention(t):
                    dve.wait_ge(S["wo_sb"], 2 * l + t + 1)
                    dve.wait_ge(S["rms_rb"], 2 * l + t + 1)
                    chain.step(nc.vector.tensor_tensor(xa[:, t, :], ao[:, t, :], cols(BANK_POST[t], HALF), ALU.mult))
                    nc.vector.scalar_tensor_tensor(X1[:, half(t)], xa[:, t, :], lp[:, L_BO:L_BO + 1], X[:, half(t)],
                                                   ALU.add, ALU.add).then_inc(S["ln_src"], 1)

                def scale_norm(t):
                    dve.wait_ge(S["ln_rb"], 2 * l + 4 + t + 1)
                    nc.vector.scalar_tensor_tensor(hn[:, half(t)], xc[:, half(t)], lp[:, L_G:L_G + 1], cols(BANK_POST[t], HALF),
                                                   ALU.mult, ALU.mult).then_inc(S["h_done"], 1)

                every = range(HSUB)
                keys_bf16(0)
                spread(0, (), every)
                dve.wait_ge(S["q_sb"], 2 * l + 1)
                spread(0, range(0, 6), ())
                maxima(0)
                dve.wait_ge(S["qk_proj"], 2 * l + 2)
                nc.vector.tensor_tensor(b1e[:, :], lp[:, L_B1:L_B1 + MC], cols(BANK_QKV[1][1], MC, at=400), ALU.add).then_inc(S["b1_done"], 1)
                keys_bf16(1)
                dve.wait_ge(S["q_sb"], 2 * l + 2)
                maxima(1)
                spread(1, (), every)
                maxima(2)
                spread(1, range(0, 2), ())
                normalize(0)
                maxima(3)
                spread(1, range(2, 4), ())
                normalize(1)
                maxima(4)
                normalize(2)
                maxima(5)
                normalize(3)
                maxima(6)
                normalize(4, lambda: mean_square(0))
                maxima(7)

                normalize(5)
                add_attention(0)
                normalize(6, lambda: center(l + 2, 0, X1, BANK_POST))
                normalize(7, lambda: variance(l + 2, 0, EPS_LN, BANK_POST))
                mean_square(1)
                scale_norm(0)
                add_attention(1)
                center(l + 2, 1, X1, BANK_POST)
                variance(l + 2, 1, EPS_LN, BANK_POST)
                scale_norm(1)
                for t in range(2):
                    dve.wait_ge(S["ffn2"], 2 * l + t + 1)
                    nc.vector.scalar_tensor_tensor(X[:, half(t)], cols(6 + t, HALF), lp[:, L_B2:L_B2 + 1], X1[:, half(t)],
                                                   ALU.add, ALU.add).then_inc(S["x_ready"], 1)
                assert chain.n == DVE_LAYER, chain.n

            chain.rebase(DVE_LAYER * LAYERS + DVE_BEFORE)
            n = LAYERS + 2
            for t in range(2):
                center(n, t, X)
            for t in range(2):
                variance(n, t, EPS_LN)
            for t in range(2):
                dve.wait_ge(S["ln_rb"], 2 * n + t + 1)
                chain.step(nc.vector.scalar_tensor_tensor(hn[:, half(t)], xc[:, half(t)], vcol[:, V_GF:V_GF + 1], cols(6 + t, HALF),
                                                          ALU.mult, ALU.mult))
                nc.vector.scalar_tensor_tensor(X1[:, half(t)], hn[:, half(t)], vcol[:, V_BF:V_BF + 1], H0[:, half(t)],
                                               ALU.add, ALU.add).then_inc(S["ln_src"], 1)
            for g in range(1, 4, 2):
                dve.wait_ge(S["exp_tr"], g + 1)
                nc.vector.tensor_copy(texp[:, 4 * g:4 * g + 4, :], cols(2 + g, 512)).then_inc(S["exp_cp_v"], 1)
            n = LAYERS + 3
            for t in range(2):
                center(n, t, X1)
            for t in range(2):
                variance(n, t, EPS_LN)
            for t in range(2):
                dve.wait_ge(S["ln_rb"], 2 * n + t + 1)
                nc.vector.tensor_tensor(X[:, half(t)], xc[:, half(t)], cols(6 + t, HALF), ALU.mult).then_inc(S["x_ready"], 1)
            dve.wait_ge(S["lg_ps"], 1)
            dve.wait_ge(S["in_sw"], 48)

            def over(v):
                return v.rearrange("p (c e) -> p c e", e=1).broadcast_to([CHUNK, NCH, EXPERTS])

            chain.step(nc.vector.tensor_tensor(lg[:, :, :], cols(0, NCH * EXPERTS, slice(0, CHUNK)).rearrange("p (c e) -> p c e", e=EXPERTS),
                                               swb[:, :].rearrange("p (c e) -> p c e", c=1).broadcast_to([CHUNK, NCH, EXPERTS]), ALU.add))
            chain.step(nc.vector.tensor_reduce(r1[:, 0, :], lg[:, :, :], AX_X, ALU.max))
            nc.vector.tensor_tensor(lg[:, :, :], lg[:, :, :], over(r1[:, 0, :]), ALU.subtract).then_inc(S["lg_done"], 1)
            dve.wait_ge(S["eg_done"], 1)
            chain.step(nc.vector.tensor_reduce(r1[:, 1, :], eg[:, :, :], AX_X, ALU.max))
            chain.step(nc.vector.tensor_tensor(lg[:, :, :], eg[:, :, :], over(r1[:, 1, :]), ALU.is_equal))
            chain.step(nc.vector.tensor_tensor(lg[:, :, :], lg[:, :, :],
                                               cst[0:CHUNK, C_RANK:C_RANK + EXPERTS].rearrange("p (c e) -> p c e", c=1).broadcast_to([CHUNK, NCH, EXPERTS]),
                                               ALU.mult))
            chain.step(nc.vector.tensor_reduce(r1[:, 2, :], lg[:, :, :], AX_X, ALU.max))
            nc.vector.tensor_tensor(ohb[:, :, :], lg[:, :, :], over(r1[:, 2, :]), ALU.is_equal).then_inc(S["oh_done"], 1)
            chain.step(nc.vector.tensor_tensor(ohf[:, :, :], lg[:, :, :], over(r1[:, 2, :]), ALU.is_equal))
            chain.step(nc.vector.tensor_reduce(r1[:, 3, :], eg[:, :, :], AX_X, ALU.add))
            chain.step(nc.vector.reciprocal(r1[:, 4, :], r1[:, 3, :]))
            nc.vector.tensor_tensor(route[:, :, EXPERTS + 1], r1[:, 1, :], r1[:, 4, :], ALU.mult)
            dve.wait_ge(S["cum_ps"], 1)
            chain.step(nc.vector.tensor_tensor(lg[:, :, :], ohf[:, :, :], cols(1, NCH * EXPERTS, slice(0, CHUNK)).rearrange("p (c e) -> p c e", e=EXPERTS), ALU.mult))
            chain.step(nc.vector.tensor_reduce(r1[:, 5, :], lg[:, :, :], AX_X, ALU.add))
            nc.vector.tensor_scalar(route[:, :, EXPERTS], r1[:, 5, :], float(CAPACITY), None, ALU.is_gt)
            chain.step(nc.vector.tensor_scalar(r1[:, 6, :], r1[:, 5, :], float(CAPACITY), None, ALU.is_le))
            nc.vector.tensor_tensor(route[:, :, 0:EXPERTS], ohf[:, :, :], over(r1[:, 6, :]), ALU.mult).then_inc(S["route_done"], 1)
            dve.wait_ge(S["route_tr"], 1)
            rT = ps[0:EXPERTS + 2, 2:4, 0:HALF]
            nc.vector.tensor_copy(routeTb[:, :].rearrange("p (t n) -> p t n", t=2), rT)
            nc.vector.tensor_copy(routeT[:, :].rearrange("p (t n) -> p t n", t=2), rT).then_inc(S["routeT_done"], 1)
            for e in range(EXPERTS + 1):
                dve.wait_ge(S["mask_ps"], e + 1)
                if e >= 3:
                    dve.wait_ge(S["exp_ps"], e - 2)
                b = 2 + 2 * (e % 2)
                nc.vector.tensor_tensor(xm[:, e % 3, :].rearrange("p (t n) -> p t n", t=2), X[:, :].rearrange("p (t n) -> p t n", t=2),
                                        ps[:, b:b + 2, 0:HALF], ALU.mult).then_inc(S["xm_done"], 1)
            dve.wait_ge(S["rp_sb"], 1)
            dve.wait_ge(S["exp_ps"], EXPERTS + 1)
            for t in range(2):
                chain.step(nc.vector.tensor_tensor(hn[:, half(t)], rpb[:, half(t)], cols(6 + t, HALF), ALU.mult))
                nc.vector.tensor_tensor(hn[:, half(t)], hn[:, half(t)], X1[:, half(t)], ALU.add).then_inc(S["y_done"], 1)
            dve.wait_ge(S["y_tr"], 2)
            nc.vector.tensor_copy(fin[:, HCH:NCH, :], cols(3, HCH * 128, slice(0, CHUNK))).then_inc(S["fin_v"], 1)

        @block.tensor
        def _(pe):
            mm = nc.tensor.matmul

            def turn(dst, src, k):
                return nc.tensor.transpose(dst, src, ident[0:k, 0:k])

            pe.wait_ge(S["in_c"], 16)
            for g in range(NTR):
                pe.wait_ge(S["win_done"], g // 2 + 1)
                if g >= 6:
                    pe.wait_ge(S["xT_cp"], g - 5)
                for w in range(3):
                    ins = turn(cols(g % 6, TOKROWS, slice(0, KWIN), TOKROWS * w), xwin[:, 3 * g + w, :], TOKROWS)
                ins.then_inc(S["xT_tr"], 1)
            pe.wait_ge(S["xT_cp"], NTR)

            def conv(t, chunks):
                for k in chunks:
                    pe.wait_ge(S["weff_done"], k // CH + 1)
                    ins = mm(cols(6 + t, HALF), wshift[:, 0, k // CH, D * (k % CH):D * (k % CH) + D],
                             xT[:, k, :, 48 * t:48 * t + 48].rearrange("p w n -> p n w"), start=(k == 0), stop=(k == ROWG * CH - 1))
                if k == ROWG * CH - 1:
                    ins.then_inc(S["conv_done"], 1)

            def mean(n, t, src, ready, value, bank=BANK_NORM):
                pe.wait_ge(ready, value)
                mm(cols(bank[t], HALF), meanw, src[:, half(t)], start=True, stop=True).then_inc(S["ln_mean"], 1)

            def stat(n, t, bank=BANK_NORM):
                pe.wait_ge(S["ln_sq"], 2 * n + t + 1)
                for c in range(HCH):
                    ins = mm(cols(bank[t], 1, slice(0, CHUNK), 300 + c), sq[:, HALF * t + CHUNK * c:HALF * t + CHUNK * c + CHUNK],
                             meanw[:, 0:1], start=True, stop=True)
                ins.then_inc(S["ln_stat"], 1)

            def bcast(n, t, bank=BANK_NORM):
                pe.wait_ge(S["ln_rs"], 2 * n + t + 1)
                for c in range(HCH):
                    ins = mm(cols(bank[t], CHUNK, at=CHUNK * c), rs[:, t, c:c + 1].broadcast_to([CHUNK, 128]), ident[0:CHUNK, 0:CHUNK],
                             start=True, stop=True)
                ins.then_inc(S["ln_rb"], 1)

            def norm(n, src, ready, value):
                for t in range(2):
                    mean(n, t, src, ready, value + t)
                for t in range(2):
                    stat(n, t)
                for t in range(2):
                    bcast(n, t)

            def dense(t):
                pe.wait_ge(S["h_done"], t + 1)
                mm(cols(t, HALF), densew[:, :], hn[:, half(t)], start=True, stop=True).then_inc(S["dense_done"], 1)

            conv(0, range(0, 6))
            pe.wait_ge(S["in_vec"], 16 * 11)
            pe.wait_ge(S["in_rms"], 48)
            turn(cols(5, V_END), vrow[:, :], V_END).then_inc(S["vec_tr"], 1)
            conv(0, range(6, 9))
            conv(1, range(0, 3))
            mean(0, 0, X1, S["ln_src"], 1)
            conv(1, range(3, 6))
            stat(0, 0)
            conv(1, range(6, 9))
            bcast(0, 0)
            mean(0, 1, X1, S["ln_src"], 2)
            pe.wait_ge(S["in_dense"], 16)
            dense(0)
            stat(0, 1)
            mean(1, 0, H0, S["ln_src"], 3)
            bcast(0, 1)
            stat(1, 0)
            dense(1)
            bcast(1, 0)
            mean(1, 1, H0, S["ln_src"], 4)
            stat(1, 1)
            bcast(1, 1)
            pe.wait_ge(S["att_zero"], 3)
            pe.wait_ge(S["cstb_done"], 1)

            with pe.Fori(0, LAYERS) as l:
                pe.wait_ge(S["in_layer"], 96 * l + 96)
                for n in range(3):
                    ins = turn(cols(4, 128, at=128 * n), nqkvo[:, n, :], 128)
                ins.then_inc(S["tr_qkv"], 1)
                pe.wait_ge(S["wo_dup"], 2 * l + 2)
                for s in range(2):
                    ins = turn(cols(5, 128, at=128 * s), nWo2[:, s, :, :, :].rearrange("p c j e -> p (c j e)"), 128)
                ins.then_inc(S["tr_wo"], 1)
                for m in range(MC):
                    ins = turn(cols(2, 128, at=128 * m), nW1[:, m, :], 128)
                ins.then_inc(S["tr_w1"], 1)
                for m in range(MC):
                    ins = turn(cols(3, 128, at=128 * m), nW2[:, m, :], 128)
                ins.then_inc(S["tr_w2"], 1)
                pe.wait_ge(S["w_qkv"], l + 1)
                for t in range(2):
                    bq, bk, bv = BANK_QKV[t]
                    pe.wait_ge(S["x_ready"], 2 * l + t + 1)
                    if t == 1:
                        pe.wait_ge(S["w_o"], l + 1)
                        pe.wait_ge(S["w_1"], l + 1)
                        for m in range(MC):
                            mm(cols(bk, 1, at=400 + m), tW1[:, m, :], lp[:, L_B:L_B + 1], start=True, stop=True)
                    for b, n in ((bq, 0), (bk, 1)):
                        for u in range(2):
                            for j in range(2):
                                ins = mm(cols(b, HALF // 2, slice(64 * j, 64 * j + 64), HALF // 2 * u), tqkv[:, n, 64 * u:64 * u + 64],
                                         of_image(X[:, half(t)], j), start=True, stop=True)
                    ins.then_inc(S["qk_proj"], 1)
                    for a in range(HPAIR):
                        for j in range(2):
                            at = HALF * t + 2 * SEQ * a + SEQ * j
                            ins = mm(cols(bv, 128, slice(64 * j, 64 * j + SEQ), 128 * a), X[:, at:at + SEQ], tqkv[:, 2, :], start=True, stop=True)
                    ins.then_inc(S["v_proj"], 1)

                def approx(p):
                    t = p // HPAIR
                    pe.wait_ge(S["qk_ev"], 2 * l + t + 1)
                    pe.wait_ge(S["kx_done"], 2 * l + t + 1)
                    if p >= 1:
                        pe.wait_ge(S["nmax_done"], PAIRS * l + p)
                    for u in range(2):
                        ins = mm(cols(u, HALF), qdb[:, p, u, :, :].rearrange("p j q -> p (j q)"), kxb[:, p, u, :, :], start=True, stop=True)
                    ins.then_inc(S["sc_max"], 1)

                def scores(p):
                    b = 2 + 2 * (p % 2)
                    pe.wait_ge(S["qx_done"], 2 * l + p // HPAIR + 1)
                    pe.wait_ge(S["qx_act"], 2 * l + p // HPAIR + 1)
                    if p == 0:
                        pe.wait_ge(S["w_1"], l + 1)
                        pe.wait_ge(S["w_2"], l + 1)
                    if p == 1:
                        pe.wait_ge(S["qk_ev"], 2 * l + 2)
                    if p >= 2:
                        pe.wait_ge(S["exp_done"], PAIRS * l + p - 1)
                    for u in range(2):
                        mm(cols(b + u, HALF), kd[:, p, u, :, :].rearrange("p j q -> p (j q)"), qx[:, p, u, :, :], start=True, stop=False)

                def less_max(p):
                    b = 2 + 2 * (p % 2)
                    pe.wait_ge(S["dmax_done"], PAIRS * l + p + 1)
                    for u in range(2):
                        ins = mm(cols(b + u, HALF), sameimg_b, dmax[:, p % 2, HSUB * u:HSUB * u + HSUB, :], start=False, stop=True)
                    ins.then_inc(S["scores_done"], 1)

                def values(p):
                    b = BANK_VALUE[p]
                    pe.wait_ge(S["exp_done"], PAIRS * l + p + 1)
                    if p < 2:
                        pe.wait_ge(S["v_ev"], 2 * l + 2)
                    same_bank = [q for q in range(p) if BANK_VALUE[q] == b]
                    if same_bank:
                        pe.wait_ge(S["o_done"], PAIRS * l + same_bank[-1] + 1)
                    for h in range(HEADS):
                        u, c = h // 4, h % 4
                        w = pT[:, p % 2, u, 2 * SEQ * c:2 * SEQ * c + 2 * SEQ]
                        r = slice(32 * c, 32 * c + 32)
                        mm(cols(b, 2 * SEQ, r, 2 * SEQ * u), vd[:, p, h, :, :].rearrange("p j e -> p (j e)"), w, start=True, stop=True)
                        ins = mm(cols(b, 2 * SEQ, r, 144 + 2 * SEQ * u), cst[:, C_SUMIMG:C_SUMIMG + 32], w, start=True, stop=True)
                    ins.then_inc(S["pv_done"], 1)

                def mean_squares(t):
                    pe.wait_ge(S["osq_done"], PAIRS * l + HPAIR * t + HPAIR)
                    for c in range(2):
                        for s in range(2):
                            a = HPAIR * t + 2 * c
                            ins = mm(cols(BANK_POST[t], 2, slice(0, RCH), 300 + 2 * c), osq[:, s, a:a + 2, :].rearrange("p a q -> p (a q)"),
                                     cst[:, C_RMS:C_RMS + 2], start=(s == 0), stop=(s == 1))
                    ins.then_inc(S["rms_ps"], 1)

                def rms_bcast(t):
                    pe.wait_ge(S["rms_r"], 2 * l + t + 1)
                    if t == 0:
                        pe.wait_ge(S["wo_sb"], 2 * l + 1)
                    for j in range(2):
                        for c in range(2):
                            ins = mm(of_image(cols(BANK_POST[t], HALF), j)[:, 2 * c:2 * c + 2, :], rs[0:RCH, t, 2 * c + j:2 * c + j + 1].broadcast_to([RCH, 128]),
                                     ident[0:RCH, 0:RCH], start=True, stop=True)
                    ins.then_inc(S["rms_rb"], 1)

                def project_out(t):
                    pe.wait_ge(S["o_done"], PAIRS * l + HPAIR * t + HPAIR)
                    if t == 0:
                        pe.wait_ge(S["rms_ms"], 2 * l + 1)
                    for j in range(2):
                        for s in range(2):
                            ins = mm(of_image(cols(BANK_WO[t], HALF), j), tWo[:, s, j, :],
                                     o[:, s, HPAIR * t:HPAIR * t + HPAIR, :].rearrange("p a q -> p (a q)"), start=(s == 0), stop=(s == 1))
                    ins.then_inc(S["wo_ps"], 1)

                def up(t, m):
                    pe.wait_ge(S["h_done"], 2 * l + 2 + t + 1)
                    if t == 1 and m >= 1:
                        pe.wait_ge(S["gelu_done"], 2 * MC * l + m)
                    mm(cols(BANK_UP[MC * t + m], HALF), tW1[:, m, :], hn[:, half(t)], start=True, stop=True).then_inc(S["ffn1"], 1)

                def down(t, m):
                    if m == 0:
                        pe.wait_ge(S["o_done"], PAIRS * l + PAIRS)
                    pe.wait_ge(S["gelu_done"], 2 * MC * l + MC * t + m + 1)
                    ins = mm(cols(6 + t, HALF), tW2[:, m, :], gact[:, t, m, :], start=(m == 0), stop=(m == MC - 1))
                    if m == MC - 1:
                        ins.then_inc(S["ffn2"], 1)

                approx(0)
                for p in range(5):
                    scores(p)
                    approx(p + 1)
                    if p >= 1:
                        values(p - 1)
                    less_max(p)
                scores(5)
                approx(6)
                values(4)
                less_max(5)
                scores(6)
                mean_squares(0)
                approx(7)
                project_out(0)
                values(5)
                less_max(6)
                rms_bcast(0)
                scores(7)
                values(6)
                less_max(7)
                mean(l + 2, 0, X1, S["ln_src"], 2 * l + 5, BANK_POST)
                values(7)
                stat(l + 2, 0, BANK_POST)
                bcast(l + 2, 0, BANK_POST)
                mean_squares(1)
                project_out(1)
                up(0, 0)
                up(0, 1)
                rms_bcast(1)
                up(0, 2)
                up(0, 3)
                mean(l + 2, 1, X1, S["ln_src"], 2 * l + 6, BANK_POST)
                down(0, 0)
                stat(l + 2, 1, BANK_POST)
                down(0, 1)
                down(0, 2)
                bcast(l + 2, 1, BANK_POST)
                down(0, 3)
                for m in range(MC):
                    up(1, m)
                for m in range(MC):
                    down(1, m)

            pe.wait_ge(S["in_exp"], 16)
            pe.wait_ge(S["in_sw"], 48)
            n = LAYERS + 2
            for t in range(2):
                mean(n, t, X, S["x_ready"], 2 * LAYERS + t + 1)
            turn(cols(0, EXPERTS), swn[:, :], EXPERTS).then_inc(S["sw_tr"], 1)
            for t in range(2):
                stat(n, t)
            for g in range(2):
                for k in range(4):
                    ins = turn(cols(2 + g, 128, at=128 * k), nexp[:, 4 * g + k, :], 128)
                ins.then_inc(S["exp_tr"], 1)
            for t in range(2):
                bcast(n, t)
            for g in range(2, 4):
                for k in range(4):
                    ins = turn(cols(2 + g, 128, at=128 * k), nexp[:, 4 * g + k, :], 128)
                ins.then_inc(S["exp_tr"], 1)
            norm(LAYERS + 3, X1, S["ln_src"], 2 * LAYERS + 5)
            pe.wait_ge(S["swT_done"], 1)
            for c in range(NCH):
                if c % HCH == 0:
                    pe.wait_ge(S["x_ready"], 2 * LAYERS + 2 + c // HCH + 1)
                ins = mm(cols(0, EXPERTS, slice(0, CHUNK), EXPERTS * c), X[:, CHUNK * c:CHUNK * c + CHUNK], swT[:, :], start=True, stop=True)
            ins.then_inc(S["lg_ps"], 1)
            pe.wait_ge(S["oh_done"], 1)
            for c in range(NCH):
                dst = cols(1, EXPERTS, slice(0, CHUNK), EXPERTS * c)
                for k in range(c):
                    mm(dst, cstb[0:CHUNK, C_ONE:C_ONE + CHUNK], ohb[:, k, :], start=(k == 0), stop=False)
                ins = mm(dst, cstb[0:CHUNK, C_CUM:C_CUM + CHUNK], ohb[:, c, :], start=(c == 0), stop=True)
            ins.then_inc(S["cum_ps"], 1)
            pe.wait_ge(S["route_done"], 1)
            pe.wait_ge(S["exp_cp_a"], 2)
            pe.wait_ge(S["exp_cp_v"], 2)
            for c in range(NCH):
                ins = turn(cols(2 + c // HCH, CHUNK, slice(0, EXPERTS + 2), CHUNK * (c % HCH)), route[:, c, :], CHUNK)
            ins.then_inc(S["route_tr"], 1)
            pe.wait_ge(S["routeT_done"], 1)

            def mask(e):
                b = 2 + 2 * (e % 2)
                if e >= 2:
                    pe.wait_ge(S["xm_done"], e - 1)
                for t in range(2):
                    ins = mm(cols(b + t, HALF), identb[0:EXPERTS + 2, e:e + 1].broadcast_to([EXPERTS + 2, 128]), routeTb[:, half(t)],
                             start=True, stop=True)
                ins.then_inc(S["mask_ps"], 1)

            mask(0)
            mask(1)
            for t in range(2):
                mm(cols(t, HALF), ident[0:EXPERTS + 2, EXPERTS + 1:EXPERTS + 2].broadcast_to([EXPERTS + 2, 128]), routeT[:, half(t)],
                   start=True, stop=True).then_inc(S["rp_ps"], 1) if t == 1 else mm(
                       cols(t, HALF), ident[0:EXPERTS + 2, EXPERTS + 1:EXPERTS + 2].broadcast_to([EXPERTS + 2, 128]), routeT[:, half(t)],
                       start=True, stop=True)
            for t in range(2):
                mm(cols(6 + t, HALF), ebn[:, :], routeT[0:EXPERTS, half(t)], start=True, stop=False)
            for e in range(EXPERTS + 1):
                pe.wait_ge(S["xm_done"], e + 1)
                for t in range(2):
                    ins = mm(cols(6 + t, HALF), texp[:, e, :] if e < EXPERTS else ident, xm[:, e % 3, half(t)],
                             start=False, stop=(e == EXPERTS))
                ins.then_inc(S["exp_ps"], 1)
                if e + 2 <= EXPERTS:
                    mask(e + 2)
            for t in range(2):
                pe.wait_ge(S["y_done"], t + 1)
                for c in range(HCH):
                    ins = turn(cols(2 + t, 128, slice(0, CHUNK), 128 * c), hn[:, HALF * t + CHUNK * c:HALF * t + CHUNK * c + CHUNK], 128)
                ins.then_inc(S["y_tr"], 1)


_ORDER = ['x', 'L0_tok_conv_w', 'L0_tok_conv_b', 'L0_tok_gamma', 'L0_tok_beta', 'L0_tok_dense_w', 'L0_tok_dense_b',
          'L0_attn_Wq', 'L0_attn_Wk', 'L0_attn_Wv', 'L0_attn_rms_w', 'L0_attn_Wo', 'L0_attn_bo', 'L0_attn_diffw',
          'L0_attn_g_ffn', 'L0_attn_b_ffn', 'L0_attn_W1', 'L0_attn_b1', 'L0_attn_W2', 'L0_attn_b2', 'L0_attn_g_f',
          'L0_attn_b_f', 'L0_ffn_switch_w', 'L0_ffn_switch_b', 'L0_ffn_expert_w', 'L0_ffn_expert_b']


def kernel(**inputs):
    import concourse.bacc as bacc
    from concourse.bass_utils import run_bass_kernel_spmd

    nc = bacc.Bacc("TRN2", target_bir_lowering=False, num_devices=1)
    arrays, args = {}, []
    for name in _ORDER + ['consts']:
        a = constants() if name == 'consts' else np.ascontiguousarray(inputs[name])
        arrays[f"in_{name}_dram"] = a
        args.append(nc.dram_tensor(f"in_{name}_dram", a.shape, mybir.dt.from_np(a.dtype), kind="ExternalInput").ap())
    args.append(nc.dram_tensor("out_0_dram", (IMGS, SEQ, D), F32, kind="ExternalOutput").ap())
    vit_tower(nc, *args)
    r = run_bass_kernel_spmd(nc, [arrays], core_ids=[0])
    return r.results[0]["out_0_dram"]
```

```python
from contextlib import ExitStack

import numpy as np

import concourse.bass as bass
from concourse import mybir

F32 = mybir.dt.float32
BF16 = mybir.dt.bfloat16
ALU = mybir.AluOpType
ACT = mybir.ActivationFunctionType
AX_X = mybir.AxisListType.X

IMGS, SIDE, CH, PATCH = 16, 96, 3, 16
GRID = SIDE // PATCH
SEQ = GRID * GRID
TOK = IMGS * SEQ
D = 128
LAYERS, HEADS, MLP, EXPERTS = 4, 8, 512, 16
EDIM = D // HEADS
FDIM = EDIM // 2
CAPACITY = int(1.2 * TOK / EXPERTS)
EPS_TOK, EPS_LN, EPS_RMS = 1e-3, 1e-5, 1.1920929e-07

PAIRS = IMGS // 2
HALF = TOK // 2
HPAIR = PAIRS // 2
CHUNK = 96
HCH = HALF // CHUNK
RCH = 2 * SEQ
HSUB = HEADS * 2 // 2
MC = MLP // D
WIN = PATCH + 2
RHO = 6
ROWG = WIN // RHO
KWIN = RHO * WIN
ROWPITCH = SIDE * CH + 48
TOKROWS = IMGS * GRID

C_IDENT, C_MEAN, C_SAMEIMG, C_SUMIMG = 0, 128, 256, 384
C_RMS, C_SUB, C_SELQ, C_CUM, C_ONE = 416, 418, 426, 462, 558
C_INDEX, C_RANK, C_TOP, C_BOT, C_POW, C_END = 654, 655, 671, 672, 673, 677

V_BO, V_G, V_B, V_B2, V_B1, V_RMS = 0, 4, 8, 12, 16, 32
V_CONVB, V_GAMMA, V_BETA, V_DENSEB, V_GF, V_BF, V_END = 40, 41, 42, 43, 44, 45, 46
L_BO, L_G, L_B, L_B2, L_B1, L_RMS, L_NDW, L_OMD, L_END = 0, 1, 2, 3, 4, 8, 12, 13, 14


def constants():
    c = np.zeros((128, C_END), np.float32)
    p = np.arange(128)
    c[:, C_IDENT:C_IDENT + 128] = np.eye(128)
    c[:, C_MEAN:C_MEAN + 128] = 1.0 / D
    f = np.arange(128)
    c[:, C_SAMEIMG:C_SAMEIMG + 128] = (p[:, None] // 64 == f[None] // 64) & (f[None] % 64 < SEQ)
    f = np.arange(32)
    c[:, C_SUMIMG:C_SUMIMG + 32] = (p[:, None] // 64 == f[None] // 16) & (p[:, None] % 64 < SEQ)
    c[:, C_RMS:C_RMS + 2] = (p[:, None] // 16 % 2 == np.arange(2)[None]) / D
    c[:, C_SUB:C_SUB + HSUB] = p[:, None] // FDIM % HSUB == np.arange(HSUB)[None]
    c[:, C_SELQ:C_SELQ + SEQ] = p[:, None] % 64 == np.arange(SEQ)[None]
    c[:, C_CUM:C_CUM + CHUNK] = p[:, None] <= np.arange(CHUNK)[None]
    c[:, C_ONE:C_ONE + CHUNK] = 1.0
    c[:, C_INDEX] = p * (p <= EXPERTS)
    c[:, C_RANK:C_RANK + EXPERTS] = EXPERTS - np.arange(EXPERTS)[None]
    c[:, C_TOP] = p % GRID != 0
    c[:, C_BOT] = p % GRID != GRID - 1
    c[:, C_POW:C_POW + 4] = -0.5
    return c


class Chain:

    def __init__(self, eng, sem):
        self.eng, self.sem, self.base, self.n = eng, sem, 0, 0

    def step(self, ins, meanwhile=None):
        self.n += 1
        ins.then_inc(self.sem, 1)
        if meanwhile:
            meanwhile()
        self.eng.wait_ge(self.sem, self.base + self.n)

    def rebase(self, base):
        self.base, self.n = base, 0


DVE_BEFORE, DVE_LAYER = 6, 18


def vit_tower(nc, x, conv_w, conv_b, gamma, beta, dense_w, dense_b, Wq, Wk, Wv, rms_w, Wo, bo, diffw,
              g_ffn, b_ffn, W1, b1, W2, b2, g_f, b_f, switch_w, switch_b, expert_w, expert_b, consts, out):
    ctx = ExitStack()
    with ctx:
        def sb(name, shape, dt=F32):
            return ctx.enter_context(nc.sbuf_tensor(name, shape, dt))

        def sem(name):
            return ctx.enter_context(nc.semaphore(name))

        ps = ctx.enter_context(nc.psum_tensor("ps", [128, 8, 512], F32))

        cst = sb("cst", [128, C_END])
        ident = cst[:, C_IDENT:C_IDENT + 128]
        meanw = cst[:, C_MEAN:C_MEAN + 128]
        cstb = sb("cstb", [128, C_RANK], BF16)
        identb = cstb[:, C_IDENT:C_IDENT + 128]
        sameimg_b = cstb[:, C_SAMEIMG:C_SAMEIMG + 128]
        selq_b = cstb[:, C_SELQ:C_SELQ + SEQ]
        vrow = sb("vrow", [V_END, 128])
        vcol = sb("vcol", [128, V_END])
        dwb = sb("dwb", [128, LAYERS])
        params = sb("params", [128, LAYERS, L_END])
        lp = sb("lp", [128, L_END])
        lrms = sb("lrms", [128, 4])
        imgbuf = sb("imgbuf", [128, WIN * ROWPITCH])
        winbuf = sb("winbuf", [128, ROWG * CH * GRID * KWIN])
        ximg = imgbuf[0:TOKROWS, :].rearrange("p (u f) -> p u f", u=WIN)
        xwin = winbuf[0:TOKROWS, :].rearrange("p (g k) -> p g k", k=KWIN)
        xT = sb("xT", [KWIN, ROWG * CH, GRID, TOKROWS])
        wbuf = sb("wbuf", [128, 5 * ROWG * CH * D])
        wshift = wbuf[0:KWIN, :].rearrange("p (g a f) -> p g a f", g=5, a=ROWG)
        densew = sb("densew", [128, 128])
        X = sb("X", [128, TOK])
        X1 = sb("X1", [128, TOK])
        H0 = sb("H0", [128, TOK])
        xc = sb("xc", [128, TOK])
        sq = sb("sq", [128, TOK])
        hn = sb("hn", [128, TOK])
        ms = sb("ms", [CHUNK, 2, 4])
        rs = sb("rs", [CHUNK, 2, 4])
        ao = sb("ao", [128, 2, HALF])
        nqkvo = sb("nqkvo", [128, 4, 128])
        nW1 = sb("nW1", [128, MC, 128])
        nW2 = sb("nW2", [128, MC, 128])
        nWo2 = sb("nWo2", [128, 2, 4, 2, EDIM])
        tqkv = sb("tqkv", [128, 3, 128])
        tWo = sb("tWo", [128, 2, 2, 128])
        tW1 = sb("tW1", [128, MC, 128])
        tW2 = sb("tW2", [128, MC, 128])
        b1e = sb("b1e", [128, MC])
        qS = sb("qS", [128, 2, 2, HPAIR, SEQ])
        kSb = sb("kSb", [128, 2, 2, HPAIR, SEQ], BF16)
        qx = sb("qx", [128, PAIRS, 2, HSUB, SEQ])
        kxb = sb("kxb", [128, PAIRS, 2, HSUB, SEQ], BF16)
        kd = sb("kd", [128, PAIRS, 2, 2, 64])
        qdb = sb("qdb", [128, PAIRS, 2, 2, 64], BF16)
        vd = sb("vd", [128, PAIRS, HEADS, 2, EDIM])
        nmax = sb("nmax", [128, 2, 2 * HSUB], BF16)
        dmax = sb("dmax", [128, 2, 2 * HSUB, SEQ], BF16)
        pT = sb("pT", [128, 2, 2, HSUB * SEQ])
        rden = sb("rden", [128, 2, 2, 2, SEQ])
        on = sb("on", [128, 2, 2, 2, SEQ])
        o = sb("o", [128, 2, PAIRS, SEQ])
        osq = sb("osq", [128, 2, PAIRS, SEQ])
        xa = hn[:, :].rearrange("p (t n) -> p t n", t=2)
        table = sb("table", [1, 1])
        gact = sb("gact", [128, 2, MC, HALF])
        swn = sb("swn", [EXPERTS, 128])
        swT = sb("swT", [128, EXPERTS])
        swb = sb("swb", [CHUNK, EXPERTS])
        ebn = sb("ebn", [EXPERTS, 128])
        nexp = imgbuf[:, 0:EXPERTS * 128].rearrange("p (e d) -> p e d", e=EXPERTS)
        texp = winbuf[:, 0:EXPERTS * 128].rearrange("p (e d) -> p e d", e=EXPERTS)
        NCH = TOK // CHUNK
        lg = sb("lg", [CHUNK, NCH, EXPERTS])
        eg = sb("eg", [CHUNK, NCH, EXPERTS])
        ohf = sb("ohf", [CHUNK, NCH, EXPERTS])
        ohb = sb("ohb", [CHUNK, NCH, EXPERTS], BF16)
        r1 = sb("r1", [CHUNK, 8, NCH])
        route = sb("route", [CHUNK, NCH, EXPERTS + 2])
        routeT = sb("routeT", [EXPERTS + 2, TOK])
        routeTb = sb("routeTb", [EXPERTS + 2, TOK], BF16)
        XM = 8
        xm = wbuf[:, 0:XM * HALF].rearrange("p (b n) -> p b n", b=XM)
        rpb = wbuf[:, 4 * TOK:5 * TOK]
        idxb = wbuf[:, 5 * TOK:6 * TOK]
        kept = wbuf[:, 6 * TOK:7 * TOK]
        fin = wbuf[0:CHUNK, 7 * TOK:7 * TOK + NCH * 128].rearrange("p (c d) -> p c d", c=NCH)

        names = """in_x0 in_x1 in_x2 in_top in_bot in_w0 in_w1 in_w2 in_w3 in_w3_pool in_w4 in_c in_vec in_diffw in_dense in_sw in_layer in_exp out_done
            halo_zero w_zero w_zero_p att_zero ximg_ok win_done xT_tr xT_cp weff_done conv_done dense_done
            cstb_done vec_tr vcol_done params_done lp_ready lrms_ready dvc
            ln_src ln_mean ln_cent ln_sq ln_stat ln_var ln_rs ln_rb h_done x_ready
            tr_qkv tr_wo tr_w1 tr_w2 wo_dup w_qkv w_o w_1 w_2 b1_ps b1_done
            qk_proj v_proj qk_ev v_ev q_sb k_sb qx_done qx_act qx_pool kx_done sc_max nmax_done dmax_done scores_done exp_done pv_done
            o_done osq_done wo_ps rms_ps rms_ms rms_r rms_rb wo_sb ffn1 gelu_done ffn2
            sw_tr swT_done exp_tr exp_cp lg_ps lg_done eg_done oh_done cum_ps route_done route_tr routeTb_done routeT_done
            idx_ps idx_sb xm_done exp_ps rp_ps rp_sb y_done y_tr fin_done""".split()
        S = {n: sem(n) for n in names}

        def half(t):
            return slice(HALF * t, HALF * t + HALF)

        def of_image(tokens, j):
            return tokens.rearrange("p (a j q) -> p a j q", j=2, q=SEQ)[:, :, j, :]

        LAST = LAYERS + 2

        def nth(n, t):
            if isinstance(n, int) and n < 2:
                return 2 * t + n
            if isinstance(n, int) and n >= LAST:
                return 2 * LAST + 2 * t + n - LAST
            return 2 * n + t

        def cols(bank, n, rows=slice(0, 128), at=0):
            return ps[rows, bank, at:at + n]

        SHIFTS = [(1, 1), (1, 0), (1, 2), (0, 1), (2, 1)]
        BANK_QKV = [(0, 1, 6), (4, 5, 7)]
        BANK_VALUE = [6, 7, 6, 7, 6, 6, 6, 0]
        BANK_NORM = [6, 7]
        BANK_POST = [7, 0]
        BANK_WO = [7, 1]
        BANK_EXPERTS = [2, 3, 2, 3]
        BANK_UP = [2, 3, 4, 5, 1, 2, 3, 4]
        COPIES_DVE = [range(0, 4), range(0, 2)]
        COPIES_POOL = [range(4, 6), range(2, 4)]
        COPIES_ACT = [range(6, 8), range(4, 8)]
        ROWG_ORDER = [1, 0, 2]
        NTR = ROWG * CH * 2

        def load_shifted(eng, g, landed, rows):
            du, dv = SHIFTS[g]
            for r in rows:
                a0 = 1 if r < du else 0
                i0 = RHO * a0 + r - du
                n = (PATCH - 1 - i0) // RHO + 1
                dst = wshift[WIN * r + dv:WIN * r + dv + PATCH, g, a0:a0 + n, :]
                src = conv_w[i0::RHO, :, CH * g:CH * g + CH, :].rearrange("i j c d -> j i (c d)")
                eng.dma_start(dst, src).then_inc(landed, 16)

        block = ctx.enter_context(nc.Block())

        @block.sync
        def _(sp):
            rows = x.rearrange("b h w c -> (b h) (w c)")
            main = rows.rearrange("(n u) f -> n u f", u=PATCH)
            row = slice(CH, CH + SIDE * CH)
            sp.dma_start(ximg[:, 6:12, row], main[:, 5:11, :]).then_inc(S["in_x1"], 16)
            sp.dma_start(cst[:, :], consts).then_inc(S["in_c"], 16)
            sp.wait_ge(S["halo_zero"], 1)
            sp.dma_start(ximg[1:TOKROWS, 0, row], rows[PATCH - 1:IMGS * SIDE - 1:PATCH, :]).then_inc(S["in_top"], 16)
            sp.dma_start(ximg[:, 1:6, row], main[:, 0:5, :]).then_inc(S["in_x0"], 16)
            for g in range(4):
                if g == 1:
                    sp.dma_start(ximg[:, 12:17, row], main[:, 11:16, :]).then_inc(S["in_x2"], 16)
                    sp.dma_start(ximg[0:TOKROWS - 1, WIN - 1, row], rows[PATCH:IMGS * SIDE:PATCH, :]).then_inc(S["in_bot"], 16)
                if g < 3:
                    sp.wait_ge(S["w_zero"], g + 1)
                else:
                    sp.wait_ge(S["w_zero_p"], 1)
                load_shifted(sp, g, S[f"in_w{g}"], range(RHO if g < 3 else RHO // 2))
            for v, n, src in ((V_BO, 4, bo), (V_G, 4, g_ffn), (V_B, 4, b_ffn), (V_B2, 4, b2),
                              (V_B1, 16, b1.rearrange("l (m p) -> (l m) p", p=128))):
                sp.dma_start(vrow[v:v + n, :], src).then_inc(S["in_vec"], 16)
            for v, src in ((V_CONVB, conv_b), (V_GAMMA, gamma), (V_BETA, beta), (V_DENSEB, dense_b),
                           (V_GF, g_f), (V_BF, b_f)):
                sp.dma_start(vrow[v:v + 1, :], src.rearrange("(a d) -> a d", a=1)).then_inc(S["in_vec"], 16)
            for j in range(2):
                dst = vrow[V_RMS:V_RMS + 8, :].rearrange("p (c j e) -> p c j e", c=4, j=2)[:, :, j, :]
                sp.dma_start(dst, rms_w.rearrange("l (s c) e -> (l s) c e", s=2)).then_inc(S["in_vec"], 16)

            def load_layer(l):
                for n, w in enumerate((Wq, Wk, Wv, Wo)):
                    sp.dma_start(nqkvo[:, n, :], w[bass.ds(l, 1), :, :].rearrange("l a b -> (l a) b")).then_inc(S["in_layer"], 16)
                sp.dma_start(nW1[:, :, :], W1[bass.ds(l, 1), :, :].rearrange("l (m p) d -> p (l m) d", p=128)).then_inc(S["in_layer"], 16)
                sp.dma_start(nW2[:, :, :], W2[bass.ds(l, 1), :, :].rearrange("l p (m k) -> p (l m) k", m=MC)).then_inc(S["in_layer"], 16)

            load_layer(0)
            with sp.Fori(1, LAYERS) as l:
                sp.wait_ge(S["tr_w2"], l)
                load_layer(l)
            for t in range(2):
                sp.wait_ge(S["fin_done"], t + 1)
                sp.dma_start(out.rearrange("b s d -> (b s) d")[half(t), :].rearrange("(c p) d -> p c d", p=CHUNK),
                             fin[:, HCH * t:HCH * t + HCH, :]).then_inc(S["out_done"], 16)
            sp.wait_ge(S["out_done"], 32)

        @block.gpsimd
        def _(pool):
            nc.gpsimd.memset(wshift[:, 3:5, :, :], 0.0).then_inc(S["w_zero_p"], 1)
            pool.wait_ge(S["w_zero_p"], 1)
            load_shifted(pool, 4, S["in_w4"], range(RHO))
            load_shifted(pool, 3, S["in_w3_pool"], range(RHO // 2, RHO))
            pool.dma_start(dwb[:, :], diffw.rearrange("(a l) -> a l", a=1).broadcast_to([128, LAYERS])).then_inc(S["in_diffw"], 16)
            pool.dma_start(densew[:, :], dense_w).then_inc(S["in_dense"], 16)
            nc.gpsimd.memset(kd[:, :, :, :, :], 0.0).then_inc(S["att_zero"], 1)
            nc.gpsimd.memset(qdb[:, :, :, :, :], 0.0).then_inc(S["att_zero"], 1)
            nc.gpsimd.memset(vd[:, :, :, :, :], 0.0).then_inc(S["att_zero"], 1)
            pool.dma_start(swn[:, :], switch_w).then_inc(S["in_sw"], 16)
            pool.dma_start(swb[:, :], switch_b.rearrange("(a l) -> a l", a=1).broadcast_to([CHUNK, EXPERTS])).then_inc(S["in_sw"], 16)
            pool.dma_start(ebn[:, :], expert_b).then_inc(S["in_sw"], 16)
            pool.wait_ge(S["win_done"], ROWG * CH)
            pool.dma_start(nexp[:, :, :], expert_w.rearrange("e f d -> f e d")).then_inc(S["in_exp"], 16)

            def power(n, t):
                pool.wait_ge(S["ln_var"], nth(n, t) + 1)
                nc.gpsimd.tensor_tensor(rs[:, t, 0:HCH], ms[:, t, 0:HCH], cst[0:CHUNK, C_POW:C_POW + HCH],
                                        ALU.pow).then_inc(S["ln_rs"], 1)

            pool.wait_ge(S["in_c"], 16)

            def twice_wo(l):
                pool.wait_ge(S["in_layer"], 96 * l + 96)
                ones_of_heads = cst[:, C_ONE:C_ONE + EDIM].rearrange("p (h e) -> p h e", h=1).broadcast_to([128, HEADS, EDIM])
                for j in range(2):
                    cols_of_heads = nqkvo[:, 3, :].rearrange("p (h e) -> p h e", e=EDIM)
                    nc.gpsimd.tensor_tensor(nWo2[:, :, :, j, :].rearrange("p s c e -> p (s c) e"),
                                            cols_of_heads, ones_of_heads, ALU.mult).then_inc(S["wo_dup"], 1)

            def spread_pool(l, t, copies):
                pool.wait_ge(S["q_sb"], 2 * l + t + 1)
                pr = slice(HPAIR * t, HPAIR * t + HPAIR)
                for a in copies:
                    mask = cst[:, C_SUB + a:C_SUB + a + 1].rearrange("p (a u q) -> p a u q", a=1, u=1).broadcast_to([128, HPAIR, 2, SEQ])
                    ins = nc.gpsimd.tensor_tensor(qx[:, pr, :, a, :], qS[:, t, :, :, :].rearrange("p u a q -> p a u q"), mask, ALU.mult)
                    if a == COPIES_POOL[t].stop - 1:
                        ins.then_inc(S["qx_pool"], 1)

            def layer(l, last=False):
                def diagonal(p):
                    pool.wait_ge(S["nmax_done"], PAIRS * l + p + 1)
                    if p >= 2:
                        pool.wait_ge(S["scores_done"], PAIRS * l + p - 1)
                    nc.gpsimd.tensor_tensor(dmax[:, p % 2, :, :], selq_b.rearrange("p (a q) -> p a q", a=1).broadcast_to([128, 2 * HSUB, SEQ]),
                                            nmax[:, p % 2, :].rearrange("p (a q) -> p a q", q=1).broadcast_to([128, 2 * HSUB, SEQ]),
                                            ALU.mult).then_inc(S["dmax_done"], 1)

                def inverse_rms(t):
                    pool.wait_ge(S["rms_ms"], 2 * l + t + 1)
                    nc.gpsimd.tensor_tensor(rs[0:RCH, t, 0:4], ms[0:RCH, t, 0:4], cst[0:RCH, C_POW:C_POW + 4],
                                            ALU.pow).then_inc(S["rms_r"], 1)

                diagonal(0)
                diagonal(1)
                spread_pool(l, 1, COPIES_POOL[1][:1])
                diagonal(2)
                spread_pool(l, 1, COPIES_POOL[1][1:])
                for p in range(3, PAIRS - 1):
                    diagonal(p)
                inverse_rms(0)
                diagonal(PAIRS - 1)
                power(l + 2, 0)
                if not last:
                    twice_wo(l + 1)
                inverse_rms(1)
                power(l + 2, 1)
                if not last:
                    spread_pool(l + 1, 0, COPIES_POOL[0])

            power(0, 0)
            twice_wo(0)
            power(1, 0)
            power(0, 1)
            power(1, 1)
            spread_pool(0, 0, COPIES_POOL[0])
            with pool.Fori(0, LAYERS - 1) as l:
                layer(l)
            layer(LAYERS - 1, last=True)
            for t in range(2):
                power(LAST, t)
                power(LAST + 1, t)

        @block.scalar
        def _(act):
            act.wait_ge(S["in_c"], 16)
            act.wait_ge(S["halo_zero"], 1)
            act.wait_ge(S["in_top"], 16)
            nc.scalar.activation(ximg[:, 0, :], ximg[:, 0, :], ACT.Copy, scale=cst[0:TOKROWS, C_TOP:C_TOP + 1]).then_inc(S["ximg_ok"], 1)
            act.wait_ge(S["in_bot"], 16)
            nc.scalar.activation(ximg[:, WIN - 1, :], ximg[:, WIN - 1, :], ACT.Copy, scale=cst[0:TOKROWS, C_BOT:C_BOT + 1]).then_inc(S["ximg_ok"], 1)
            for g in range(NTR):
                act.wait_ge(S["xT_tr"], g + 1)
                k = CH * ROWG_ORDER[g // 2 // CH] + g // 2 % CH
                nc.scalar.copy(xT[:, k, 3 * (g % 2):3 * (g % 2) + 3, :],
                               cols(g % 6, 3 * TOKROWS, slice(0, KWIN)).rearrange("p (w n) -> p w n", w=3)).then_inc(S["xT_cp"], 1)
            act.wait_ge(S["vec_tr"], 1)
            nc.scalar.copy(vcol[:, :], cols(5, V_END)).then_inc(S["vcol_done"], 1)

            def square(n, t):
                act.wait_ge(S["ln_cent"], nth(n, t) + 1)
                nc.scalar.activation(sq[:, half(t)], xc[:, half(t)], ACT.Square).then_inc(S["ln_sq"], 1)

            def copy_experts(g):
                act.wait_ge(S["exp_tr"], g + 1)
                nc.scalar.copy(texp[:, 4 * g:4 * g + 4, :], cols(BANK_EXPERTS[g], 512)).then_inc(S["exp_cp"], 1)

            square(0, 0)
            act.wait_ge(S["sw_tr"], 1)
            nc.scalar.copy(swT[:, :], cols(4, EXPERTS)).then_inc(S["swT_done"], 1)
            copy_experts(0)
            square(1, 0)
            square(0, 1)
            copy_experts(1)

            def copy_wqkv(l):
                act.wait_ge(S["tr_qkv"], l + 1)
                nc.scalar.copy(tqkv[:, :, :], cols(4, 384)).then_inc(S["w_qkv"], 1)

            def spread_act(l, t, copies):
                act.wait_ge(S["q_sb"], 2 * l + t + 1)
                pr = slice(HPAIR * t, HPAIR * t + HPAIR)
                for a in copies:
                    ins = nc.scalar.activation(qx[:, pr, :, a, :].rearrange("p a u q -> p u a q"), qS[:, t, :, :, :],
                                               ACT.Copy, scale=cst[:, C_SUB + a:C_SUB + a + 1])
                if a == HSUB - 1:
                    ins.then_inc(S["qx_act"], 1)

            def copy_qk(l, t):
                bq, bk, _ = BANK_QKV[t]
                act.wait_ge(S["qk_proj"], 2 * l + t + 1)
                q_v = cols(bq, HALF).rearrange("p (u a q) -> p u a q", u=2, q=SEQ)
                k_v = cols(bk, HALF).rearrange("p (u a q) -> p u a q", u=2, q=SEQ)
                nc.scalar.copy(qS[:, t, :, :, :], q_v).then_inc(S["q_sb"], 1)
                pr = slice(HPAIR * t, HPAIR * t + HPAIR)
                for j in range(2):
                    r = slice(64 * j, 64 * j + 64)
                    nc.scalar.copy(qdb[r, pr, :, j, 0:SEQ].rearrange("p a u q -> p u a q"), q_v[r])
                act.wait_ge(S["k_sb"], 2 * l + t + 1)
                for j in range(2):
                    r = slice(64 * j, 64 * j + 64)
                    ins = nc.scalar.copy(kd[r, pr, :, j, 0:SEQ].rearrange("p a u q -> p u a q"), k_v[r])
                ins.then_inc(S["qk_ev"], 1)

            def copy_v(l, t):
                bv = BANK_QKV[t][2]
                act.wait_ge(S["v_proj"], 2 * l + t + 1)
                pr = slice(HPAIR * t, HPAIR * t + HPAIR)
                for j in range(2):
                    r = slice(64 * j, 64 * j + SEQ)
                    ins = nc.scalar.copy(vd[r, pr, :, j, :], cols(bv, 512, r).rearrange("p (a h e) -> p a h e", a=HPAIR, h=HEADS))
                ins.then_inc(S["v_ev"], 1)

            def layer(l, last=False):
                act.wait_ge(S["tr_w1"], l + 1)
                nc.scalar.copy(tW1[:, :, :], cols(2, 512)).then_inc(S["w_1"], 1)
                act.wait_ge(S["tr_w2"], l + 1)
                nc.scalar.copy(tW2[:, :, :], cols(3, 512)).then_inc(S["w_2"], 1)
                copy_v(l, 0)
                copy_qk(l, 1)

                def exps(p):
                    b = 2 + 2 * (p % 2)
                    act.wait_ge(S["scores_done"], PAIRS * l + p + 1)
                    if p >= 2:
                        act.wait_ge(S["pv_done"], PAIRS * l + p - 1)
                    nc.scalar.activation(pT[:, p % 2, :, :], ps[:, b:b + 2, 0:HALF], ACT.Exp,
                                         scale=float(FDIM) ** -0.5).then_inc(S["exp_done"], 1)

                def square_heads(p):
                    act.wait_ge(S["o_done"], PAIRS * l + p + 1)
                    nc.scalar.activation(osq[:, :, p, :], o[:, :, p, :], ACT.Square).then_inc(S["osq_done"], 1)

                def copy_out(t):
                    act.wait_ge(S["wo_ps"], 2 * l + t + 1)
                    nc.scalar.activation(ao[:, t, :], cols(BANK_WO[t], HALF), ACT.Copy, scale=lp[:, L_OMD:L_OMD + 1]).then_inc(S["wo_sb"], 1)

                def gelu(t, m):
                    act.wait_ge(S["ffn1"], 2 * MC * l + MC * t + m + 1)
                    nc.scalar.activation(gact[:, t, m, :], cols(BANK_UP[MC * t + m], HALF), ACT.Gelu,
                                         bias=b1e[:, m:m + 1]).then_inc(S["gelu_done"], 1)

                exps(0)
                copy_v(l, 1)
                exps(1)
                spread_act(l, 1, COPIES_ACT[1][:2])
                exps(2)
                square_heads(0)
                spread_act(l, 1, COPIES_ACT[1][2:])
                for p in range(3, 5):
                    exps(p)
                    square_heads(p - 2)
                square_heads(3)
                exps(5)
                square_heads(4)
                copy_out(0)
                exps(6)
                square_heads(5)
                exps(7)
                square(l + 2, 0)
                square_heads(6)
                square_heads(7)
                nc.scalar.activation(table[:, :], cst[0:1, 0:1], ACT.Gelu)
                if not last:
                    copy_wqkv(l + 1)
                copy_out(1)
                act.wait_ge(S["b1_done"], l + 1)
                gelu(0, 0)
                gelu(0, 1)
                square(l + 2, 1)
                gelu(0, 2)
                gelu(0, 3)
                gelu(1, 0)
                gelu(1, 1)
                if last:
                    square(LAST, 0)
                gelu(1, 2)
                gelu(1, 3)
                if not last:
                    copy_qk(l + 1, 0)
                    spread_act(l + 1, 0, COPIES_ACT[0])

            copy_wqkv(0)
            copy_experts(2)
            act.wait_ge(S["att_zero"], 3)
            square(1, 1)
            copy_qk(0, 0)
            copy_experts(3)
            spread_act(0, 0, COPIES_ACT[0])
            with act.Fori(0, LAYERS - 1) as l:
                layer(l)
            layer(LAYERS - 1, last=True)

            def exp_logits(t):
                act.wait_ge(S["lg_done"], t + 1)
                nc.scalar.activation(eg[:, HCH * t:HCH * t + HCH, :], lg[:, HCH * t:HCH * t + HCH, :], ACT.Exp).then_inc(S["eg_done"], 1)

            def copy_prob(t):
                act.wait_ge(S["rp_ps"], t + 1)
                nc.scalar.copy(rpb[:, half(t)], cols(5, HALF)).then_inc(S["rp_sb"], 1)

            def copy_index(t):
                act.wait_ge(S["idx_ps"], t + 1)
                nc.scalar.copy(idxb[:, half(t)], cols(2 + t, HALF)).then_inc(S["idx_sb"], 1)

            def copy_out_rows(t):
                act.wait_ge(S["y_tr"], t + 1)
                nc.scalar.copy(fin[:, HCH * t:HCH * t + HCH, :], cols(5, HCH * 128, slice(0, CHUNK))).then_inc(S["fin_done"], 1)

            square(LAST + 1, 0)
            square(LAST, 1)
            exp_logits(0)
            square(LAST + 1, 1)
            copy_index(0)
            copy_prob(0)
            exp_logits(1)
            copy_index(1)
            copy_prob(1)
            copy_out_rows(0)
            copy_out_rows(1)

        @block.vector
        def _(dve):
            chain = Chain(dve, S["dvc"])
            nc.vector.memset(ximg[:, 0, :], 0.0)
            nc.vector.memset(ximg[:, WIN - 1, :], 0.0)
            nc.vector.memset(ximg[:, 1:WIN - 1, 0:CH], 0.0)
            nc.vector.memset(ximg[:, 1:WIN - 1, CH + SIDE * CH:SIDE * CH + 2 * CH], 0.0).then_inc(S["halo_zero"], 1)
            for g in range(3):
                nc.vector.memset(wshift[:, g, :, :], 0.0).then_inc(S["w_zero"], 1)

            dve.wait_ge(S["halo_zero"], 1)
            for a in ROWG_ORDER:
                dve.wait_ge(S[f"in_x{a}"], 16)
                if a == 0:
                    dve.wait_ge(S["ximg_ok"], 1)
                if a == ROWG - 1:
                    dve.wait_ge(S["ximg_ok"], 2)
                for c in range(CH):
                    dst = xwin[:, (a * CH + c) * GRID:(a * CH + c + 1) * GRID, :].rearrange("n w (r v) -> n w r v", v=WIN)
                    rws = ximg[:, RHO * a:RHO * a + RHO, :]
                    body = rws[:, :, 0:GRID * 48].rearrange("n r (w v c) -> n w r v c", w=GRID, c=CH)[:, :, :, :, c]
                    tail = rws[:, :, 48:48 + GRID * 48].rearrange("n r (w v c) -> n w r v c", w=GRID, c=CH)[:, :, :, 0:2, c]
                    nc.vector.tensor_copy(dst[:, :, :, 0:PATCH], body)
                    nc.vector.tensor_copy(dst[:, :, :, PATCH:WIN], tail).then_inc(S["win_done"], 1)
            dve.wait_ge(S["in_c"], 16)
            nc.vector.tensor_copy(cstb[:, :], cst[:, 0:C_RANK]).then_inc(S["cstb_done"], 1)
            dve.wait_ge(S["in_w0"], 16 * RHO)
            for g in (1, 4, 2):
                dve.wait_ge(S[f"in_w{g}"], 16 * RHO)
                chain.step(nc.vector.tensor_tensor(wshift[:, 0, :, :], wshift[:, 0, :, :], wshift[:, g, :, :], ALU.add))
            dve.wait_ge(S["in_w3"], 16 * (RHO // 2))
            dve.wait_ge(S["in_w3_pool"], 16 * (RHO - RHO // 2))
            for a in range(ROWG):
                nc.vector.tensor_tensor(wshift[:, 0, a, :], wshift[:, 0, a, :], wshift[:, 3, a, :], ALU.add).then_inc(S["weff_done"], 1)
            dve.wait_ge(S["vcol_done"], 1)

            def center(n, t, src, bank=BANK_NORM):
                dve.wait_ge(S["ln_mean"], nth(n, t) + 1)
                nc.vector.tensor_tensor(xc[:, half(t)], src[:, half(t)], cols(bank[t], HALF), ALU.subtract).then_inc(S["ln_cent"], 1)

            def variance(n, t, eps, bank=BANK_NORM):
                dve.wait_ge(S["ln_stat"], nth(n, t) + 1)
                nc.vector.tensor_scalar(ms[:, t, 0:HCH], cols(bank[t], HCH, slice(0, CHUNK), 300), eps, None, ALU.add).then_inc(S["ln_var"], 1)

            def token_norm(t):
                dve.wait_ge(S["ln_rb"], nth(0, t) + 1)
                chain.step(nc.vector.scalar_tensor_tensor(hn[:, half(t)], xc[:, half(t)], vcol[:, V_GAMMA:V_GAMMA + 1],
                                                          cols(6 + t, HALF), ALU.mult, ALU.mult))
                nc.vector.tensor_scalar(hn[:, half(t)], hn[:, half(t)], vcol[:, V_BETA:V_BETA + 1], None, ALU.add).then_inc(S["h_done"], 1)

            def conv_bias(t):
                dve.wait_ge(S["conv_done"], t + 1)
                nc.vector.tensor_scalar(X1[:, half(t)], cols(6 + t, HALF), vcol[:, V_CONVB:V_CONVB + 1], None, ALU.add).then_inc(S["ln_src"], 1)

            def dense_bias(t):
                dve.wait_ge(S["dense_done"], t + 1)
                nc.vector.tensor_scalar(H0[:, half(t)], cols(6 + t, HALF), vcol[:, V_DENSEB:V_DENSEB + 1], None, ALU.add).then_inc(S["ln_src"], 1)

            def scale_only(t):
                dve.wait_ge(S["ln_rb"], nth(1, t) + 1)
                nc.vector.tensor_tensor(X[:, half(t)], xc[:, half(t)], cols(6 + t, HALF), ALU.mult).then_inc(S["x_ready"], 1)

            conv_bias(0)
            center(0, 0, X1)
            variance(0, 0, EPS_TOK)
            token_norm(0)
            dense_bias(0)
            conv_bias(1)
            center(1, 0, H0)
            center(0, 1, X1)
            variance(1, 0, EPS_LN)
            variance(0, 1, EPS_TOK)
            dve.wait_ge(S["in_diffw"], 16)
            nc.vector.tensor_copy(params[:, :, 0:4].rearrange("p l k -> p k l"), vcol[:, 0:16].rearrange("p (k l) -> p k l", k=4))
            nc.vector.tensor_copy(params[:, :, L_B1:L_B1 + MC], vcol[:, V_B1:V_B1 + 16].rearrange("p (l m) -> p l m", l=LAYERS))
            for s in range(2):
                for j in range(2):
                    k = L_RMS + 2 * s + j
                    nc.vector.tensor_scalar(params[:, :, k], vcol[:, V_RMS:V_RMS + 8].rearrange("p (l s) -> p l s", s=2)[:, :, s],
                                            cst[:, C_RMS + j:C_RMS + j + 1], float(D), ALU.mult, ALU.mult)
            nc.vector.tensor_scalar(params[:, :, L_NDW], dwb[:, :], -1.0, None, ALU.mult)
            chain.step(nc.vector.tensor_scalar(params[:, :, L_OMD], dwb[:, :], -1.0, 1.0, ALU.mult, ALU.add))
            nc.vector.tensor_tensor(params[:, :, L_BO], params[:, :, L_BO], params[:, :, L_OMD], ALU.mult).then_inc(S["params_done"], 1)
            scale_only(0)
            token_norm(1)
            assert chain.n == DVE_BEFORE, chain.n
            dve.wait_ge(S["params_done"], 1)

            def last_norm(t):
                dve.wait_ge(S["ln_rb"], nth(LAST, t) + 1)
                chain.step(nc.vector.scalar_tensor_tensor(hn[:, half(t)], xc[:, half(t)], vcol[:, V_GF:V_GF + 1], cols(6 + t, HALF),
                                                          ALU.mult, ALU.mult))
                nc.vector.scalar_tensor_tensor(X1[:, half(t)], hn[:, half(t)], vcol[:, V_BF:V_BF + 1], H0[:, half(t)],
                                               ALU.add, ALU.add).then_inc(S["ln_src"], 1)

            def expert_norm(t):
                dve.wait_ge(S["ln_rb"], nth(LAST + 1, t) + 1)
                nc.vector.tensor_tensor(X[:, half(t)], xc[:, half(t)], cols(6 + t, HALF), ALU.mult).then_inc(S["x_ready"], 1)

            def spread(l, t, queries, keys):
                pr = slice(HPAIR * t, HPAIR * t + HPAIR)
                for buf, src, done, end in ((qx, qS, queries, COPIES_DVE[t].stop), (kxb, kSb, keys, HSUB)):
                    for a in done:
                        ins = nc.vector.tensor_scalar(buf[:, pr, :, a, :].rearrange("p a u q -> p u a q"), src[:, t, :, :, :],
                                                      cst[:, C_SUB + a:C_SUB + a + 1], None, ALU.mult)
                        if a == end - 1:
                            ins.then_inc(S["qx_done" if buf is qx else "kx_done"], 1)

            def keys_bf16(l, t):
                dve.wait_ge(S["qk_proj"], 2 * l + t + 1)
                nc.vector.tensor_copy(kSb[:, t, :, :, :], cols(BANK_QKV[t][1], HALF).rearrange("p (u a q) -> p u a q", u=2, q=SEQ)).then_inc(S["k_sb"], 1)
                dve.wait_ge(S["k_sb"], 2 * l + t + 1)

            def rms_weights(l):
                nc.vector.tensor_copy(lrms[:, :], params[:, bass.ds(l, 1), L_RMS:L_RMS + 4].rearrange("p l k -> p (l k)")).then_inc(S["lrms_ready"], 1)

            def scaled_wo(l):
                dve.wait_ge(S["lrms_ready"], l + 1)
                dve.wait_ge(S["tr_wo"], l + 1)
                for s in range(2):
                    for j in range(2):
                        k = 2 * s + j
                        ins = nc.vector.tensor_scalar(tWo[:, s, j, :], cols(5, 128, at=128 * s), lrms[:, k:k + 1], None, ALU.mult)
                ins.then_inc(S["w_o"], 1)

            def layer(l, last=False):
                chain.rebase(DVE_LAYER * l + DVE_BEFORE)
                dve.wait_ge(S["x_ready"], 2 * l + 2)
                nc.vector.tensor_copy(lp[:, :], params[:, bass.ds(l, 1), :].rearrange("p l k -> p (l k)")).then_inc(S["lp_ready"], 1)

                def maxima(p):
                    dve.wait_ge(S["sc_max"], PAIRS * l + p + 1)
                    if p >= 2:
                        dve.wait_ge(S["dmax_done"], PAIRS * l + p - 1)
                    nc.vector.tensor_reduce(nmax[:, p % 2, :], ps[:, 0:2, 0:HALF].rearrange("p u (a k) -> p u a k", k=SEQ),
                                            AX_X, ALU.max, negate=True).then_inc(S["nmax_done"], 1)

                def normalize(p, meanwhile=None):
                    b = BANK_VALUE[p]
                    dve.wait_ge(S["pv_done"], PAIRS * l + p + 1)
                    sums = cols(b, 144, at=144).rearrange("p (s i q) -> p s i q", s=2, i=2)
                    vals = cols(b, 144).rearrange("p (s i q) -> p s i q", s=2, i=2)
                    r, w = rden[:, p % 2], on[:, p % 2]
                    chain.step(nc.vector.reciprocal(r, sums), meanwhile)
                    chain.step(nc.vector.tensor_tensor(w, vals, r, ALU.mult))
                    nc.vector.scalar_tensor_tensor(o[:, :, p, :], w[:, :, 1, :], lp[:, L_NDW:L_NDW + 1], w[:, :, 0, :],
                                                   ALU.mult, ALU.add).then_inc(S["o_done"], 1)

                def mean_square(t):
                    dve.wait_ge(S["rms_ps"], 2 * l + t + 1)
                    nc.vector.tensor_scalar(ms[0:RCH, t, :], cols(BANK_POST[t], 4, slice(0, RCH), 300), EPS_RMS, None, ALU.add).then_inc(S["rms_ms"], 1)

                def add_attention(t):
                    dve.wait_ge(S["wo_sb"], 2 * l + t + 1)
                    dve.wait_ge(S["rms_rb"], 2 * l + t + 1)
                    chain.step(nc.vector.tensor_tensor(xa[:, t, :], ao[:, t, :], cols(BANK_POST[t], HALF), ALU.mult))
                    nc.vector.scalar_tensor_tensor(X1[:, half(t)], xa[:, t, :], lp[:, L_BO:L_BO + 1], X[:, half(t)],
                                                   ALU.add, ALU.add).then_inc(S["ln_src"], 1)

                def scale_norm(t):
                    dve.wait_ge(S["ln_rb"], 2 * l + 4 + t + 1)
                    nc.vector.scalar_tensor_tensor(hn[:, half(t)], xc[:, half(t)], lp[:, L_G:L_G + 1], cols(BANK_POST[t], HALF),
                                                   ALU.mult, ALU.mult).then_inc(S["h_done"], 1)

                dve.wait_ge(S["q_sb"], 2 * l + 1)
                spread(l, 0, COPIES_DVE[0], ())
                maxima(0)
                keys_bf16(l, 1)
                dve.wait_ge(S["q_sb"], 2 * l + 2)
                maxima(1)
                spread(l, 1, (), range(HSUB))
                maxima(2)
                spread(l, 1, COPIES_DVE[1], ())
                normalize(0)
                maxima(3)
                normalize(1)
                maxima(4)
                normalize(2)
                maxima(5)
                normalize(3)
                maxima(6)
                normalize(4, lambda: mean_square(0))
                maxima(7)
                normalize(5)
                add_attention(0)
                normalize(6, lambda: center(l + 2, 0, X1, BANK_POST))
                normalize(7, lambda: variance(l + 2, 0, EPS_LN, BANK_POST))
                dve.wait_ge(S["b1_ps"], l + 1)
                nc.vector.tensor_tensor(b1e[:, :], lp[:, L_B1:L_B1 + MC], cols(5, MC), ALU.add).then_inc(S["b1_done"], 1)
                mean_square(1)
                scale_norm(0)
                add_attention(1)
                center(l + 2, 1, X1, BANK_POST)
                variance(l + 2, 1, EPS_LN, BANK_POST)
                scale_norm(1)
                if not last:
                    rms_weights(l + 1)

                def add_mlp(t):
                    dve.wait_ge(S["ffn2"], 2 * l + t + 1)
                    nc.vector.scalar_tensor_tensor(X[:, half(t)], cols(6 + t, HALF), lp[:, L_B2:L_B2 + 1], X1[:, half(t)],
                                                   ALU.add, ALU.add).then_inc(S["x_ready"], 1)

                add_mlp(0)
                if not last:
                    scaled_wo(l + 1)
                    keys_bf16(l + 1, 0)
                    spread(l + 1, 0, (), range(HSUB))
                else:
                    center(LAST, 0, X)
                    variance(LAST, 0, EPS_LN)
                    last_norm(0)
                    center(LAST + 1, 0, X1)
                    variance(LAST + 1, 0, EPS_LN)
                add_mlp(1)
                assert last or chain.n == DVE_LAYER, chain.n

            rms_weights(0)
            dense_bias(1)
            scaled_wo(0)
            center(1, 1, H0)
            keys_bf16(0, 0)
            variance(1, 1, EPS_LN)
            spread(0, 0, (), range(HSUB))
            scale_only(1)
            with dve.Fori(0, LAYERS - 1) as l:
                layer(l)
            layer(LAYERS - 1, last=True)

            def over(v):
                return v.rearrange("p (c e) -> p c e", e=1).broadcast_to([CHUNK, HCH, EXPERTS])

            def chunks(buf, t):
                return buf[:, HCH * t:HCH * t + HCH, :]

            def r(k, t):
                return r1[:, k, HCH * t:HCH * t + HCH]

            def shift_logits(t):
                dve.wait_ge(S["lg_ps"], t + 1)
                dve.wait_ge(S["ln_rs"], nth(LAST + 1, t) + 1)
                lgt = chunks(lg, t)
                for c in range(HCH):
                    ins = nc.vector.scalar_tensor_tensor(lg[:, HCH * t + c, :], cols(t, EXPERTS, slice(0, CHUNK), EXPERTS * c), rs[:, t, c:c + 1],
                                                         swb[:, :], ALU.mult, ALU.add)
                chain.step(ins)
                chain.step(nc.vector.tensor_reduce(r(0, t), lgt, AX_X, ALU.max))
                nc.vector.tensor_tensor(lgt, lgt, over(r(0, t)), ALU.subtract).then_inc(S["lg_done"], 1)

            def pick(t):
                dve.wait_ge(S["eg_done"], t + 1)
                lgt, egt = chunks(lg, t), chunks(eg, t)
                chain.step(nc.vector.tensor_reduce(r(1, t), egt, AX_X, ALU.max))
                chain.step(nc.vector.tensor_tensor(lgt, egt, over(r(1, t)), ALU.is_equal))
                chain.step(nc.vector.tensor_tensor(lgt, lgt, cst[0:CHUNK, C_RANK:C_RANK + EXPERTS].rearrange("p (c e) -> p c e", c=1).broadcast_to([CHUNK, HCH, EXPERTS]),
                                                   ALU.mult))
                chain.step(nc.vector.tensor_reduce(r(2, t), lgt, AX_X, ALU.max))
                nc.vector.tensor_tensor(chunks(ohb, t), lgt, over(r(2, t)), ALU.is_equal).then_inc(S["oh_done"], 1)
                nc.vector.tensor_tensor(chunks(ohf, t), lgt, over(r(2, t)), ALU.is_equal)

            def probability(t):
                chain.step(nc.vector.tensor_reduce(r(3, t), chunks(eg, t), AX_X, ALU.add))
                chain.step(nc.vector.reciprocal(r(4, t), r(3, t)))
                nc.vector.tensor_tensor(chunks(route, t)[:, :, EXPERTS + 1], r(1, t), r(4, t), ALU.mult)

            def place(t):
                dve.wait_ge(S["cum_ps"], t + 1)
                chain.step(nc.vector.tensor_tensor(chunks(lg, t), chunks(ohf, t),
                                                   cols(t, HCH * EXPERTS, slice(0, CHUNK), 64).rearrange("p (c e) -> p c e", e=EXPERTS), ALU.mult))
                chain.step(nc.vector.tensor_reduce(r(5, t), chunks(lg, t), AX_X, ALU.add))
                nc.vector.tensor_scalar(chunks(route, t)[:, :, EXPERTS], r(5, t), float(CAPACITY), None, ALU.is_gt)
                chain.step(nc.vector.tensor_scalar(r(6, t), r(5, t), float(CAPACITY), None, ALU.is_le))
                nc.vector.tensor_tensor(chunks(route, t)[:, :, 0:EXPERTS], chunks(ohf, t), over(r(6, t)), ALU.mult).then_inc(S["route_done"], 1)

            def copy_route(t):
                dve.wait_ge(S["route_tr"], t + 1)
                rT = cols(t, HALF, slice(0, EXPERTS + 2), 128)
                nc.vector.tensor_copy(routeTb[:, half(t)], rT).then_inc(S["routeTb_done"], 1)
                nc.vector.tensor_copy(routeT[:, half(t)], rT).then_inc(S["routeT_done"], 1)

            def mask_tokens(t, experts):
                for e in experts:
                    k = EXPERTS * t + e
                    if e == 0:
                        dve.wait_ge(S["idx_sb"], t + 1)
                    if k >= XM:
                        dve.wait_ge(S["exp_ps"], k - XM + 1)
                    nc.vector.scalar_tensor_tensor(xm[:, k % XM, :], idxb[:, half(t)], float(e), X[:, half(t)], ALU.is_equal, ALU.mult).then_inc(S["xm_done"], 1)

            def keep_dropped(t):
                k = kept[:, half(t)]
                chain.step(nc.vector.scalar_tensor_tensor(k, idxb[:, half(t)], float(EXPERTS), X[:, half(t)], ALU.is_equal, ALU.mult))
                dve.wait_ge(S["rp_sb"], t + 1)
                chain.step(nc.vector.tensor_tensor(k, k, rpb[:, half(t)], ALU.mult))
                chain.step(nc.vector.tensor_tensor(k, k, X1[:, half(t)], ALU.add))

            def finish(t):
                dve.wait_ge(S["exp_ps"], EXPERTS * (t + 1))
                chain.step(nc.vector.tensor_tensor(hn[:, half(t)], rpb[:, half(t)], cols(6 + t, HALF), ALU.mult))
                nc.vector.tensor_tensor(hn[:, half(t)], hn[:, half(t)], kept[:, half(t)], ALU.add).then_inc(S["y_done"], 1)

            center(LAST, 1, X)
            dve.wait_ge(S["in_sw"], 48)
            shift_logits(0)
            expert_norm(0)
            variance(LAST, 1, EPS_LN)
            pick(0)
            last_norm(1)
            probability(0)
            place(0)
            center(LAST + 1, 1, X1)
            copy_route(0)
            variance(LAST + 1, 1, EPS_LN)
            mask_tokens(0, range(0, 3))
            shift_logits(1)
            mask_tokens(0, range(3, 6))
            expert_norm(1)
            keep_dropped(0)
            mask_tokens(0, range(6, 7))
            pick(1)
            mask_tokens(0, range(7, 9))
            probability(1)
            place(1)
            mask_tokens(0, range(9, 12))
            copy_route(1)
            mask_tokens(0, range(12, EXPERTS))
            mask_tokens(1, range(0, 3))
            finish(0)
            mask_tokens(1, range(3, 10))
            keep_dropped(1)
            mask_tokens(1, range(10, EXPERTS))
            finish(1)

        @block.tensor
        def _(pe):
            mm = nc.tensor.matmul

            def turn(dst, src, k):
                return nc.tensor.transpose(dst, src, ident[0:k, 0:k])

            pe.wait_ge(S["in_c"], 16)
            for g in range(NTR):
                pe.wait_ge(S["win_done"], g // 2 + 1)
                if g >= 6:
                    pe.wait_ge(S["xT_cp"], g - 5)
                k = CH * ROWG_ORDER[g // 2 // CH] + g // 2 % CH
                for w in range(3):
                    ins = turn(cols(g % 6, TOKROWS, slice(0, KWIN), TOKROWS * w), xwin[:, GRID * k + 3 * (g % 2) + w, :], TOKROWS)
                ins.then_inc(S["xT_tr"], 1)
            pe.wait_ge(S["xT_cp"], NTR)

            def conv(t, chunks):
                for k in chunks:
                    pe.wait_ge(S["weff_done"], k // CH + 1)
                    ins = mm(cols(6 + t, HALF), wshift[:, 0, k // CH, D * (k % CH):D * (k % CH) + D],
                             xT[:, k, :, 48 * t:48 * t + 48].rearrange("p w n -> p n w"), start=(k == 0), stop=(k == ROWG * CH - 1))
                if k == ROWG * CH - 1:
                    ins.then_inc(S["conv_done"], 1)

            def mean(n, t, src, ready, value, bank=BANK_NORM):
                pe.wait_ge(ready, value)
                mm(cols(bank[t], HALF), meanw, src[:, half(t)], start=True, stop=True).then_inc(S["ln_mean"], 1)

            def stat(n, t, bank=BANK_NORM):
                pe.wait_ge(S["ln_sq"], nth(n, t) + 1)
                for c in range(HCH):
                    ins = mm(cols(bank[t], 1, slice(0, CHUNK), 300 + c), sq[:, HALF * t + CHUNK * c:HALF * t + CHUNK * c + CHUNK],
                             meanw[:, 0:1], start=True, stop=True)
                ins.then_inc(S["ln_stat"], 1)

            def bcast(n, t, bank=BANK_NORM):
                pe.wait_ge(S["ln_rs"], nth(n, t) + 1)
                for c in range(HCH):
                    ins = mm(cols(bank[t], CHUNK, at=CHUNK * c), rs[:, t, c:c + 1].broadcast_to([CHUNK, 128]), ident[0:CHUNK, 0:CHUNK],
                             start=True, stop=True)
                ins.then_inc(S["ln_rb"], 1)

            def dense(t):
                pe.wait_ge(S["h_done"], t + 1)
                mm(cols(6 + t, HALF), densew[:, :], hn[:, half(t)], start=True, stop=True).then_inc(S["dense_done"], 1)

            def turn_qkv(l):
                pe.wait_ge(S["in_layer"], 96 * l + 96)
                for n in range(3):
                    ins = turn(cols(4, 128, at=128 * n), nqkvo[:, n, :], 128)
                ins.then_inc(S["tr_qkv"], 1)

            def turn_wo(l):
                pe.wait_ge(S["wo_dup"], 2 * l + 2)
                for s in range(2):
                    ins = turn(cols(5, 128, at=128 * s), nWo2[:, s, :, :, :].rearrange("p c j e -> p (c j e)"), 128)
                ins.then_inc(S["tr_wo"], 1)

            def turn_experts(g):
                if g >= 2:
                    pe.wait_ge(S["exp_cp"], g - 1)
                for k in range(4):
                    ins = turn(cols(BANK_EXPERTS[g], 128, at=128 * k), nexp[:, 4 * g + k, :], 128)
                ins.then_inc(S["exp_tr"], 1)

            conv(0, range(0, 6))
            pe.wait_ge(S["in_vec"], 16 * 13)
            turn(cols(5, V_END), vrow[:, :], V_END).then_inc(S["vec_tr"], 1)
            conv(0, range(6, 9))
            conv(1, range(0, 3))
            mean(0, 0, X1, S["ln_src"], 1)
            conv(1, range(3, 6))
            stat(0, 0)
            conv(1, range(6, 9))
            bcast(0, 0)
            pe.wait_ge(S["in_sw"], 48)
            turn(cols(4, EXPERTS), swn[:, :], EXPERTS).then_inc(S["sw_tr"], 1)
            pe.wait_ge(S["in_exp"], 16)
            turn_experts(0)
            pe.wait_ge(S["in_dense"], 16)
            dense(0)
            turn_experts(1)
            mean(1, 0, H0, S["ln_src"], 2)
            mean(0, 1, X1, S["ln_src"], 3)
            pe.wait_ge(S["swT_done"], 1)
            turn_qkv(0)
            stat(1, 0)
            stat(0, 1)
            turn_wo(0)
            turn_experts(2)
            bcast(1, 0)
            bcast(0, 1)
            pe.wait_ge(S["att_zero"], 3)
            pe.wait_ge(S["cstb_done"], 1)

            def project_qk(l, t, first=False):
                bq, bk, _ = BANK_QKV[t]
                pe.wait_ge(S["x_ready"], 2 * l + t + 1)
                pe.wait_ge(S["w_qkv"], l + 1)
                if t == 0 and not first:
                    pe.wait_ge(S["gelu_done"], 2 * MC * l - MC + 1)
                if t == 1:
                    pe.wait_ge(S["w_o"], l + 1)
                for b, n in ((bq, 0), (bk, 1)):
                    for u in range(2):
                        for j in range(2):
                            ins = mm(cols(b, HALF // 2, slice(64 * j, 64 * j + 64), HALF // 2 * u), tqkv[:, n, 64 * u:64 * u + 64],
                                     of_image(X[:, half(t)], j), start=True, stop=True)
                ins.then_inc(S["qk_proj"], 1)

            def project_v(l, t):
                bv = BANK_QKV[t][2]
                for a in range(HPAIR):
                    for j in range(2):
                        at = HALF * t + 2 * SEQ * a + SEQ * j
                        ins = mm(cols(bv, 128, slice(64 * j, 64 * j + SEQ), 128 * a), X[:, at:at + SEQ], tqkv[:, 2, :], start=True, stop=True)
                ins.then_inc(S["v_proj"], 1)

            def layer(l, last=False):
                pe.wait_ge(S["exp_cp"], 3)
                for m in range(MC):
                    ins = turn(cols(2, 128, at=128 * m), nW1[:, m, :], 128)
                ins.then_inc(S["tr_w1"], 1)
                pe.wait_ge(S["exp_cp"], 4)
                for m in range(MC):
                    ins = turn(cols(3, 128, at=128 * m), nW2[:, m, :], 128)
                ins.then_inc(S["tr_w2"], 1)
                project_qk(l, 1)

                def approx(p):
                    t = p // HPAIR
                    pe.wait_ge(S["qk_ev"], 2 * l + t + 1)
                    pe.wait_ge(S["kx_done"], 2 * l + t + 1)
                    if p >= 1:
                        pe.wait_ge(S["nmax_done"], PAIRS * l + p)
                    for u in range(2):
                        ins = mm(cols(u, HALF), qdb[:, p, u, :, :].rearrange("p j q -> p (j q)"), kxb[:, p, u, :, :], start=True, stop=True)
                    ins.then_inc(S["sc_max"], 1)

                def scores(p):
                    b = 2 + 2 * (p % 2)
                    pe.wait_ge(S["qx_done"], 2 * l + p // HPAIR + 1)
                    pe.wait_ge(S["qx_act"], 2 * l + p // HPAIR + 1)
                    pe.wait_ge(S["qx_pool"], 2 * l + p // HPAIR + 1)
                    if p == 0:
                        pe.wait_ge(S["w_1"], l + 1)
                        pe.wait_ge(S["w_2"], l + 1)
                    if p == 1:
                        pe.wait_ge(S["qk_ev"], 2 * l + 2)
                    if p >= 2:
                        pe.wait_ge(S["exp_done"], PAIRS * l + p - 1)
                    for u in range(2):
                        mm(cols(b + u, HALF), kd[:, p, u, :, :].rearrange("p j q -> p (j q)"), qx[:, p, u, :, :], start=True, stop=False)

                def less_max(p):
                    b = 2 + 2 * (p % 2)
                    pe.wait_ge(S["dmax_done"], PAIRS * l + p + 1)
                    for u in range(2):
                        ins = mm(cols(b + u, HALF), sameimg_b, dmax[:, p % 2, HSUB * u:HSUB * u + HSUB, :], start=False, stop=True)
                    ins.then_inc(S["scores_done"], 1)

                def values(p):
                    b = BANK_VALUE[p]
                    pe.wait_ge(S["exp_done"], PAIRS * l + p + 1)
                    if p < 2:
                        pe.wait_ge(S["v_ev"], 2 * l + p + 1)
                    same_bank = [q for q in range(p) if BANK_VALUE[q] == b]
                    if same_bank:
                        pe.wait_ge(S["o_done"], PAIRS * l + same_bank[-1] + 1)
                    for h in range(HEADS):
                        u, c = h // 4, h % 4
                        w = pT[:, p % 2, u, 2 * SEQ * c:2 * SEQ * c + 2 * SEQ]
                        r = slice(32 * c, 32 * c + 32)
                        mm(cols(b, 2 * SEQ, r, 2 * SEQ * u), vd[:, p, h, :, :].rearrange("p j e -> p (j e)"), w, start=True, stop=True)
                        ins = mm(cols(b, 2 * SEQ, r, 144 + 2 * SEQ * u), cst[:, C_SUMIMG:C_SUMIMG + 32], w, start=True, stop=True)
                    ins.then_inc(S["pv_done"], 1)

                def mean_squares(t):
                    pe.wait_ge(S["osq_done"], PAIRS * l + HPAIR * t + HPAIR)
                    for c in range(2):
                        for s in range(2):
                            a = HPAIR * t + 2 * c
                            ins = mm(cols(BANK_POST[t], 2, slice(0, RCH), 300 + 2 * c), osq[:, s, a:a + 2, :].rearrange("p a q -> p (a q)"),
                                     cst[:, C_RMS:C_RMS + 2], start=(s == 0), stop=(s == 1))
                    ins.then_inc(S["rms_ps"], 1)

                def rms_bcast(t):
                    pe.wait_ge(S["rms_r"], 2 * l + t + 1)
                    if t == 0:
                        pe.wait_ge(S["wo_sb"], 2 * l + 1)
                    for j in range(2):
                        for c in range(2):
                            ins = mm(of_image(cols(BANK_POST[t], HALF), j)[:, 2 * c:2 * c + 2, :], rs[0:RCH, t, 2 * c + j:2 * c + j + 1].broadcast_to([RCH, 128]),
                                     ident[0:RCH, 0:RCH], start=True, stop=True)
                    ins.then_inc(S["rms_rb"], 1)

                def project_out(t, first, end):
                    pe.wait_ge(S["o_done"], PAIRS * l + HPAIR * t + end)
                    if t == 0:
                        pe.wait_ge(S["rms_ms"], 2 * l + 1)
                    for j in range(2):
                        for s in range(2):
                            ins = mm(of_image(cols(BANK_WO[t], HALF), j)[:, first:end, :], tWo[:, s, j, :],
                                     o[:, s, HPAIR * t + first:HPAIR * t + end, :].rearrange("p a q -> p (a q)"), start=(s == 0), stop=(s == 1))
                    if end == HPAIR:
                        ins.then_inc(S["wo_ps"], 1)

                def up(t, m):
                    pe.wait_ge(S["h_done"], 2 * l + 2 + t + 1)
                    if t == 1 and m >= 1:
                        pe.wait_ge(S["gelu_done"], 2 * MC * l + m)
                    if t == 0 and m == 3:
                        pe.wait_ge(S["b1_done"], l + 1)
                    if t == 0 and m == 2 and not last:
                        pe.wait_ge(S["w_qkv"], l + 2)
                    mm(cols(BANK_UP[MC * t + m], HALF), tW1[:, m, :], hn[:, half(t)], start=True, stop=True).then_inc(S["ffn1"], 1)

                def down(t, m):
                    if m == 0:
                        pe.wait_ge(S["o_done"], PAIRS * l + PAIRS)
                    pe.wait_ge(S["gelu_done"], 2 * MC * l + MC * t + m + 1)
                    ins = mm(cols(6 + t, HALF), tW2[:, m, :], gact[:, t, m, :], start=(m == 0), stop=(m == MC - 1))
                    if m == MC - 1:
                        ins.then_inc(S["ffn2"], 1)

                def mlp_bias():
                    pe.wait_ge(S["lp_ready"], l + 1)
                    for m in range(MC):
                        ins = mm(cols(5, 1, at=m), tW1[:, m, :], lp[:, L_B:L_B + 1], start=True, stop=True)
                    ins.then_inc(S["b1_ps"], 1)

                approx(0)
                scores(0)
                approx(1)
                project_v(l, 1)
                less_max(0)
                for p in range(1, 5):
                    scores(p)
                    approx(p + 1)
                    values(p - 1)
                    less_max(p)
                scores(5)
                approx(6)
                values(4)
                less_max(5)
                scores(6)
                mean_squares(0)
                approx(7)
                less_max(6)
                project_out(0, 0, HPAIR)
                values(5)
                rms_bcast(0)
                scores(7)
                values(6)
                less_max(7)
                mean(l + 2, 0, X1, S["ln_src"], 2 * l + 5, BANK_POST)
                values(7)
                stat(l + 2, 0, BANK_POST)
                project_out(1, 0, HPAIR - 1)
                mlp_bias()
                if not last:
                    turn_qkv(l + 1)
                bcast(l + 2, 0, BANK_POST)
                mean_squares(1)
                project_out(1, HPAIR - 1, HPAIR)
                up(0, 0)
                rms_bcast(1)
                up(0, 1)
                up(0, 2)
                mean(l + 2, 1, X1, S["ln_src"], 2 * l + 6, BANK_POST)
                up(0, 3)
                down(0, 0)
                stat(l + 2, 1, BANK_POST)
                down(0, 1)
                down(0, 2)
                bcast(l + 2, 1, BANK_POST)
                down(0, 3)
                if not last:
                    turn_wo(l + 1)
                up(1, 0)
                up(1, 1)
                if last:
                    mean(LAST, 0, X, S["x_ready"], 2 * LAYERS + 1)
                up(1, 2)
                if last:
                    stat(LAST, 0)
                up(1, 3)
                if not last:
                    project_qk(l + 1, 0)
                    project_v(l + 1, 0)
                else:
                    bcast(LAST, 0)
                down(1, 0)
                if last:
                    mean(LAST + 1, 0, X1, S["ln_src"], 2 * LAYERS + 5)
                down(1, 1)
                if last:
                    stat(LAST + 1, 0)
                down(1, 2)
                down(1, 3)

            dense(1)
            turn_experts(3)
            mean(1, 1, H0, S["ln_src"], 4)
            project_qk(0, 0, first=True)
            project_v(0, 0)
            stat(1, 1)
            bcast(1, 1)
            with pe.Fori(0, LAYERS - 1) as l:
                layer(l)
            layer(LAYERS - 1, last=True)

            def logits(t):
                pe.wait_ge(S["ln_cent"], nth(LAST + 1, t) + 1)
                for c in range(HCH):
                    at = HALF * t + CHUNK * c
                    ins = mm(cols(t, EXPERTS, slice(0, CHUNK), EXPERTS * c), xc[:, at:at + CHUNK], swT[:, :], start=True, stop=True)
                ins.then_inc(S["lg_ps"], 1)

            def queue(t):
                pe.wait_ge(S["oh_done"], t + 1)
                for c in range(HCH * t, HCH * t + HCH):
                    dst = cols(t, EXPERTS, slice(0, CHUNK), 64 + EXPERTS * (c % HCH))
                    for k in range(c):
                        mm(dst, cstb[0:CHUNK, C_ONE:C_ONE + CHUNK], ohb[:, k, :], start=(k == 0), stop=False)
                    ins = mm(dst, cstb[0:CHUNK, C_CUM:C_CUM + CHUNK], ohb[:, c, :], start=(c == 0), stop=True)
                ins.then_inc(S["cum_ps"], 1)

            def turn_route(t):
                pe.wait_ge(S["route_done"], t + 1)
                for c in range(HCH):
                    ins = turn(cols(t, CHUNK, slice(0, EXPERTS + 2), 128 + CHUNK * c), route[:, HCH * t + c, :], CHUNK)
                ins.then_inc(S["route_tr"], 1)

            def index(t):
                pe.wait_ge(S["routeTb_done"], t + 1)
                mm(cols(2 + t, HALF), cstb[0:EXPERTS + 2, C_INDEX:C_INDEX + 1].broadcast_to([EXPERTS + 2, 128]), routeTb[:, half(t)],
                   start=True, stop=True).then_inc(S["idx_ps"], 1)

            def probability(t):
                pe.wait_ge(S["routeT_done"], t + 1)
                mm(cols(5, HALF), ident[0:EXPERTS + 2, EXPERTS + 1:EXPERTS + 2].broadcast_to([EXPERTS + 2, 128]), routeT[:, half(t)],
                   start=True, stop=True).then_inc(S["rp_ps"], 1)

            def bias(t):
                mm(cols(6 + t, HALF), ebn[:, :], routeT[0:EXPERTS, half(t)], start=False, stop=False)

            def experts(t, some):
                for e in some:
                    k = EXPERTS * t + e
                    pe.wait_ge(S["xm_done"], k + 1)
                    mm(cols(6 + t, HALF), texp[:, e, :], xm[:, k % XM, :],
                       start=(e == 0), stop=(e == EXPERTS - 1)).then_inc(S["exp_ps"], 1)

            def turn_out(t):
                pe.wait_ge(S["y_done"], t + 1)
                if t == 0:
                    pe.wait_ge(S["rp_sb"], 2)
                else:
                    pe.wait_ge(S["fin_done"], 1)
                for c in range(HCH):
                    at = HALF * t + CHUNK * c
                    ins = turn(cols(5, 128, slice(0, CHUNK), 128 * c), hn[:, at:at + CHUNK], 128)
                ins.then_inc(S["y_tr"], 1)

            logits(0)
            mean(LAST, 1, X, S["x_ready"], 2 * LAYERS + 2)
            bcast(LAST + 1, 0)
            stat(LAST, 1)
            bcast(LAST, 1)
            queue(0)
            mean(LAST + 1, 1, X1, S["ln_src"], 2 * LAYERS + 6)
            turn_route(0)
            logits(1)
            stat(LAST + 1, 1)
            index(0)
            probability(0)
            experts(0, range(0, 1))
            bcast(LAST + 1, 1)
            experts(0, range(1, 3))
            experts(0, range(3, 6))
            queue(1)
            experts(0, range(6, 9))
            bias(0)
            turn_route(1)
            experts(0, range(9, 11))
            index(1)
            experts(0, range(11, EXPERTS))
            probability(1)
            experts(1, range(0, 3))
            bias(1)
            turn_out(0)
            experts(1, range(3, EXPERTS))
            turn_out(1)


_ORDER = ['x', 'L0_tok_conv_w', 'L0_tok_conv_b', 'L0_tok_gamma', 'L0_tok_beta', 'L0_tok_dense_w', 'L0_tok_dense_b',
          'L0_attn_Wq', 'L0_attn_Wk', 'L0_attn_Wv', 'L0_attn_rms_w', 'L0_attn_Wo', 'L0_attn_bo', 'L0_attn_diffw',
          'L0_attn_g_ffn', 'L0_attn_b_ffn', 'L0_attn_W1', 'L0_attn_b1', 'L0_attn_W2', 'L0_attn_b2', 'L0_attn_g_f',
          'L0_attn_b_f', 'L0_ffn_switch_w', 'L0_ffn_switch_b', 'L0_ffn_expert_w', 'L0_ffn_expert_b']


def kernel(**inputs):
    import concourse.bacc as bacc
    from concourse.bass_utils import run_bass_kernel_spmd

    nc = bacc.Bacc("TRN2", target_bir_lowering=False, num_devices=1)
    arrays, args = {}, []
    for name in _ORDER + ['consts']:
        a = constants() if name == 'consts' else np.ascontiguousarray(inputs[name])
        arrays[f"in_{name}_dram"] = a
        args.append(nc.dram_tensor(f"in_{name}_dram", a.shape, mybir.dt.from_np(a.dtype), kind="ExternalInput").ap())
    args.append(nc.dram_tensor("out_0_dram", (IMGS, SEQ, D), F32, kind="ExternalOutput").ap())
    vit_tower(nc, *args)
    r = run_bass_kernel_spmd(nc, [arrays], core_ids=[0])
    return r.results[0]["out_0_dram"]
```
